# Optimizing a Trainium2 kernel written in Bass

```python
import numpy as np
import jax
import jax.numpy as jnp

def _softmax(x, axis=-1):
    return jax.nn.softmax(x, axis=axis)

def _gelu(x):
    return jax.nn.gelu(x, approximate=True)

def _silu(x):
    return jax.nn.silu(x)

def _sigmoid(x):
    return jax.nn.sigmoid(x)

def _layernorm(x, axis=-1, eps=1e-05):
    m = jnp.mean(x, axis=axis, keepdims=True)
    v = jnp.var(x, axis=axis, keepdims=True)
    return (x - m) / jnp.sqrt(v + eps)

def _scatter_add(tgt, idx, src, axis=0):
    return tgt.at[idx].add(src)

def _segment_sum(src, seg, n):
    return jax.ops.segment_sum(src, seg, n)
kernel_name = 'mk_gps_d1_gnn_r8_e70254'

def setup_inputs(seed: int=0):
    np.random.seed(seed)
    _w = jnp.asarray

    def _rec_inputs():
        import jax
        import jax.numpy as jnp
        _gk = jax.random.key(seed)
        x = -0.0002117 + 1 * jax.random.normal(jax.random.fold_in(_gk, 1), (1250, 512), jnp.float32)
        src = jax.random.randint(jax.random.fold_in(_gk, 2), (20000,), 0, 1250, jnp.int32)
        dst = jnp.minimum((1250 * jax.random.uniform(jax.random.fold_in(_gk, 3), (20000,)) ** 2.0).astype(jnp.int32), 9999)
        _o = jnp.argsort(dst, stable=True)
        src = src[_o]
        dst = dst[_o]
        edge_attr_512 = -8.16379e-05 + 0.999858 * jax.random.normal(jax.random.fold_in(_gk, 12), (20000, 512), jnp.float32)
        return (x, src, dst, edge_attr_512)
    x, src, dst, edge_attr_512 = _rec_inputs()

    def _L0_gnn_setup():
        import jax, jax.numpy as jnp
        import numpy as np
        N = 6250
        E = 25000
        IN = 512
        H = 8
        D = 64
        EPS = 1e-05

        def _xavier(k, out_f, in_f):
            std = float(np.sqrt(2.0 / (in_f + out_f)))
            return jax.random.normal(k, (out_f, in_f), dtype=jnp.float32) * std
        key = jax.random.key(seed)
        ks = jax.random.split(key, 10)
        z = jnp.zeros((H * D,), jnp.float32)
        return {'node_feat': jax.random.normal(ks[0], (N, IN), dtype=jnp.float32), 'edge_feat': jax.random.normal(ks[1], (E, IN), dtype=jnp.float32), 'src': jax.random.randint(ks[2], (E,), 0, N), 'dst': jax.random.randint(ks[3], (E,), 0, N), 'Wq': _xavier(ks[4], H * D, IN), 'bq': z, 'Wr': _xavier(ks[5], H * D, 3 * IN), 'br': z, 'Wk': _xavier(ks[6], H * D, H * D), 'bk': z, 'Wv': _xavier(ks[7], H * D, H * D), 'bv': z, 'Wo': _xavier(ks[8], H * D, H * D), 'bo': z, 'gamma': jnp.ones((IN,), jnp.float32), 'beta': jnp.zeros((IN,), jnp.float32)}
    _L0_gnn_all = _L0_gnn_setup()
    _L0_gnn_in = {k: v for k, v in _L0_gnn_all.items() if k in ('Wq', 'bq', 'Wr', 'br', 'Wk', 'bk', 'Wv', 'bv', 'Wo', 'bo', 'gamma', 'beta')}
    del _L0_gnn_all

    def _L0_mix_setup():
        import jax, jax.numpy as jnp
        import numpy as np
        B, N, C = (8, 1024, 512)
        H = 8
        D = C // H
        EPS = 1e-06

        def _linear_attention(q, k, v):
            qf = jax.nn.elu(q) + 1.0
            kf = jax.nn.elu(k) + 1.0
            kv = jnp.einsum('bhnd,bhne->bhde', kf, v)
            z = jnp.einsum('bhnd,bhd->bhn', qf, kf.sum(axis=2))
            out = jnp.einsum('bhnd,bhde->bhne', qf, kv) / (z[..., None] + EPS)
            return out
        key = jax.random.key(seed)
        k1, k2, k3, k4 = jax.random.split(key, 4)
        x = jax.random.normal(k1, (B, N, C), dtype=jnp.float32)
        w_qkv = jax.random.normal(k2, (C, 3 * C), dtype=jnp.float32) * (1.0 / np.sqrt(C))
        w_proj = jax.random.normal(k3, (C, C), dtype=jnp.float32) * (1.0 / np.sqrt(C))
        b_proj = jax.random.normal(k4, (C,), dtype=jnp.float32) * 0.01
        return {'x': x, 'w_qkv': w_qkv, 'w_proj': w_proj, 'b_proj': b_proj}
    _L0_mix_all = _L0_mix_setup()
    _L0_mix_in = {k: v for k, v in _L0_mix_all.items() if k in ('w_qkv', 'w_proj', 'b_proj')}
    del _L0_mix_all

    def _L0_ffn_setup():
        import jax, jax.numpy as jnp
        import numpy as np
        EPS = 1e-05

        def _bitlinear(x, w):
            w_scale = jnp.clip(jnp.mean(jnp.abs(w)), EPS, None)
            w_q = jnp.clip(jnp.round(w / w_scale), -1.0, 1.0) * w_scale
            w_eff = w + jax.lax.stop_gradient(w_q - w)
            x_scale = 127.0 / jnp.clip(jnp.max(jnp.abs(x), axis=-1, keepdims=True), EPS, None)
            x_q = jnp.clip(jnp.round(x * x_scale), -128.0, 127.0) / x_scale
            x_eff = x + jax.lax.stop_gradient(x_q - x)
            return jnp.einsum('bsi,oi->bso', x_eff, w_eff)

        def _ste_round_clamp_int8(h):
            h_q = jnp.clip(jnp.round(h), -128.0, 127.0)
            return h + jax.lax.stop_gradient(h_q - h)
        key = jax.random.key(seed)
        k1, k2, k3 = jax.random.split(key, 3)
        B, S, D, F = (8, 1024, 512, 256)
        x = jax.random.normal(k1, (B, S, D), dtype=jnp.float32)
        w_up = jax.random.normal(k2, (F, D), dtype=jnp.float32) * (1.0 / np.sqrt(D))
        w_down = jax.random.normal(k3, (D, F), dtype=jnp.float32) * (1.0 / np.sqrt(F))
        return {'x': x, 'w_up': w_up, 'w_down': w_down}
    _L0_ffn_all = _L0_ffn_setup()
    _L0_ffn_in = {k: v for k, v in _L0_ffn_all.items() if k in ('w_up', 'w_down')}
    del _L0_ffn_all
    return {'x': x, 'src': src, 'dst': dst, 'edge_attr_512': edge_attr_512, 'L0_gnn_Wq': _L0_gnn_in['Wq'], 'L0_gnn_bq': _L0_gnn_in['bq'], 'L0_gnn_Wr': _L0_gnn_in['Wr'], 'L0_gnn_br': _L0_gnn_in['br'], 'L0_gnn_Wk': _L0_gnn_in['Wk'], 'L0_gnn_bk': _L0_gnn_in['bk'], 'L0_gnn_Wv': _L0_gnn_in['Wv'], 'L0_gnn_bv': _L0_gnn_in['bv'], 'L0_gnn_Wo': _L0_gnn_in['Wo'], 'L0_gnn_bo': _L0_gnn_in['bo'], 'L0_gnn_gamma': _L0_gnn_in['gamma'], 'L0_gnn_beta': _L0_gnn_in['beta'], 'L0_mix_w_qkv': _L0_mix_in['w_qkv'], 'L0_mix_w_proj': _L0_mix_in['w_proj'], 'L0_mix_b_proj': _L0_mix_in['b_proj'], 'L0_ffn_w_up': _L0_ffn_in['w_up'], 'L0_ffn_w_down': _L0_ffn_in['w_down']}

def reference(x, src, dst, edge_attr_512, L0_gnn_Wq, L0_gnn_bq, L0_gnn_Wr, L0_gnn_br, L0_gnn_Wk, L0_gnn_bk, L0_gnn_Wv, L0_gnn_bv, L0_gnn_Wo, L0_gnn_bo, L0_gnn_gamma, L0_gnn_beta, L0_mix_w_qkv, L0_mix_w_proj, L0_mix_b_proj, L0_ffn_w_up, L0_ffn_w_down):
    import jax
    import jax.numpy as jnp

    def _L0_gnn_ref(node_feat, edge_feat, src, dst, Wq, bq, Wr, br, Wk, bk, Wv, bv, Wo, bo, gamma, beta):
        import jax, jax.numpy as jnp
        import numpy as np
        N = 6250
        E = 25000
        IN = 512
        H = 8
        D = 64
        EPS = 1e-05

        def _xavier(k, out_f, in_f):
            std = float(np.sqrt(2.0 / (in_f + out_f)))
            return jax.random.normal(k, (out_f, in_f), dtype=jnp.float32) * std
        n = node_feat.shape[0]
        e = edge_feat.shape[0]
        scaler = 1.0 / np.sqrt(D)
        x_cat = jnp.concatenate([node_feat[src], node_feat[dst], edge_feat], axis=-1)
        r = x_cat @ Wr.T + br
        q = (node_feat @ Wq.T + bq).reshape(n, H, D)
        k = (r @ Wk.T + bk).reshape(e, H, D)
        v = (r @ Wv.T + bv).reshape(e, H, D)
        a = jnp.einsum('ehd,ehd->eh', q[dst], k) * scaler
        amax = jax.ops.segment_max(a, dst, num_segments=n)
        ae = jnp.exp(a - amax[dst])
        asum = jax.ops.segment_sum(ae, dst, num_segments=n)
        attn = ae / asum[dst]
        m = v * attn[..., None]
        out = jax.ops.segment_sum(m, dst, num_segments=n).reshape(n, H * D)
        out = out @ Wo.T + bo
        out = node_feat + out
        mean = out.mean(axis=0)
        var = jnp.mean(jnp.square(out - mean), axis=0)
        out = (out - mean) * jax.lax.rsqrt(var + EPS) * gamma + beta
        return out

    def _L0_mix_ref(x, w_qkv, w_proj, b_proj):
        import jax, jax.numpy as jnp
        import numpy as np
        B, N, C = (8, 1024, 512)
        H = 8
        D = C // H
        EPS = 1e-06

        def _linear_attention(q, k, v):
            qf = jax.nn.elu(q) + 1.0
            kf = jax.nn.elu(k) + 1.0
            kv = jnp.einsum('bhnd,bhne->bhde', kf, v)
            z = jnp.einsum('bhnd,bhd->bhn', qf, kf.sum(axis=2))
            out = jnp.einsum('bhnd,bhde->bhne', qf, kv) / (z[..., None] + EPS)
            return out
        b, n, c = x.shape
        qkv = x @ w_qkv
        qkv = qkv.reshape(b, n, 3, H, D).transpose(2, 0, 3, 1, 4)
        q, k, v = (qkv[0], qkv[1], qkv[2])
        attn = _linear_attention(q, k, v)
        y = attn.transpose(0, 2, 1, 3).reshape(b, n, c)
        return y @ w_proj + b_proj

    def _L0_ffn_ref(x, w_up, w_down):
        import jax, jax.numpy as jnp
        import numpy as np
        EPS = 1e-05

        def _bitlinear(x, w):
            w_scale = jnp.clip(jnp.mean(jnp.abs(w)), EPS, None)
            w_q = jnp.clip(jnp.round(w / w_scale), -1.0, 1.0) * w_scale
            w_eff = w + jax.lax.stop_gradient(w_q - w)
            x_scale = 127.0 / jnp.clip(jnp.max(jnp.abs(x), axis=-1, keepdims=True), EPS, None)
            x_q = jnp.clip(jnp.round(x * x_scale), -128.0, 127.0) / x_scale
            x_eff = x + jax.lax.stop_gradient(x_q - x)
            return jnp.einsum('bsi,oi->bso', x_eff, w_eff)

        def _ste_round_clamp_int8(h):
            h_q = jnp.clip(jnp.round(h), -128.0, 127.0)
            return h + jax.lax.stop_gradient(h_q - h)
        h = _bitlinear(x, w_up)
        h = jax.nn.relu(h)
        h = _ste_round_clamp_int8(h)
        return _bitlinear(h, w_down)
    xn = _layernorm(x, axis=-1)
    x = x + _L0_gnn_ref(xn, edge_attr_512, src, dst, L0_gnn_Wq, L0_gnn_bq, L0_gnn_Wr, L0_gnn_br, L0_gnn_Wk, L0_gnn_bk, L0_gnn_Wv, L0_gnn_bv, L0_gnn_Wo, L0_gnn_bo, L0_gnn_gamma, L0_gnn_beta) + _L0_mix_ref(xn[None], L0_mix_w_qkv, L0_mix_w_proj, L0_mix_b_proj)[0]
    x = x + _L0_ffn_ref(_layernorm(x, axis=-1)[None], L0_ffn_w_up, L0_ffn_w_down)[0]
    return x

_drawn_inputs = setup_inputs


def setup_inputs(seed=0):
    import zlib

    import numpy as np

    out = dict(_drawn_inputs(seed))
    spreads = {'L0_gnn_bq': (0.0, 0.299),
     'L0_gnn_br': (0.0, 0.8),
     'L0_gnn_bk': (0.0, 0.8),
     'L0_gnn_bv': (0.0, 0.8),
     'L0_gnn_bo': (0.0, 0.8),
     'L0_gnn_gamma': (1.0, 0.2),
     'L0_gnn_beta': (0.0, 0.1)}
    factors = {'L0_mix_b_proj': 3.891}
    for name, (base, spread) in spreads.items():
        noise = np.random.default_rng([zlib.crc32(name.encode()), seed]).standard_normal(out[name].shape)
        drawn = base * np.exp(spread * noise) if base else spread * noise
        out[name] = jnp.asarray(drawn.astype(out[name].dtype))
    for name, factor in factors.items():
        out[name] = (out[name] * factor).astype(out[name].dtype)
    return out
```

```python
import numpy as np
import concourse.bass as bass
from concourse import mybir
from contextlib import ExitStack

F32 = mybir.dt.float32
BF16 = mybir.dt.bfloat16
I32 = mybir.dt.int32
ALU = mybir.AluOpType
ACT = mybir.ActivationFunctionType
AX = mybir.AxisListType

P = 128
N, D, E, H = 1250, 512, 20000, 8
DH = D // H
C = D // P
NT = -(-N // P)
NP = NT * P
NLAST = N - (NT - 1) * P
ET = -(-E // P)
ELAST = E - (ET - 1) * P
HW = DH + 1
ROW = H * HW
TROW = ROW + H
QROW = D + H
FF = 256
SCALE = 1.0 / 8.0
NEG = -3.0e38
OOB = 2048.0
LN_EPS = 1e-5
MIX_EPS = 1e-6
RINT = 12582912.0
NCH = [(0, 512), (512, 512), (1024, 256)]


def node_rows(t):
    return P if t < NT - 1 else NLAST


def bc(ap, n):
    return ap.unsqueeze(len(ap.shape)).to_broadcast(list(ap.shape) + [n])


def layer(nc, x, src, dst, ef, Wq, bq, Wr, br, Wk, bk, Wv, bv, Wo, bo, gamma, beta,
          w_qkv, w_proj, b_proj, w_up, w_down, out):
    q_table = nc.dram_tensor("q_table", [NP, QROW], F32, kind="Internal").ap()
    kv_table = nc.dram_tensor("kv_table", [NP, 2 * D], F32, kind="Internal").ap()
    merge = [nc.dram_tensor(f"merge{i}", [NP, TROW], F32, kind="Internal").ap() for i in range(2)]

    top = ExitStack()
    with top:
        def keep(name, shape, dt=F32):
            return top.enter_context(nc.sbuf_tensor(name, shape, dt))

        ident = keep("ident", [P, P])
        xnT = keep("xnT", [P, C, NP])
        res = keep("res", [P, NT, D])
        v2 = keep("v2", [P, NT, D])
        WoT = keep("WoT", [P, C, D])
        Me = keep("Me", [P, C, 2 * D])
        ones = keep("ones", [1, P])

        with ExitStack() as mid:
            def sb(name, shape, dt=F32):
                return mid.enter_context(nc.sbuf_tensor(name, shape, dt))
            Mn = sb("Mn", [P, 2, C, 2 * D])
            WqT = sb("WqT", [P, C, D])
            kv_bias = sb("kv_bias", [1, 2 * D])
            prepare(nc, x, Wq, bq, Wr, br, Wk, bk, Wv, bv, Wo, ident, ones, xnT, res, WqT, WoT, Me, Mn, kv_bias)
            node_tables(nc, bq, q_table, kv_table, merge, xnT, ones, WqT, Mn, kv_bias, v2)
        mix_branch(nc, w_qkv, w_proj, b_proj, xnT, ident, ones, res)
        edges(nc, src, dst, ef, q_table, kv_table, merge, ident, Me)
        gnn_end(nc, merge, bo, gamma, beta, ident, xnT, v2, WoT, res)
        ffn(nc, w_up, w_down, ident, res, out)


def prepare(nc, x, Wq, bq, Wr, br, Wk, bk, Wv, bv, Wo, ident, ones, xnT, res, WqT, WoT, Me, Mn, kv_bias):
    with ExitStack() as ctx:
        def sb(name, shape, dt=F32):
            return ctx.enter_context(nc.sbuf_tensor(name, shape, dt))

        def sem(name):
            return ctx.enter_context(nc.semaphore(name))

        raw = sb("raw", [P, C, D])
        raw2 = sb("raw2", [P, C, D])
        wr = sb("wr", [P, C, 3 * D])
        WkT = sb("WkT", [P, C, D])
        WvT = sb("WvT", [P, C, D])
        br_col = sb("br_col", [P, C])
        bkv = sb("bkv", [1, 2 * D])
        stats = sb("stats", [P, NT, 6])
        mv = sb("mv", [P, NT, 2])
        std = sb("std", [P, NT])
        rstd = sb("rstd", [P, NT])
        xn = sb("xn", [P, 2, D])
        banks = [ctx.enter_context(nc.psum_tensor(f"bank{i}", [P, D], F32)) for i in range(8)]
        x_clear, x_in, w_in = sem("x_clear"), sem("x_in"), [sem(f"w_in{i}") for i in range(4)]
        wr_in, small_in = sem("wr_in"), sem("small_in")
        ident_step, ones_set = sem("ident_step"), sem("ones_set")
        stats_done, mv_done, var_eps, std_done, rstd_done, xn_done = (
            sem("stats_done"), sem("mv_done"), sem("var_eps"), sem("std_done"), sem("rstd_done"), sem("xn_done"))
        turned, copied = sem("turned"), sem("copied")
        folded, fold_copied = sem("folded"), sem("fold_copied")
        block = ctx.enter_context(nc.Block())
        raws = [raw, raw2]
        weights = [(Wk, WkT), (Wv, WvT), (Wq, WqT), (Wo, WoT)]

        @block.sync
        def _(sp):
            sp.wait_ge(x_clear, 1)
            sp.dma_start(res[:, 0:NT - 1, :], x[0:(NT - 1) * P, :].rearrange("(t p) d -> p t d", p=P)).then_inc(x_in, 16)
            sp.dma_start(res[0:NLAST, NT - 1, :], x[(NT - 1) * P:N, :]).then_inc(x_in, 16)
            for i, (w, _) in enumerate(weights):
                if i >= 2:
                    sp.wait_ge(turned, C * (i - 1))
                sp.dma_start(raws[i % 2][:, :, :], w.rearrange("(c p) i -> p c i", p=P)).then_inc(w_in[i], 16)

        @block.gpsimd
        def _(pool):
            pool.memset(ident[:, :], 0.0).then_inc(ident_step, 1)
            pool.memset(ones[:, :], 1.0).then_inc(ones_set, 1)
            pool.wait_ge(ident_step, 1)
            pool.affine_select(out=ident[:, :], in_=ident[:, :], compare_op=ALU.not_equal, fill=1.0, base=0,
                               pattern=[[-1, P]], channel_multiplier=1).then_inc(ident_step, 1)

        @block.vector
        def _(dve):
            dve.memset(res[:, NT - 1, :], 0.0).then_inc(x_clear, 1)
            dve.wait_ge(x_in, 32)
            for t in range(NT):
                dve.bn_stats(stats[:, t, :], res[:, t, :]).then_inc(stats_done, 1)
            for t in range(NT):
                dve.wait_ge(stats_done, t + 1)
                dve.bn_aggr(mv[:, t, :], stats[:, t, :]).then_inc(mv_done, 1)
            dve.wait_ge(mv_done, NT)
            dve.tensor_scalar(std[:, :], mv[:, :, 1], LN_EPS, None, ALU.add).then_inc(var_eps, 1)
            dve.wait_ge(std_done, 1)
            dve.reciprocal(rstd[:, :], std[:, :]).then_inc(rstd_done, 1)
            dve.wait_ge(rstd_done, 1)
            for t in range(NT):
                if t >= 2:
                    dve.wait_ge(turned, 4 * C + t - 1)
                dve.tensor_scalar(xn[:, t % 2, :], res[:, t, :], mv[:, t, 0:1], rstd[:, t:t + 1],
                                  ALU.subtract, ALU.mult).then_inc(xn_done, 1)
            dve.wait_ge(small_in, 48)
            for half in range(2):
                dve.wait_ge(folded, 24 + half + 1)
                dve.tensor_tensor(kv_bias[0:1, half * D:(half + 1) * D], banks[half][0:1, :],
                                  bkv[0:1, half * D:(half + 1) * D], ALU.add).then_inc(fold_copied, 1)

        @block.scalar
        def _(act):
            act.dma_start(wr[:, :, :], Wr.rearrange("(c p) i -> p c i", p=P)).then_inc(wr_in, 16)
            act.dma_start(br_col[:, :], br.rearrange("(c p) -> p c", p=P),
                              allow_slow_non_contiguous=True).then_inc(small_in, 16)
            act.dma_start(bkv[:, 0:D], bk.unsqueeze(0)).then_inc(small_in, 16)
            act.dma_start(bkv[:, D:2 * D], bv.unsqueeze(0)).then_inc(small_in, 16)
            act.wait_ge(var_eps, 1)
            act.activation(std[:, :], std[:, :], ACT.Sqrt).then_inc(std_done, 1)
            for k in range(4 * C + NT):
                act.wait_ge(turned, k + 1)
                bank = banks[k % 8][:, :].rearrange("p (c o) -> p c o", c=C)
                if k < 4 * C:
                    to = weights[k // C][1][:, :, (k % C) * P:(k % C + 1) * P]
                else:
                    to = xnT[:, :, (k - 4 * C) * P:(k - 4 * C + 1) * P]
                act.activation(to, bank, ACT.Copy).then_inc(copied, 1)
            for k in range(24):
                act.wait_ge(folded, k + 1)
                part, ic, half = k // 8, k // 2 % C, k % 2
                to = (Me[:, ic, half * D:(half + 1) * D] if part == 2
                      else Mn[:, part, ic, half * D:(half + 1) * D])
                act.activation(to, banks[k % 8][:, :], ACT.Copy).then_inc(fold_copied, 1)

        @block.tensor
        def _(pe):
            pe.wait_ge(ident_step, 2)
            for k in range(4 * C + NT):
                if k >= 8:
                    pe.wait_ge(copied, k - 7)
                if k < 4 * C:
                    pe.wait_ge(w_in[k // C], 16)
                    source = raws[(k // C) % 2][:, k % C, :]
                else:
                    pe.wait_ge(xn_done, k - 4 * C + 1)
                    source = xn[:, (k - 4 * C) % 2, :]
                for c in range(C):
                    last = pe.transpose(banks[k % 8][:, c * P:(c + 1) * P], source[:, c * P:(c + 1) * P], ident[:, :])
                last.then_inc(turned, 1)
            pe.wait_ge(wr_in, 16)
            pe.wait_ge(copied, 4 * C + NT)
            for k in range(24):
                part, ic, half = k // 8, k // 2 % C, k % 2
                if k >= 8:
                    pe.wait_ge(fold_copied, k - 7)
                for rc in range(C):
                    last = pe.matmul(banks[k % 8][:, :], wr[:, rc, part * D + ic * P:part * D + (ic + 1) * P],
                                     (WkT, WvT)[half][:, rc, :], start=rc == 0, stop=rc == C - 1)
                last.then_inc(folded, 1)
            pe.wait_ge(small_in, 48)
            pe.wait_ge(fold_copied, 24)
            for half in range(2):
                for rc in range(C):
                    last = pe.matmul(banks[half][0:1, :], br_col[:, rc:rc + 1], (WkT, WvT)[half][:, rc, :],
                                     start=rc == 0, stop=rc == C - 1)
                last.then_inc(folded, 1)


def node_tables(nc, bq, q_table, kv_table, merge, xnT, ones, WqT, Mn, kv_bias, v2):
    with ExitStack() as ctx:
        def sb(name, shape, dt=F32):
            return ctx.enter_context(nc.sbuf_tensor(name, shape, dt))

        def sem(name):
            return ctx.enter_context(nc.semaphore(name))

        bq_row = sb("bq_row", [1, D])
        q_out = sb("q_out", [P, 2, QROW])
        kv_out = sb("kv_out", [P, 2, 2 * D])
        own = sb("own", [P, D])
        empty = sb("empty", [P, TROW])
        banks = [ctx.enter_context(nc.psum_tensor(f"nbank{i}", [P, D], F32)) for i in range(5)]
        bq_in, done, empty_set, tables_out = sem("bq_in"), sem("done"), sem("empty_set"), sem("tables_out")
        q_copied, kv_copied, own_mul, own_sum, v2_copied = (
            sem("q_copied"), sem("kv_copied"), sem("own_mul"), sem("own_sum"), sem("v2_copied"))
        q_stored = [sem(f"q_stored{i}") for i in range(2)]
        kv_stored = [sem(f"kv_stored{i}") for i in range(2)]
        block = ctx.enter_context(nc.Block())

        @block.sync
        def _(sp):
            sp.dma_start(bq_row[:, :], bq.unsqueeze(0)).then_inc(bq_in, 16)
            for t in range(NT):
                sp.wait_ge(kv_copied, 2 * (t + 1))
                sp.dma_start(kv_table[t * P:(t + 1) * P, :], kv_out[:, t % 2, :]).then_inc(kv_stored[t % 2], 16)
                sp.wait_ge(own_sum, t + 1)
                sp.dma_start(q_table[t * P:(t + 1) * P, :], q_out[:, t % 2, :]).then_inc(q_stored[t % 2], 16)
            for i in range(2):
                sp.wait_ge(kv_stored[i], 16 * (NT // 2))
                sp.wait_ge(q_stored[i], 16 * (NT // 2))

        @block.gpsimd
        def _(pool):
            pool.memset(empty[:, 0:ROW], 0.0).then_inc(empty_set, 1)
            pool.memset(empty[:, ROW:TROW], NEG).then_inc(empty_set, 1)
            pool.wait_ge(empty_set, 2)
            for i in range(2):
                for t in range(NT):
                    pool.dma_start(merge[i][t * P:(t + 1) * P, :], empty[:, :]).then_inc(tables_out, 16)
            pool.wait_ge(tables_out, 16 * 2 * NT)

        @block.tensor
        def _(pe):
            pe.wait_ge(bq_in, 16)
            for t in range(NT):
                for b in range(5):
                    if t >= 1:
                        if b == 0:
                            pe.wait_ge(q_copied, t)
                        elif b <= 2:
                            pe.wait_ge(kv_copied, 2 * (t - 1) + b)
                        elif b == 3:
                            pe.wait_ge(own_mul, t)
                        else:
                            pe.wait_ge(v2_copied, t)
                    for c in range(C):
                        rhs = WqT[:, c, :] if b == 0 else Mn[:, (b - 1) // 2, c, ((b - 1) % 2) * D:((b - 1) % 2 + 1) * D]
                        last = pe.matmul(banks[b][:, :], xnT[:, c, t * P:(t + 1) * P], rhs,
                                         start=c == 0, stop=c == C - 1 and b in (1, 2))
                    if b == 0:
                        last = pe.matmul(banks[b][:, :], ones[:, :], bq_row[:, :], start=False, stop=True)
                    elif b >= 3:
                        last = pe.matmul(banks[b][:, :], ones[:, :], kv_bias[:, (b - 3) * D:(b - 2) * D],
                                         start=False, stop=True)
                    last.then_inc(done, 1)

        @block.scalar
        def _(act):
            for t in range(NT):
                act.wait_ge(done, 5 * t + 1)
                if t >= 2:
                    act.wait_ge(q_stored[t % 2], 16 * (t // 2))
                act.activation(q_out[:, t % 2, 0:D], banks[0][:, :], ACT.Copy).then_inc(q_copied, 1)
                if t >= 2:
                    act.wait_ge(kv_stored[t % 2], 16 * (t // 2))
                for half in range(2):
                    act.wait_ge(done, 5 * t + 2 + half)
                    act.activation(kv_out[:, t % 2, half * D:(half + 1) * D], banks[1 + half][:, :],
                                   ACT.Copy).then_inc(kv_copied, 1)
                act.wait_ge(done, 5 * t + 5)
                act.activation(v2[:, t, :], banks[4][:, :], ACT.Copy).then_inc(v2_copied, 1)

        @block.vector
        def _(dve):
            for t in range(NT):
                dve.wait_ge(done, 5 * t + 4)
                dve.wait_ge(q_copied, t + 1)
                if t >= 1:
                    dve.wait_ge(own_sum, t)
                dve.tensor_tensor(own[:, :], banks[3][:, :], q_out[:, t % 2, 0:D], ALU.mult).then_inc(own_mul, 1)
                dve.wait_ge(own_mul, t + 1)
                dve.tensor_reduce(q_out[:, t % 2, D:QROW], own[:, :].rearrange("p (h d) -> p h d", h=H),
                                  AX.X, ALU.add).then_inc(own_sum, 1)


def mix_branch(nc, w_qkv, w_proj, b_proj, xnT, ident, ones, res):
    with ExitStack() as ctx:
        def sb(name, shape, dt=F32):
            return ctx.enter_context(nc.sbuf_tensor(name, shape, dt))

        def sem(name):
            return ctx.enter_context(nc.semaphore(name))

        PAIR = 2 * HW
        w = sb("w_mix", [P, C, 3 * D])
        wp = sb("wp", [P, C, D])
        bp = sb("bp", [1, D])
        qfT = sb("qfT", [P, C, NP])
        small = sb("small", [P, 2, D])
        big = sb("big", [P, 2, D])
        kf = sb("kf", [P, 2, D])
        v1 = sb("v1", [P, 2, H, HW])
        kvd = sb("kvd", [P, C, PAIR])
        z = sb("z", [P, 2, H])
        y = sb("y", [P, 2, D])
        yT = sb("yT", [P, 2, D])
        kb = [ctx.enter_context(nc.psum_tensor(f"kb{i}", [P, D], F32)) for i in range(2)]
        vb = [ctx.enter_context(nc.psum_tensor(f"vb{i}", [P, D], F32)) for i in range(2)]
        kvb = [ctx.enter_context(nc.psum_tensor(f"kvb{i}", [P, D], F32)) for i in range(4)]
        w_in, wp_in = sem("w_in"), sem("wp_in")
        k_done, v_done, q_done = sem("k_done"), sem("v_done"), sem("q_done")
        low, exped, high = sem("low"), sem("exped"), sem("high")
        v_copied, v_ones, kv_added, kvd_zero, kvd_done = (
            sem("v_copied"), sem("v_ones"), sem("kv_added"), sem("kvd_zero"), sem("kvd_done"))
        y_done, z_eps, z_inv, y_scaled, y_turned, yT_copied, p_done, res_done = (
            sem("y_done"), sem("z_eps"), sem("z_inv"), sem("y_scaled"), sem("y_turned"), sem("yT_copied"),
            sem("p_done"), sem("res_done"))
        block = ctx.enter_context(nc.Block())
        QJ = [(c, n0, nn) for c in range(C) for n0, nn in NCH]

        @block.sync
        def _(sp):
            sp.dma_start(w[:, :, :], w_qkv.rearrange("(c p) o -> p c o", p=P)).then_inc(w_in, 16)
            sp.dma_start(wp[:, :, :], w_proj.rearrange("(c p) o -> p c o", p=P)).then_inc(wp_in, 16)
            sp.dma_start(bp[:, :], b_proj.unsqueeze(0)).then_inc(wp_in, 16)

        @block.gpsimd
        def _(pool):
            pool.memset(v1[:, :, :, DH:HW], 1.0).then_inc(v_ones, 1)
            pool.memset(kvd[:, :, :], 0.0).then_inc(kvd_zero, 1)

        @block.vector
        def _(dve):
            for t in range(NT):
                dve.wait_ge(k_done, t + 1)
                if t >= 2:
                    dve.wait_ge(high, t - 1)
                dve.tensor_scalar(small[:, t % 2, :], kb[t % 2][:, :], 0.0, None, ALU.min).then_inc(low, 1)
                dve.wait_ge(exped, t + 1)
                if t >= 2:
                    dve.wait_ge(kv_added, t - 1)
                dve.scalar_tensor_tensor(kf[:, t % 2, :], kb[t % 2][:, :], 0.0, big[:, t % 2, :],
                                         ALU.max, ALU.add).then_inc(high, 1)
            for j, (c, n0, nn) in enumerate(QJ):
                t = NT + j
                dve.wait_ge(q_done, j + 1)
                dve.wait_ge(high, t - 1)
                dve.tensor_scalar(small[:, t % 2, 0:nn], kb[t % 2][:, 0:nn], 0.0, None, ALU.min).then_inc(low, 1)
                dve.wait_ge(exped, t + 1)
                dve.scalar_tensor_tensor(qfT[:, c, n0:n0 + nn], kb[t % 2][:, 0:nn], 0.0, big[:, t % 2, 0:nn],
                                         ALU.max, ALU.add).then_inc(high, 1)
            dve.wait_ge(kv_added, NT)
            dve.wait_ge(kvd_zero, 1)
            for c in range(C):
                dve.tensor_copy(kvd[0:DH, c, 0:HW], kvb[c][0:DH, 0:HW]).then_inc(kvd_done, 1)
                dve.tensor_copy(kvd[DH:P, c, HW:PAIR], kvb[c][DH:P, HW:PAIR]).then_inc(kvd_done, 1)
            for t in range(NT):
                dve.wait_ge(y_done, t + 1)
                if t >= 1:
                    dve.wait_ge(y_scaled, 2 * t)
                for b in range(2):
                    heads = kb[b][:, 0:2 * PAIR].rearrange("p (h e) -> p h e", e=HW)
                    dve.tensor_scalar(z[:, 0, 4 * b:4 * b + 4], heads[:, :, DH], MIX_EPS, None,
                                      ALU.add).then_inc(z_eps, 1)
                dve.wait_ge(z_eps, 2 * (t + 1))
                dve.reciprocal(z[:, 1, :], z[:, 0, :]).then_inc(z_inv, 1)
                dve.wait_ge(z_inv, t + 1)
                if t >= 2:
                    dve.wait_ge(y_turned, t - 1)
                for b in range(2):
                    heads = kb[b][:, 0:2 * PAIR].rearrange("p (h e) -> p h e", e=HW)
                    dve.tensor_tensor(y[:, t % 2, b * 256:(b + 1) * 256].rearrange("p (h d) -> p h d", d=DH),
                                      heads[:, :, 0:DH], bc(z[:, 1, 4 * b:4 * b + 4], DH), ALU.mult).then_inc(y_scaled, 1)
                dve.wait_ge(p_done, t + 1)
                dve.tensor_tensor(res[:, t, :], vb[1][:, :], res[:, t, :], ALU.add).then_inc(res_done, 1)

        @block.scalar
        def _(act):
            for t in range(NT):
                act.wait_ge(low, t + 1)
                if t >= 2:
                    act.wait_ge(high, t - 1)
                act.activation(big[:, t % 2, :], small[:, t % 2, :], ACT.Exp).then_inc(exped, 1)
                act.wait_ge(v_done, t + 1)
                act.wait_ge(v_ones, 1)
                if t >= 2:
                    act.wait_ge(kv_added, t - 1)
                act.activation(v1[:, t % 2, :, 0:DH], vb[t % 2][:, :].rearrange("p (h d) -> p h d", h=H),
                               ACT.Copy).then_inc(v_copied, 1)
            for j, (c, n0, nn) in enumerate(QJ):
                t = NT + j
                act.wait_ge(low, t + 1)
                act.wait_ge(high, t - 1)
                act.activation(big[:, t % 2, 0:nn], small[:, t % 2, 0:nn], ACT.Exp).then_inc(exped, 1)
            for t in range(NT):
                act.wait_ge(y_turned, t + 1)
                if t >= 2:
                    act.wait_ge(p_done, t - 1)
                act.activation(yT[:, t % 2, :], vb[0][:, :], ACT.Copy).then_inc(yT_copied, 1)

        @block.tensor
        def _(pe):
            pe.wait_ge(w_in, 16)

            def add_kv(t):
                pe.wait_ge(high, t + 1)
                pe.wait_ge(v_copied, t + 1)
                r = node_rows(t)
                for c in range(C):
                    last = pe.matmul(kvb[c][:, 0:PAIR], kf[0:r, t % 2, c * P:(c + 1) * P],
                                     v1[0:r, t % 2, 2 * c:2 * c + 2, :], start=t == 0, stop=t == NT - 1)
                last.then_inc(kv_added, 1)

            for t in range(NT):
                if t >= 2:
                    pe.wait_ge(high, t - 1)
                for c in range(C):
                    last = pe.matmul(kb[t % 2][:, :], xnT[:, c, t * P:(t + 1) * P], w[:, c, D:2 * D],
                                     start=c == 0, stop=c == C - 1)
                last.then_inc(k_done, 1)
                if t >= 2:
                    pe.wait_ge(v_copied, t - 1)
                for c in range(C):
                    last = pe.matmul(vb[t % 2][:, :], xnT[:, c, t * P:(t + 1) * P], w[:, c, 2 * D:3 * D],
                                     start=c == 0, stop=c == C - 1)
                last.then_inc(v_done, 1)
                if t >= 1:
                    add_kv(t - 1)
            add_kv(NT - 1)
            for j, (c, n0, nn) in enumerate(QJ):
                pe.wait_ge(high, NT + j - 1)
                for k in range(C):
                    last = pe.matmul(kb[(NT + j) % 2][:, 0:nn], w[:, k, c * P:(c + 1) * P], xnT[:, k, n0:n0 + nn],
                                     start=k == 0, stop=k == C - 1)
                last.then_inc(q_done, 1)
            pe.wait_ge(kvd_done, 2 * C)
            pe.wait_ge(high, NT + len(QJ))
            pe.wait_ge(v_copied, NT)
            pe.wait_ge(wp_in, 32)
            for t in range(NT):
                if t >= 1:
                    pe.wait_ge(y_scaled, 2 * t)
                for c in range(C):
                    last = pe.matmul(kb[c // 2][:, (c % 2) * PAIR:(c % 2 + 1) * PAIR], qfT[:, c, t * P:(t + 1) * P],
                                     kvd[:, c, :], start=True, stop=True)
                last.then_inc(y_done, 1)
                pe.wait_ge(y_scaled, 2 * (t + 1))
                if t >= 1:
                    pe.wait_ge(yT_copied, t)
                for c in range(C):
                    last = pe.transpose(vb[0][:, c * P:(c + 1) * P], y[:, t % 2, c * P:(c + 1) * P], ident[:, :])
                last.then_inc(y_turned, 1)
                pe.wait_ge(yT_copied, t + 1)
                if t >= 1:
                    pe.wait_ge(res_done, t)
                for c in range(C):
                    pe.matmul(vb[1][:, :], yT[:, t % 2, c * P:(c + 1) * P], wp[:, c, :], start=c == 0, stop=False)
                pe.matmul(vb[1][:, :], ones[:, :], bp[:, :], start=False, stop=True).then_inc(p_done, 1)


def edges(nc, src, dst, ef, q_table, kv_table, merge, ident, Me):
    with ExitStack() as ctx:
        def sb(name, shape, dt=F32):
            return ctx.enter_context(nc.sbuf_tensor(name, shape, dt))

        def two(name, shape, dt=F32):
            return [sb(f"{name}{u}", shape, dt) for u in range(2)]

        def sem(name):
            return ctx.enter_context(nc.semaphore(name))

        ident16 = sb("ident16", [P, 4, P], BF16)
        pick = sb("pick", [3 * H, H, P], BF16)
        before = sb("before", [P, P])
        efs = two("efs", [P, D])
        efT = two("efT", [P, C, P])
        src_id = two("src_id", [P, 1], I32)
        dst_id = two("dst_id", [P, 1], I32)
        dst_row = two("dst_row", [P, P], I32)
        dst_f = two("dst_f", [P, 1])
        same = two("same", [P, P])
        apart = two("apart", [P, P], BF16)
        junk = sb("junk", [P, P])
        count = sb("count", [P, 1])
        put_id = two("put_id", [P, 1], I32)
        kv = two("kv", [P, 2 * D])
        qc = two("qc", [P, QROW])
        old = two("old", [P, TROW])
        new = two("new", [P, TROW])
        score0 = sb("score_sum", [P, H])
        score = two("score", [P, H])
        rest = sb("rest", [P, 2, H])
        parts = sb("parts", [P, 3 * H], BF16)
        partsT = sb("partsT", [3 * H, P], BF16)
        top = two("top", [P, H])
        diff = two("diff", [P, 3 * H])
        expd = two("expd", [P, 3 * H])
        wv = two("wv", [P, H, HW])
        psT = ctx.enter_context(nc.psum_tensor("psT", [P, D], F32))
        psK = ctx.enter_context(nc.psum_tensor("psK", [P, D], F32))
        psV = ctx.enter_context(nc.psum_tensor("psV", [P, D], F32))
        psB = ctx.enter_context(nc.psum_tensor("psB", [P, 2, D], F32))
        psS = ctx.enter_context(nc.psum_tensor("psS", [P, 2, D], F32))
        psA = ctx.enter_context(nc.psum_tensor("psA", [P, 2 * D], BF16))

        consts = sem("consts")
        ids_in, ef_in, kv_in, q_in, old_in, put = ([sem(f"{n}{u}") for u in range(2)] for n in
                                                   ("ids_in", "ef_in", "kv_in", "q_in", "old_in", "put"))
        turned, efT_ready, k_done, v_done = sem("ef_turned"), sem("efT_ready"), sem("k_edges"), sem("v_edges")
        dstf_ready, same_ready, apart_ready, counted, putid_ready = (
            sem("dstf_ready"), sem("same_ready"), sem("apart_ready"), sem("counted"), sem("putid_ready"))
        k_added, k_times_q, k_summed, score_ready = (
            sem("k_added"), sem("k_times_q"), sem("k_summed"), sem("score_ready"))
        part_step, parts_ready, parts_turned, partsT_ready, spread = (
            sem("part_step"), sem("parts_ready"), sem("parts_turned"), sem("partsT_ready"), sem("spread"))
        v_added, top_ready, newmax_ready, diff_step, diff_ready, exp_ready = (
            sem("v_added"), sem("top_ready"), sem("newmax_ready"), sem("diff_step"), sem("diff_ready"), sem("exp_ready"))
        wv_ready, summed, sum_scaled, old_scaled, new_ready = (
            sem("wv_ready"), sem("summed"), sem("sum_scaled"), sem("old_scaled"), sem("new_ready"))
        block = ctx.enter_context(nc.Block())
        J = ET // 2
        assert ET % 2 == 1 and ELAST == 32

        def over_tiles(eng, engine, body):
            body(0, 0, P)
            body(0, 1, P)
            with nc.Fori(1, J, engines=[engine]) as i:
                j = eng.snap(i)
                body(j, 0, P)
                body(j, 1, P)
            body(J, 0, ELAST)

        def later(j):
            return not (isinstance(j, int) and j == 0)

        def fixed(eng):
            eng.wait_ge(consts, 8)

        def value(eng, v):
            if not isinstance(v, int):
                v = eng.snap(v)
                eng.compute_val(v)
            return v

        @block.sync
        def _(sp):
            def load(j, u, r):
                t = 2 * j + u
                row, before_last, dmas = value(sp, t * P), value(sp, t - 1), value(sp, 16 * j)
                if later(j):
                    fixed(sp)
                    sp.wait_ge(putid_ready, before_last)
                    sp.wait_ge(kv_in[u], dmas)
                    sp.wait_ge(q_in[u], dmas)
                    sp.wait_ge(old_in[u], dmas)
                    sp.wait_ge(turned, before_last)
                sp.dma_start(src_id[u][0:r, :], src[bass.ds(row, r)].unsqueeze(1)).then_inc(ids_in[u], 16)
                sp.dma_start(dst_id[u][0:r, :], dst[bass.ds(row, r)].unsqueeze(1)).then_inc(ids_in[u], 16)
                sp.dma_start(dst_row[u][0:r, 0:r],
                             dst[bass.ds(row, r)].unsqueeze(0).to_broadcast([r, r])).then_inc(ids_in[u], 16)
                sp.dma_start(efs[u][0:r, :], ef[bass.ds(row, r), :]).then_inc(ef_in[u], 16)
            over_tiles(sp, mybir.EngineType.SP, load)

        @block.gpsimd
        def _(pool):
            pool.memset(ident16[:, :, :], 0.0).then_inc(consts, 1)
            pool.memset(pick[:, :, :], 0.0).then_inc(consts, 1)
            pool.memset(before[:, :], 1.0).then_inc(consts, 1)
            pool.wait_ge(consts, 3)
            pool.affine_select(out=ident16[:, :, :], in_=ident16[:, :, :], compare_op=ALU.not_equal, fill=1.0, base=0,
                               pattern=[[0, 4], [-1, P]], channel_multiplier=1).then_inc(consts, 1)
            pool.affine_select(out=before[:, :], in_=before[:, :], compare_op=ALU.is_gt, fill=0.0, base=0,
                               pattern=[[-1, P]], channel_multiplier=1).then_inc(consts, 1)
            for part in range(3):
                pool.wait_ge(consts, 5 + part)
                pool.affine_select(out=pick[:, :, :], in_=pick[:, :, :], compare_op=ALU.not_equal, fill=1.0,
                                   base=-H * part, pattern=[[-1, H], [0, P]], channel_multiplier=1).then_inc(consts, 1)

            def fetch(out, table, ids, r, done):
                pool.indirect_dma_start(out=out[0:r, :], out_offset=None, in_=table[:, :],
                                        in_offset=bass.IndirectOffsetOnAxis(ap=ids[0:r, 0:1], axis=0)).then_inc(done, 16)

            def store(tp, u, r):
                pool.wait_ge(exp_ready, tp)
                pool.tensor_tensor(old[u][0:r, 0:ROW].rearrange("p (h e) -> p h e", e=HW),
                                   old[u][0:r, 0:ROW].rearrange("p (h e) -> p h e", e=HW),
                                   bc(expd[u][0:r, H:2 * H], HW), ALU.mult).then_inc(old_scaled, 1)
                fixed(pool)
                pool.wait_ge(new_ready, tp)
                pool.wait_ge(putid_ready, tp)
                pool.indirect_dma_start(out=merge[u][:, :], out_offset=bass.IndirectOffsetOnAxis(ap=put_id[u][0:r, 0:1], axis=0),
                                        in_=new[u][0:r, :], in_offset=None, bounds_check=N - 1,
                                        oob_is_err=False).then_inc(put[u], 16)

            def move(j, u, r):
                t = 2 * j + u
                ids, dmas = value(pool, 48 * (j + 1)), value(pool, 16 * j)
                now, before_last = value(pool, t), value(pool, t - 1)
                fixed(pool)
                pool.wait_ge(ids_in[u], ids)
                if later(j):
                    pool.wait_ge(v_added, before_last)
                    pool.wait_ge(score_ready, before_last)
                fetch(kv[u], kv_table, src_id[u], r, kv_in[u])
                fetch(qc[u], q_table, dst_id[u], r, q_in[u])
                if later(j):
                    fixed(pool)
                    pool.wait_ge(put[u], dmas)
                fetch(old[u], merge[u], dst_id[u], r, old_in[u])
                if isinstance(t, int) and t == 0:
                    return
                store(now, 1 - u, P)
            over_tiles(pool, mybir.EngineType.Pool, move)
            store(ET, 0, ELAST)
            pool.wait_ge(put[0], 16 * (J + 1))
            pool.wait_ge(put[1], 16 * J)

        @block.scalar
        def _(act):
            def turn(j, u, r):
                t = 2 * j + u
                act.wait_ge(turned, t + 1)
                if later(j):
                    act.wait_ge(v_done, t - 1)
                act.activation(efT[u][:, :, 0:r], psT[:, :].rearrange("p (c e) -> p c e", c=C)[:, :, 0:r],
                               ACT.Copy).then_inc(efT_ready, 1)

            def rest_of(j, u, r):
                t = 2 * j + u
                act.wait_ge(parts_turned, t + 1)
                if not (isinstance(t, int) and t == 0):
                    act.wait_ge(spread, t)
                act.activation(partsT[:, 0:r], psA[0:3 * H, 0:r], ACT.Copy).then_inc(partsT_ready, 1)
                act.wait_ge(diff_ready, t + 1)
                if later(j):
                    act.wait_ge(new_ready, t - 1)
                    act.wait_ge(old_scaled, t - 1)
                act.activation(expd[u][0:r, :], diff[u][0:r, :], ACT.Exp, scale=SCALE).then_inc(exp_ready, 1)

            turn(0, 0, P)
            turn(0, 1, P)
            rest_of(0, 0, P)
            with nc.Fori(1, J, engines=[mybir.EngineType.Activation]) as i:
                j = act.snap(i)
                turn(j, 0, P)
                rest_of(j - 1, 1, P)
                turn(j, 1, P)
                rest_of(j, 0, P)
            turn(J, 0, ELAST)
            rest_of(J - 1, 1, P)
            rest_of(J, 0, ELAST)

        @block.vector
        def _(dve):
            def merge_step(j, u, r):
                t = 2 * j + u
                dve.wait_ge(summed, t + 1)
                sums = psS[0:r, :, 0:4 * HW].rearrange("p b (h e) -> p b h e", e=HW)
                dve.tensor_tensor(sums, sums, bc(expd[u][0:r, 2 * H:3 * H].rearrange("p (b h) -> p b h", b=2), HW),
                                  ALU.mult).then_inc(sum_scaled, 1)
                dve.wait_ge(sum_scaled, t + 1)
                dve.wait_ge(old_scaled, t + 1)
                dve.tensor_tensor(new[u][0:r, 0:ROW].rearrange("p (b e) -> p b e", b=2), psS[0:r, :, 0:4 * HW],
                                  old[u][0:r, 0:ROW].rearrange("p (b e) -> p b e", b=2), ALU.add).then_inc(new_ready, 1)

            def tile(j, u, r):
                t = 2 * j + u
                first = isinstance(t, int) and t == 0
                dve.wait_ge(ids_in[u], 48 * (j + 1))
                dve.tensor_copy(dst_f[u][0:r, :], dst_id[u][0:r, :]).then_inc(dstf_ready, 1)
                dve.wait_ge(dstf_ready, t + 1)
                if later(j):
                    dve.wait_ge(summed, t - 1)
                dve.tensor_scalar(same[u][0:r, 0:r], dst_row[u][0:r, 0:r], dst_f[u][0:r, 0:1], None,
                                  ALU.is_equal).then_inc(same_ready, 1)
                dve.wait_ge(same_ready, t + 1)
                dve.tensor_scalar(apart[u][0:r, 0:r], same[u][0:r, 0:r], -1.0, -NEG, ALU.add,
                                  ALU.mult).then_inc(apart_ready, 1)
                dve.wait_ge(consts, 5)
                if not first:
                    dve.wait_ge(putid_ready, t)
                dve.tensor_tensor_reduce(out=junk[0:r, 0:r], in0=same[u][0:r, 0:r], in1=before[0:r, 0:r], scale=OOB,
                                         scalar=0.0, op0=ALU.mult, op1=ALU.add,
                                         accum_out=count[0:r, 0:1]).then_inc(counted, 1)
                dve.wait_ge(counted, t + 1)
                if later(j):
                    dve.wait_ge(put[u], 16 * j)
                dve.tensor_tensor(put_id[u][0:r, :], count[0:r, :], dst_f[u][0:r, :], ALU.add).then_inc(putid_ready, 1)
                dve.wait_ge(k_done, t + 1)
                dve.wait_ge(kv_in[u], 16 * (j + 1))
                dve.tensor_tensor(psK[0:r, :], psK[0:r, :], kv[u][0:r, 0:D], ALU.add).then_inc(k_added, 1)
                dve.wait_ge(k_added, t + 1)
                dve.wait_ge(q_in[u], 16 * (j + 1))
                dve.tensor_tensor(psK[0:r, :], psK[0:r, :], qc[u][0:r, 0:D], ALU.mult).then_inc(k_times_q, 1)
                dve.wait_ge(k_times_q, t + 1)
                dve.tensor_reduce(score0[0:r, :], psK[0:r, :].rearrange("p (h d) -> p h d", h=H), AX.X,
                                  ALU.add).then_inc(k_summed, 1)
                dve.wait_ge(k_summed, t + 1)
                if later(j):
                    dve.wait_ge(diff_ready, t - 1)
                dve.tensor_tensor(score[u][0:r, :], score0[0:r, :], qc[u][0:r, D:QROW], ALU.add).then_inc(score_ready, 1)
                dve.wait_ge(score_ready, t + 1)
                if not first:
                    dve.wait_ge(parts_turned, t)
                dve.tensor_copy(parts[0:r, 0:H], score[u][0:r, :]).then_inc(part_step, 1)
                dve.wait_ge(part_step, 4 * t + 1)
                dve.tensor_tensor(rest[0:r, 0, :], score[u][0:r, :], parts[0:r, 0:H], ALU.subtract).then_inc(part_step, 1)
                dve.wait_ge(part_step, 4 * t + 2)
                dve.tensor_copy(parts[0:r, H:2 * H], rest[0:r, 0, :]).then_inc(part_step, 1)
                dve.wait_ge(part_step, 4 * t + 3)
                dve.tensor_tensor(rest[0:r, 1, :], rest[0:r, 0, :], parts[0:r, H:2 * H], ALU.subtract).then_inc(part_step, 1)
                dve.wait_ge(part_step, 4 * t + 4)
                dve.tensor_copy(parts[0:r, 2 * H:3 * H], rest[0:r, 1, :]).then_inc(parts_ready, 1)
                dve.wait_ge(v_done, t + 1)
                dve.tensor_tensor(psV[0:r, :], psV[0:r, :], kv[u][0:r, D:2 * D], ALU.add).then_inc(v_added, 1)
                if not first:
                    merge_step(j if u == 1 else j - 1, 1 - u, P)
                dve.wait_ge(spread, t + 1)
                dve.tensor_reduce(top[u][0:r, :], psB[0:r, :, 0:4 * r].rearrange("p b (h e) -> p b h e", h=4), AX.X,
                                  ALU.max).then_inc(top_ready, 1)
                dve.wait_ge(top_ready, t + 1)
                dve.wait_ge(old_in[u], 16 * (j + 1))
                dve.tensor_tensor(new[u][0:r, ROW:TROW], old[u][0:r, ROW:TROW], top[u][0:r, :], ALU.max).then_inc(newmax_ready, 1)
                dve.tensor_tensor(diff[u][0:r, 0:H], score[u][0:r, :], top[u][0:r, :], ALU.subtract).then_inc(diff_step, 1)
                dve.wait_ge(newmax_ready, t + 1)
                dve.tensor_tensor(diff[u][0:r, H:2 * H], old[u][0:r, ROW:TROW], new[u][0:r, ROW:TROW],
                                  ALU.subtract).then_inc(diff_step, 1)
                dve.wait_ge(diff_step, 2 * (t + 1))
                dve.tensor_tensor(diff[u][0:r, 2 * H:3 * H], top[u][0:r, :], new[u][0:r, ROW:TROW],
                                  ALU.subtract).then_inc(diff_ready, 1)
                dve.wait_ge(exp_ready, t + 1)
                dve.wait_ge(v_added, t + 1)
                dve.tensor_tensor(wv[u][0:r, :, 0:DH], psV[0:r, :].rearrange("p (h d) -> p h d", h=H),
                                  bc(expd[u][0:r, 0:H], DH), ALU.mult).then_inc(wv_ready, 1)
                dve.tensor_copy(wv[u][0:r, :, DH:HW], expd[u][0:r, 0:H].unsqueeze(2)).then_inc(wv_ready, 1)
            over_tiles(dve, mybir.EngineType.DVE, tile)
            merge_step(J, 0, ELAST)

        @block.tensor
        def _(pe):
            def turn(j, u, r):
                t = 2 * j + u
                pe.wait_ge(ef_in[u], 16 * (j + 1))
                if not (isinstance(t, int) and t == 0):
                    pe.wait_ge(efT_ready, t)
                for c in range(C):
                    last = pe.transpose(psT[:, c * P:c * P + r], efs[u][0:r, c * P:(c + 1) * P], ident[0:r, 0:r])
                last.then_inc(turned, 1)

            def sum_step(j, u, r):
                t = 2 * j + u
                pe.wait_ge(wv_ready, 2 * (t + 1))
                pe.wait_ge(same_ready, t + 1)
                if not (isinstance(t, int) and t == 0):
                    pe.wait_ge(new_ready, t)
                for b in range(2):
                    last = pe.matmul(psS[0:r, b, 0:4 * HW], same[u][0:r, 0:r], wv[u][0:r, 4 * b:4 * b + 4, :],
                                     start=True, stop=True)
                last.then_inc(summed, 1)

            def tile(j, u, r, ahead):
                t = 2 * j + u
                first = isinstance(t, int) and t == 0
                if ahead is not None:
                    turn(*ahead)
                pe.wait_ge(efT_ready, t + 1)
                if not first:
                    pe.wait_ge(k_summed, t)
                for c in range(C):
                    last = pe.matmul(psK[0:r, :], efT[u][:, c, 0:r], Me[:, c, 0:D], start=c == 0, stop=c == C - 1)
                last.then_inc(k_done, 1)
                if not first:
                    pe.wait_ge(wv_ready, 2 * t)
                for c in range(C):
                    last = pe.matmul(psV[0:r, :], efT[u][:, c, 0:r], Me[:, c, D:2 * D], start=c == 0, stop=c == C - 1)
                last.then_inc(v_done, 1)
                pe.wait_ge(parts_ready, t + 1)
                if not first:
                    pe.wait_ge(partsT_ready, t)
                pe.transpose(psA[0:3 * H, 0:r], parts[0:r, :], ident16[0:r, 0, 0:r]).then_inc(parts_turned, 1)
                if not first:
                    sum_step(j if u == 1 else j - 1, 1 - u, P)
                pe.wait_ge(partsT_ready, t + 1)
                pe.wait_ge(apart_ready, t + 1)
                if not first:
                    pe.wait_ge(top_ready, t)
                for b in range(2):
                    pe.matmul(psB[0:r, b, 0:4 * r].rearrange("p (h e) -> p h e", h=4), apart[u][0:r, 0:r],
                              ident16[0:r, :, 0:r], start=True, stop=True)
                    for h in range(4):
                        last = pe.matmul(psB[0:r, b, h * r:(h + 1) * r], pick[:, 4 * b + h, 0:r], partsT[:, 0:r],
                                         start=False, stop=True, skip_group_check=True)
                last.then_inc(spread, 1)

            pe.wait_ge(consts, 8)
            turn(0, 0, P)
            tile(0, 0, P, (0, 1, P))
            tile(0, 1, P, (1, 0, P))
            with nc.Fori(1, J - 1, engines=[mybir.EngineType.PE]) as i:
                j = pe.snap(i)
                tile(j, 0, P, (j, 1, P))
                tile(j, 1, P, (j + 1, 0, P))
            tile(J - 1, 0, P, (J - 1, 1, P))
            tile(J - 1, 1, P, (J, 0, ELAST))
            tile(J, 0, ELAST, None)
            sum_step(J, 0, ELAST)


def gnn_end(nc, merge, bo, gamma, beta, ident, xnT, v2, WoT, res):
    with ExitStack() as ctx:
        def sb(name, shape, dt=F32):
            return ctx.enter_context(nc.sbuf_tensor(name, shape, dt))

        def sem(name):
            return ctx.enter_context(nc.semaphore(name))

        rows = sb("rows", [P, 2, 2, TROW])
        nmax = sb("nmax", [P, H])
        dif = sb("dif", [P, 2, H])
        scl = sb("scl", [P, 2, H])
        part = sb("part", [P, 2, ROW])
        tot = sb("tot", [P, ROW])
        safe = sb("safe", [P, 3, H])
        own = sb("own2", [P, D])
        g = sb("g", [P, 2, D])
        gT = sb("gT", [P, C, NP])
        oT = sb("oT", [P, C, NP])
        col = sb("col", [P, 3, C])
        stats = sb("bstats", [P, C, 3, 6])
        mv = sb("bmv", [P, C, 2])
        sd = sb("sd", [P, 4, C])
        banks = [ctx.enter_context(nc.psum_tensor(f"gbank{i}", [P, D], F32)) for i in range(4)]
        rows_in = [sem(f"rows_in{i}") for i in range(2)]
        col_in, step, dif_done, scl_done, g_done, g_turned, gT_done, o_done, oT_done, bn, sd_in, sd_out, norm, back, added = (
            sem(n) for n in ("col_in", "merge_link", "dif_done", "scl_done", "g_done", "g_turned", "gT_done", "o_done",
                             "oT_done", "bn_link", "sd_in", "sd_out", "norm", "back", "added"))
        block = ctx.enter_context(nc.Block())
        OJ = [(c, n0, nn) for c in range(C) for n0, nn in NCH]
        REAL = [(0, 512), (512, 512), (1024, N - 1024)]

        @block.sync
        def _(sp):
            for i, v in enumerate((bo, gamma, beta)):
                sp.dma_start(col[:, i, :], v.rearrange("(c p) -> p c", p=P),
                              allow_slow_non_contiguous=True).then_inc(col_in, 16)
            for t in range(NT):
                if t >= 2:
                    sp.wait_ge(g_done, t - 1)
                for i in range(2):
                    sp.dma_start(rows[:, t % 2, i, :], merge[i][t * P:(t + 1) * P, :]).then_inc(rows_in[t % 2], 16)

        @block.vector
        def _(dve):
            links = [0]

            def link(ins):
                links[0] += 1
                ins.then_inc(step, 1)
                dve.wait_ge(step, links[0])

            for t in range(NT):
                a = rows[:, t % 2, :, :]
                dve.wait_ge(rows_in[t % 2], 32 * (t // 2 + 1))
                link(dve.tensor_tensor(nmax[:, :], a[:, 0, ROW:TROW], a[:, 1, ROW:TROW], ALU.max))
                for i in range(2):
                    last = dve.tensor_tensor(dif[:, i, :], a[:, i, ROW:TROW], nmax[:, :], ALU.subtract)
                    last.then_inc(dif_done, 1)
                dve.wait_ge(scl_done, t + 1)
                for i in range(2):
                    link(dve.tensor_tensor(part[:, i, :].rearrange("p (h e) -> p h e", e=HW),
                                           a[:, i, 0:ROW].rearrange("p (h e) -> p h e", e=HW),
                                           bc(scl[:, i, :], HW), ALU.mult))
                link(dve.tensor_tensor(tot[:, :], part[:, 0, :], part[:, 1, :], ALU.add))
                th = tot[:, :].rearrange("p (h e) -> p h e", e=HW)
                link(dve.tensor_scalar(safe[:, 0, :], th[:, :, DH], 0.0, None, ALU.is_equal))
                link(dve.tensor_tensor(safe[:, 1, :], safe[:, 0, :], th[:, :, DH], ALU.add))
                link(dve.reciprocal(safe[:, 2, :], safe[:, 1, :]))
                link(dve.tensor_scalar(safe[:, 1, :], th[:, :, DH], 0.0, None, ALU.is_gt))
                link(dve.tensor_tensor(own[:, :].rearrange("p (h d) -> p h d", h=H),
                                       v2[:, t, :].rearrange("p (h d) -> p h d", h=H), bc(safe[:, 1, :], DH), ALU.mult))
                if t >= 2:
                    dve.wait_ge(g_turned, t - 1)
                link(dve.tensor_tensor(g[:, t % 2, :].rearrange("p (h d) -> p h d", h=H), th[:, :, 0:DH],
                                       bc(safe[:, 2, :], DH), ALU.mult))
                dve.tensor_tensor(g[:, t % 2, :], g[:, t % 2, :], own[:, :], ALU.add).then_inc(g_done, 1)
                dve.wait_ge(g_done, t + 1)
            dve.wait_ge(col_in, 48)
            for j, (c, n0, nn) in enumerate(OJ):
                dve.wait_ge(o_done, j + 1)
                dve.scalar_tensor_tensor(oT[:, c, n0:n0 + nn], banks[j % 4][:, 0:nn], col[:, 0, c:c + 1],
                                         xnT[:, c, n0:n0 + nn], ALU.add, ALU.add).then_inc(oT_done, 1)
                dve.wait_ge(oT_done, j + 1)
            for c in range(C):
                for k, (n0, nn) in enumerate(REAL):
                    link(dve.bn_stats(stats[:, c, k, :], oT[:, c, n0:n0 + nn]))
                link(dve.bn_aggr(mv[:, c, :], stats[:, c, :, :].rearrange("p k s -> p (k s)")))
            dve.tensor_scalar(sd[:, 0, :], mv[:, :, 1], LN_EPS, None, ALU.add).then_inc(sd_in, 1)
            dve.wait_ge(sd_out, 1)
            link(dve.reciprocal(sd[:, 2, :], sd[:, 1, :]))
            link(dve.tensor_tensor(sd[:, 3, :], sd[:, 2, :], col[:, 1, :], ALU.mult))
            link(dve.tensor_tensor(sd[:, 0, :], mv[:, :, 0], sd[:, 3, :], ALU.mult))
            link(dve.tensor_tensor(sd[:, 2, :], col[:, 2, :], sd[:, 0, :], ALU.subtract))
            for c in range(C):
                dve.tensor_scalar(oT[:, c, :], oT[:, c, :], sd[:, 3, c:c + 1], sd[:, 2, c:c + 1], ALU.mult,
                                  ALU.add).then_inc(norm, 1)
            for t in range(NT):
                dve.wait_ge(back, t + 1)
                dve.tensor_tensor(res[:, t, :], banks[t % 4][:, :], res[:, t, :], ALU.add).then_inc(added, 1)

        @block.scalar
        def _(act):
            for t in range(NT):
                act.wait_ge(dif_done, 2 * (t + 1))
                act.activation(scl[:, :, :], dif[:, :, :], ACT.Exp, scale=SCALE).then_inc(scl_done, 1)
                act.wait_ge(g_turned, t + 1)
                act.activation(gT[:, :, t * P:(t + 1) * P], banks[t % 4][:, :].rearrange("p (c e) -> p c e", c=C),
                               ACT.Copy).then_inc(gT_done, 1)
            act.wait_ge(sd_in, 1)
            act.activation(sd[:, 1, :], sd[:, 0, :], ACT.Sqrt).then_inc(sd_out, 1)

        @block.tensor
        def _(pe):
            for t in range(NT):
                pe.wait_ge(g_done, t + 1)
                if t >= 4:
                    pe.wait_ge(gT_done, t - 3)
                for c in range(C):
                    last = pe.transpose(banks[t % 4][:, c * P:(c + 1) * P], g[:, t % 2, c * P:(c + 1) * P], ident[:, :])
                last.then_inc(g_turned, 1)
            pe.wait_ge(gT_done, NT)
            for j, (c, n0, nn) in enumerate(OJ):
                if j >= 4:
                    pe.wait_ge(oT_done, j - 3)
                for k in range(C):
                    last = pe.matmul(banks[j % 4][:, 0:nn], WoT[:, k, c * P:(c + 1) * P], gT[:, k, n0:n0 + nn],
                                     start=k == 0, stop=k == C - 1)
                last.then_inc(o_done, 1)
            pe.wait_ge(norm, C)
            for t in range(NT):
                if t >= 4:
                    pe.wait_ge(added, t - 3)
                for c in range(C):
                    last = pe.transpose(banks[t % 4][:, c * P:(c + 1) * P], oT[:, c, t * P:(t + 1) * P], ident[:, :])
                last.then_inc(back, 1)


def ffn(nc, w_up, w_down, ident, res, out):
    with ExitStack() as ctx:
        def sb(name, shape, dt=F32):
            return ctx.enter_context(nc.sbuf_tensor(name, shape, dt))

        def sem(name):
            return ctx.enter_context(nc.semaphore(name))

        UC, DC = FF // P, C
        wu = sb("wu", [P, UC, D])
        wd = sb("wd", [P, DC, FF])
        tern = sb("tern", [P, 2, 2 * D])
        tern16 = sb("tern16", [P, 2, 2 * D], BF16)
        wuT = sb("wuT", [P, C, FF], BF16)
        wdT = sb("wdT", [P, UC, D], BF16)
        ident_b = sb("ident_b", [P, P], BF16)
        sums = sb("sums", [P, 2])
        onem = sb("onem", [P, P])
        wsc = sb("wsc", [P, 3, 2])
        stats = sb("fstats", [P, NT, 6])
        mv = sb("fmv", [P, NT, 2])
        sd = sb("fsd", [P, 3, NT])
        xn = sb("fxn", [P, D])
        xs = sb("xs", [P, 2, 4])
        xq = sb("xq", [P, D])
        xq16 = sb("xq16", [P, 2, D], BF16)
        xqT = sb("xqT", [P, 2, D], BF16)
        hid = sb("hid", [P, FF])
        hs = sb("hs", [P, 2, 4])
        hq16 = sb("hq16", [P, 2, FF], BF16)
        hqT = sb("hqT", [P, 2, FF], BF16)
        y = sb("fy", [P, 2, D])
        pw = ctx.enter_context(nc.psum_tensor("pw", [P, D], F32))
        pt = ctx.enter_context(nc.psum_tensor("pt", [P, 2 * D], BF16))
        ph = [ctx.enter_context(nc.psum_tensor(f"ph{i}", [P, D], F32)) for i in range(2)]
        pht = ctx.enter_context(nc.psum_tensor("pht", [P, 2 * D], BF16))
        py = [ctx.enter_context(nc.psum_tensor(f"py{i}", [P, D], F32)) for i in range(2)]
        w_in, cst, idb, step, total, sd_in, sd_out = (sem(n) for n in (
            "fw_in", "fcst", "fidb", "ffn_link", "w_total", "fsd_in", "fsd_out"))
        w_ready, w_turned, w_copied = sem("w_ready"), sem("fw_turned"), sem("fw_copied")
        x_ready, x_turned, xT_ready, h_done, h_ready, h_turned, hT_ready, y_done, y_ready = (sem(n) for n in (
            "fx_ready", "fx_turned", "fxT_ready", "fh_done", "fh_ready", "fh_turned", "fhT_ready", "fy_done", "fy_ready"))
        stored = [sem(f"stored{i}") for i in range(2)]
        block = ctx.enter_context(nc.Block())

        @block.sync
        def _(sp):
            sp.dma_start(wu[:, :, :], w_up.rearrange("(c p) i -> p c i", p=P)).then_inc(w_in, 16)
            sp.dma_start(wd[:, :, :], w_down.rearrange("(c p) i -> p c i", p=P)).then_inc(w_in, 16)
            for t in range(NT):
                sp.wait_ge(y_ready, t + 1)
                r = node_rows(t)
                sp.dma_start(out[t * P:t * P + r, :], y[0:r, t % 2, :]).then_inc(stored[t % 2], 16)
            sp.wait_ge(stored[0], 16 * (NT // 2))
            sp.wait_ge(stored[1], 16 * (NT // 2))

        @block.gpsimd
        def _(pool):
            pool.memset(onem[:, :], 1.0).then_inc(cst, 1)

        @block.vector
        def _(dve):
            links = [0]

            def link(ins):
                links[0] += 1
                ins.then_inc(step, 1)
                dve.wait_ge(step, links[0])

            dve.tensor_copy(ident_b[:, :], ident[:, :]).then_inc(idb, 1)
            dve.wait_ge(w_in, 32)
            flat = [wu[:, :, :].rearrange("p a b -> p (a b)"), wd[:, :, :].rearrange("p a b -> p (a b)")]
            for i in range(2):
                link(dve.tensor_reduce(sums[:, i:i + 1], flat[i], AX.X, ALU.add, apply_absolute_value=True))
            dve.wait_ge(total, 1)
            link(dve.tensor_scalar(wsc[:, 0, :], pw[:, 0:2], 1.0 / (FF * D), LN_EPS, ALU.mult, ALU.max))
            link(dve.reciprocal(wsc[:, 1, :], wsc[:, 0, :]))
            for i in range(2):
                link(dve.tensor_scalar(tern[:, i, :], flat[i], wsc[:, 1, i:i + 1], RINT, ALU.mult, ALU.add))
                link(dve.tensor_scalar(tern[:, i, :], tern[:, i, :], -RINT, -1.0, ALU.add, ALU.max))
                dve.tensor_scalar(tern16[:, i, :], tern[:, i, :], 1.0, None, ALU.min).then_inc(w_ready, 1)
            for t in range(NT):
                link(dve.bn_stats(stats[:, t, :], res[:, t, :]))
                link(dve.bn_aggr(mv[:, t, :], stats[:, t, :]))
            dve.tensor_scalar(sd[:, 0, :], mv[:, :, 1], LN_EPS, None, ALU.add).then_inc(sd_in, 1)
            dve.wait_ge(sd_out, 1)
            link(dve.reciprocal(sd[:, 2, :], sd[:, 1, :]))

            def quantise(t):
                s = xs[:, t % 2, :]
                link(dve.tensor_scalar(xn[:, :], res[:, t, :], mv[:, t, 0:1], sd[:, 2, t:t + 1], ALU.subtract, ALU.mult))
                link(dve.tensor_reduce(s[:, 0:1], xn[:, :], AX.X, ALU.max, apply_absolute_value=True))
                link(dve.tensor_scalar(s[:, 0:1], s[:, 0:1], LN_EPS, None, ALU.max))
                link(dve.reciprocal(s[:, 1:2], s[:, 0:1]))
                link(dve.tensor_scalar(s[:, 2:3], s[:, 1:2], 127.0, None, ALU.mult))
                link(dve.tensor_scalar(s[:, 3:4], s[:, 0:1], 1.0 / 127.0, wsc[:, 0, 0:1], ALU.mult, ALU.mult))
                link(dve.tensor_scalar(xq[:, :], xn[:, :], s[:, 2:3], RINT, ALU.mult, ALU.add))
                link(dve.tensor_scalar(xq[:, :], xq[:, :], -RINT, -128.0, ALU.add, ALU.max))
                if t >= 2:
                    dve.wait_ge(x_turned, t - 1)
                dve.tensor_scalar(xq16[:, t % 2, :], xq[:, :], 127.0, None, ALU.min).then_inc(x_ready, 1)
                dve.wait_ge(x_ready, t + 1)

            def hidden(t):
                s = hs[:, t % 2, :]
                dve.wait_ge(h_done, t + 1)
                link(dve.tensor_scalar(hid[:, :], ph[t % 2][:, 0:FF], xs[:, t % 2, 3:4], 0.0, ALU.mult, ALU.max))
                link(dve.tensor_scalar(hid[:, :], hid[:, :], RINT, -RINT, ALU.add, ALU.add))
                link(dve.tensor_scalar(hid[:, :], hid[:, :], 127.0, None, ALU.min))
                link(dve.tensor_reduce(s[:, 0:1], hid[:, :], AX.X, ALU.max))
                link(dve.tensor_scalar(s[:, 0:1], s[:, 0:1], LN_EPS, None, ALU.max))
                link(dve.reciprocal(s[:, 1:2], s[:, 0:1]))
                link(dve.tensor_scalar(s[:, 2:3], s[:, 1:2], 127.0, None, ALU.mult))
                link(dve.tensor_scalar(s[:, 3:4], s[:, 0:1], 1.0 / 127.0, wsc[:, 0, 1:2], ALU.mult, ALU.mult))
                link(dve.tensor_scalar(hid[:, :], hid[:, :], s[:, 2:3], RINT, ALU.mult, ALU.add))
                link(dve.tensor_scalar(hid[:, :], hid[:, :], -RINT, 127.0, ALU.add, ALU.min))
                if t >= 2:
                    dve.wait_ge(h_turned, t - 1)
                dve.tensor_copy(hq16[:, t % 2, :], hid[:, :]).then_inc(h_ready, 1)
                dve.wait_ge(h_ready, t + 1)

            def finish(t):
                dve.wait_ge(y_done, t + 1)
                if t >= 2:
                    dve.wait_ge(stored[t % 2], 16 * (t // 2))
                dve.scalar_tensor_tensor(y[:, t % 2, :], py[t % 2][:, :], hs[:, t % 2, 3:4], res[:, t, :],
                                         ALU.mult, ALU.add).then_inc(y_ready, 1)
                dve.wait_ge(y_ready, t + 1)

            quantise(0)
            for t in range(NT):
                if t + 1 < NT:
                    quantise(t + 1)
                hidden(t)
                if t >= 1:
                    finish(t - 1)
            finish(NT - 1)

        @block.scalar
        def _(act):
            for k in range(3):
                act.wait_ge(w_turned, k + 1)
                if k < 2:
                    act.activation(wuT[:, :, k * P:(k + 1) * P], pt[:, 0:D].rearrange("p (c f) -> p c f", c=C),
                                   ACT.Copy).then_inc(w_copied, 1)
                else:
                    act.activation(wdT[:, :, :], pt[:, :].rearrange("p (a o) -> p a o", a=UC), ACT.Copy).then_inc(w_copied, 1)
            act.wait_ge(sd_in, 1)
            act.activation(sd[:, 1, :], sd[:, 0, :], ACT.Sqrt).then_inc(sd_out, 1)

            def x_copy(t):
                act.wait_ge(x_turned, t + 1)
                if t >= 2:
                    act.wait_ge(h_done, t - 1)
                act.activation(xqT[:, t % 2, :], pt[:, 0:D], ACT.Copy).then_inc(xT_ready, 1)

            x_copy(0)
            for t in range(NT):
                if t + 1 < NT:
                    x_copy(t + 1)
                act.wait_ge(h_turned, t + 1)
                if t >= 2:
                    act.wait_ge(y_done, t - 1)
                act.activation(hqT[:, t % 2, :], pht[:, 0:FF], ACT.Copy).then_inc(hT_ready, 1)

        @block.tensor
        def _(pe):
            pe.wait_ge(cst, 1)
            pe.wait_ge(step, 2)
            pe.matmul(pw[:, 0:2], onem[:, :], sums[:, :], start=True, stop=True).then_inc(total, 1)
            pe.wait_ge(idb, 1)
            pe.wait_ge(w_ready, 1)
            for k in range(2):
                if k:
                    pe.wait_ge(w_copied, k)
                for c in range(C):
                    last = pe.transpose(pt[:, c * P:(c + 1) * P], tern16[:, 0, k * D + c * P:k * D + (c + 1) * P], ident_b[:, :])
                last.then_inc(w_turned, 1)
            pe.wait_ge(w_ready, 2)
            pe.wait_ge(w_copied, 2)
            for a in range(UC):
                for o in range(DC):
                    last = pe.transpose(pt[:, a * D + o * P:a * D + (o + 1) * P],
                                        tern16[:, 1, o * FF + a * P:o * FF + (a + 1) * P], ident_b[:, :])
            last.then_inc(w_turned, 1)
            pe.wait_ge(w_copied, 3)

            def up(t):
                pe.wait_ge(x_ready, t + 1)
                if t >= 1:
                    pe.wait_ge(xT_ready, t)
                for c in range(C):
                    last = pe.transpose(pt[:, c * P:(c + 1) * P], xq16[:, t % 2, c * P:(c + 1) * P], ident_b[:, :])
                last.then_inc(x_turned, 1)
                pe.wait_ge(xT_ready, t + 1)
                if t >= 2:
                    pe.wait_ge(h_ready, t - 1)
                for c in range(C):
                    last = pe.matmul(ph[t % 2][:, 0:FF], xqT[:, t % 2, c * P:(c + 1) * P], wuT[:, c, :],
                                     start=c == 0, stop=c == C - 1)
                last.then_inc(h_done, 1)

            def down(t):
                pe.wait_ge(h_ready, t + 1)
                if t >= 1:
                    pe.wait_ge(hT_ready, t)
                for a in range(UC):
                    last = pe.transpose(pht[:, a * P:(a + 1) * P], hq16[:, t % 2, a * P:(a + 1) * P], ident_b[:, :])
                last.then_inc(h_turned, 1)
                pe.wait_ge(hT_ready, t + 1)
                if t >= 2:
                    pe.wait_ge(y_ready, t - 1)
                for a in range(UC):
                    last = pe.matmul(py[t % 2][:, :], hqT[:, t % 2, a * P:(a + 1) * P], wdT[:, a, :],
                                     start=a == 0, stop=a == UC - 1)
                last.then_inc(y_done, 1)

            up(0)
            for t in range(NT):
                if t + 1 < NT:
                    up(t + 1)
                down(t)


_INS = ["x", "src", "dst", "edge_attr_512", "L0_gnn_Wq", "L0_gnn_bq", "L0_gnn_Wr", "L0_gnn_br", "L0_gnn_Wk", "L0_gnn_bk",
        "L0_gnn_Wv", "L0_gnn_bv", "L0_gnn_Wo", "L0_gnn_bo", "L0_gnn_gamma", "L0_gnn_beta", "L0_mix_w_qkv",
        "L0_mix_w_proj", "L0_mix_b_proj", "L0_ffn_w_up", "L0_ffn_w_down"]


def kernel(**inputs):
    import numpy as _np
    import concourse.bacc as _bacc
    from concourse import mybir as _mybir
    from concourse.bass_utils import run_bass_kernel_spmd as _run

    nc = _bacc.Bacc("TRN2", target_bir_lowering=False, num_devices=1)
    arrays, args = {}, []
    for name in _INS:
        a = _np.ascontiguousarray(inputs[name])
        arrays[f"in_{name}_dram"] = a
        args.append(nc.dram_tensor(f"in_{name}_dram", a.shape, _mybir.dt.from_np(a.dtype), kind="ExternalInput").ap())
    out = nc.dram_tensor("out_dram", [N, D], _mybir.dt.float32, kind="ExternalOutput").ap()
    layer(nc, *args, out)
    r = _run(nc, [arrays], core_ids=[0])
    return r.results[0]["out_dram"]
```

```python
import numpy as np
import concourse.bass as bass
from concourse import mybir
from contextlib import ExitStack

F32 = mybir.dt.float32
F32R = mybir.dt.float32r
BF16 = mybir.dt.bfloat16
I32 = mybir.dt.int32
ALU = mybir.AluOpType
ACT = mybir.ActivationFunctionType
AX = mybir.AxisListType

P = 128
N, D, E, H = 1250, 512, 20000, 8
DH = D // H
C = D // P
NT = -(-N // P)
NP = NT * P
NLAST = N - (NT - 1) * P
ET = -(-E // P)
ELAST = E - (ET - 1) * P
HW = DH + 1
ROW = H * HW
TROW = ROW + H
QROW = D + H
FF = 256
SCALE = 1.0 / 8.0
NEG = -3.0e38
OOB = 2048.0
LN_EPS = 1e-5
MIX_EPS = 1e-6
RINT = 12582912.0
NCH = [(0, 512), (512, 512), (1024, 256)]


def node_rows(t):
    return P if t < NT - 1 else NLAST


def bc(ap, n):
    return ap.unsqueeze(len(ap.shape)).to_broadcast(list(ap.shape) + [n])


def layer(nc, x, src, dst, ef, Wq, bq, Wr, br, Wk, bk, Wv, bv, Wo, bo, gamma, beta,
          w_qkv, w_proj, b_proj, w_up, w_down, out):
    q_table = nc.dram_tensor("q_table", [NP, QROW], F32, kind="Internal").ap()
    kv_table = nc.dram_tensor("kv_table", [NP, 2 * D], F32, kind="Internal").ap()
    merge = [nc.dram_tensor(f"merge{i}", [NP, TROW], F32, kind="Internal").ap() for i in range(2)]

    top = ExitStack()
    with top:
        def keep(name, shape, dt=F32):
            return top.enter_context(nc.sbuf_tensor(name, shape, dt))

        ident = keep("ident", [P, P])
        xnT = keep("xnT", [P, C, NP])
        res = keep("res", [P, NT, D])
        v2 = keep("v2", [P, NT, D])
        WoT = keep("WoT", [P, C, D])
        Me_hi = keep("Me_hi", [P, C, 2 * D], F32R)
        Me_lo = keep("Me_lo", [P, C, 2 * D], F32R)
        ones = keep("ones", [1, P])

        with ExitStack() as mid:
            def sb(name, shape, dt=F32):
                return mid.enter_context(nc.sbuf_tensor(name, shape, dt))
            Mn = sb("Mn", [P, 2, C, 2 * D])
            WqT = sb("WqT", [P, C, D])
            kv_bias = sb("kv_bias", [1, 2 * D])
            prepare(nc, x, Wq, bq, Wr, br, Wk, bk, Wv, bv, Wo, ident, ones, xnT, res, WqT, WoT, Me_hi, Me_lo, Mn, kv_bias, v2)
            node_tables(nc, bq, q_table, kv_table, merge, xnT, ones, WqT, Mn, kv_bias, v2)
        mix_branch(nc, w_qkv, w_proj, b_proj, xnT, ident, ones, res)
        edges(nc, src, dst, ef, q_table, kv_table, merge, ident, Me_hi, Me_lo)
        gnn_end(nc, merge, bo, gamma, beta, ident, xnT, v2, WoT, res)
        ffn(nc, w_up, w_down, ident, res, out)


def prepare(nc, x, Wq, bq, Wr, br, Wk, bk, Wv, bv, Wo, ident, ones, xnT, res, WqT, WoT, Me_hi, Me_lo, Mn, kv_bias, v2):
    with ExitStack() as ctx:
        def sb(name, shape, dt=F32):
            return ctx.enter_context(nc.sbuf_tensor(name, shape, dt))

        def sem(name):
            return ctx.enter_context(nc.semaphore(name))

        raw = sb("raw", [P, C, D])
        raw2 = sb("raw2", [P, C, D])
        wr = sb("wr", [P, C, 3 * D])
        WkT = sb("WkT", [P, C, D])
        WvT = sb("WvT", [P, C, D])
        br_col = sb("br_col", [P, C])
        bkv = sb("bkv", [1, 2 * D])
        stats = sb("stats", [P, NT, 6])
        mv = sb("mv", [P, NT, 2])
        std = sb("std", [P, NT])
        rstd = sb("rstd", [P, NT])
        xn = v2[:, 0:2, :]
        banks = [ctx.enter_context(nc.psum_tensor(f"bank{i}", [P, D], F32)) for i in range(8)]
        x_clear, x_in, w_in = sem("x_clear"), sem("x_in"), [sem(f"w_in{i}") for i in range(4)]
        wr_in, small_in = sem("wr_in"), sem("small_in")
        ident_step, ones_set = sem("ident_step"), sem("ones_set")
        stats_done, mv_done, var_eps, std_done, rstd_done, xn_done = (
            sem("stats_done"), sem("mv_done"), sem("var_eps"), sem("std_done"), sem("rstd_done"), sem("xn_done"))
        turned, copied = sem("turned"), sem("copied")
        folded, fold_copied, hi_ready = sem("folded"), sem("fold_copied"), sem("hi_ready")
        block = ctx.enter_context(nc.Block())
        raws = [raw, raw2]
        weights = [(Wk, WkT), (Wv, WvT), (Wq, WqT), (Wo, WoT)]

        @block.sync
        def _(sp):
            sp.wait_ge(x_clear, 1)
            sp.dma_start(res[:, 0:NT - 1, :], x[0:(NT - 1) * P, :].rearrange("(t p) d -> p t d", p=P)).then_inc(x_in, 16)
            sp.dma_start(res[0:NLAST, NT - 1, :], x[(NT - 1) * P:N, :]).then_inc(x_in, 16)
            for i, (w, _) in enumerate(weights):
                if i >= 2:
                    sp.wait_ge(turned, C * (i - 1))
                sp.dma_start(raws[i % 2][:, :, :], w.rearrange("(c p) i -> p c i", p=P)).then_inc(w_in[i], 16)

        @block.gpsimd
        def _(pool):
            pool.memset(ident[:, :], 0.0).then_inc(ident_step, 1)
            pool.memset(ones[:, :], 1.0).then_inc(ones_set, 1)
            pool.wait_ge(ident_step, 1)
            pool.affine_select(out=ident[:, :], in_=ident[:, :], compare_op=ALU.not_equal, fill=1.0, base=0,
                               pattern=[[-1, P]], channel_multiplier=1).then_inc(ident_step, 1)

        @block.vector
        def _(dve):
            dve.memset(res[:, NT - 1, :], 0.0).then_inc(x_clear, 1)
            dve.wait_ge(x_in, 32)
            for t in range(NT):
                dve.bn_stats(stats[:, t, :], res[:, t, :]).then_inc(stats_done, 1)
            for t in range(NT):
                dve.wait_ge(stats_done, t + 1)
                dve.bn_aggr(mv[:, t, :], stats[:, t, :]).then_inc(mv_done, 1)
            dve.wait_ge(mv_done, NT)
            dve.tensor_scalar(std[:, :], mv[:, :, 1], LN_EPS, None, ALU.add).then_inc(var_eps, 1)
            dve.wait_ge(std_done, 1)
            dve.reciprocal(rstd[:, :], std[:, :]).then_inc(rstd_done, 1)
            dve.wait_ge(rstd_done, 1)
            for t in range(NT):
                if t >= 2:
                    dve.wait_ge(turned, 4 * C + t - 1)
                dve.tensor_scalar(xn[:, t % 2, :], res[:, t, :], mv[:, t, 0:1], rstd[:, t:t + 1],
                                  ALU.subtract, ALU.mult).then_inc(xn_done, 1)
            for k in range(16, 24):
                ic, half = k // 2 % C, k % 2
                dve.wait_ge(hi_ready, k - 15)
                dve.tensor_tensor(Me_lo[:, ic, half * D:(half + 1) * D], banks[k % 8][:, :],
                                  Me_hi[:, ic, half * D:(half + 1) * D].bitcast(F32), ALU.subtract).then_inc(fold_copied, 1)
            dve.wait_ge(small_in, 48)
            for half in range(2):
                dve.wait_ge(folded, 24 + half + 1)
                dve.tensor_tensor(kv_bias[0:1, half * D:(half + 1) * D], banks[half][0:1, :],
                                  bkv[0:1, half * D:(half + 1) * D], ALU.add).then_inc(fold_copied, 1)

        @block.scalar
        def _(act):
            act.dma_start(wr[:, :, :], Wr.rearrange("(c p) i -> p c i", p=P)).then_inc(wr_in, 16)
            act.dma_start(br_col[:, :], br.rearrange("(c p) -> p c", p=P),
                              allow_slow_non_contiguous=True).then_inc(small_in, 16)
            act.dma_start(bkv[:, 0:D], bk.unsqueeze(0)).then_inc(small_in, 16)
            act.dma_start(bkv[:, D:2 * D], bv.unsqueeze(0)).then_inc(small_in, 16)
            act.wait_ge(var_eps, 1)
            act.activation(std[:, :], std[:, :], ACT.Sqrt).then_inc(std_done, 1)
            for k in range(4 * C + NT):
                act.wait_ge(turned, k + 1)
                bank = banks[k % 8][:, :].rearrange("p (c o) -> p c o", c=C)
                if k < 4 * C:
                    to = weights[k // C][1][:, :, (k % C) * P:(k % C + 1) * P]
                else:
                    to = xnT[:, :, (k - 4 * C) * P:(k - 4 * C + 1) * P]
                act.activation(to, bank, ACT.Copy).then_inc(copied, 1)
            for k in range(24):
                act.wait_ge(folded, k + 1)
                part, ic, half = k // 8, k // 2 % C, k % 2
                if part == 2:
                    act.activation(Me_hi[:, ic, half * D:(half + 1) * D], banks[k % 8][:, :], ACT.Copy).then_inc(hi_ready, 1)
                else:
                    act.activation(Mn[:, part, ic, half * D:(half + 1) * D], banks[k % 8][:, :],
                                   ACT.Copy).then_inc(fold_copied, 1)

        @block.tensor
        def _(pe):
            pe.wait_ge(ident_step, 2)
            for k in range(4 * C + NT):
                if k >= 8:
                    pe.wait_ge(copied, k - 7)
                if k < 4 * C:
                    pe.wait_ge(w_in[k // C], 16)
                    source = raws[(k // C) % 2][:, k % C, :]
                else:
                    pe.wait_ge(xn_done, k - 4 * C + 1)
                    source = xn[:, (k - 4 * C) % 2, :]
                for c in range(C):
                    last = pe.transpose(banks[k % 8][:, c * P:(c + 1) * P], source[:, c * P:(c + 1) * P], ident[:, :])
                last.then_inc(turned, 1)
            pe.wait_ge(wr_in, 16)
            pe.wait_ge(copied, 4 * C + NT)
            for k in range(24):
                part, ic, half = k // 8, k // 2 % C, k % 2
                if k >= 8:
                    pe.wait_ge(fold_copied, k - 7)
                for rc in range(C):
                    last = pe.matmul(banks[k % 8][:, :], wr[:, rc, part * D + ic * P:part * D + (ic + 1) * P],
                                     (WkT, WvT)[half][:, rc, :], start=rc == 0, stop=rc == C - 1)
                last.then_inc(folded, 1)
            pe.wait_ge(small_in, 48)
            pe.wait_ge(fold_copied, 24)
            for half in range(2):
                for rc in range(C):
                    last = pe.matmul(banks[half][0:1, :], br_col[:, rc:rc + 1], (WkT, WvT)[half][:, rc, :],
                                     start=rc == 0, stop=rc == C - 1)
                last.then_inc(folded, 1)


def node_tables(nc, bq, q_table, kv_table, merge, xnT, ones, WqT, Mn, kv_bias, v2):
    with ExitStack() as ctx:
        def sb(name, shape, dt=F32):
            return ctx.enter_context(nc.sbuf_tensor(name, shape, dt))

        def sem(name):
            return ctx.enter_context(nc.semaphore(name))

        bq_row = sb("bq_row", [1, D])
        q_out = sb("q_out", [P, 2, QROW])
        kv_out = sb("kv_out", [P, 2, 2 * D])
        own = sb("own", [P, D])
        empty = sb("empty", [P, TROW])
        banks = [ctx.enter_context(nc.psum_tensor(f"nbank{i}", [P, D], F32)) for i in range(5)]
        bq_in, done, empty_set, tables_out = sem("bq_in"), sem("done"), sem("empty_set"), sem("tables_out")
        q_copied, kv_copied, own_mul, own_sum, v2_copied = (
            sem("q_copied"), sem("kv_copied"), sem("own_mul"), sem("own_sum"), sem("v2_copied"))
        q_stored = [sem(f"q_stored{i}") for i in range(2)]
        kv_stored = [sem(f"kv_stored{i}") for i in range(2)]
        block = ctx.enter_context(nc.Block())

        @block.sync
        def _(sp):
            sp.dma_start(bq_row[:, :], bq.unsqueeze(0)).then_inc(bq_in, 16)
            for t in range(NT):
                sp.wait_ge(kv_copied, 2 * (t + 1))
                sp.dma_start(kv_table[t * P:(t + 1) * P, :], kv_out[:, t % 2, :]).then_inc(kv_stored[t % 2], 16)
                sp.wait_ge(own_sum, t + 1)
                sp.dma_start(q_table[t * P:(t + 1) * P, :], q_out[:, t % 2, :]).then_inc(q_stored[t % 2], 16)
            for i in range(2):
                sp.wait_ge(kv_stored[i], 16 * (NT // 2))
                sp.wait_ge(q_stored[i], 16 * (NT // 2))

        @block.gpsimd
        def _(pool):
            pool.memset(empty[:, 0:ROW], 0.0).then_inc(empty_set, 1)
            pool.memset(empty[:, ROW:TROW], NEG).then_inc(empty_set, 1)
            pool.wait_ge(empty_set, 2)
            for i in range(2):
                for t in range(NT):
                    pool.dma_start(merge[i][t * P:(t + 1) * P, :], empty[:, :]).then_inc(tables_out, 16)
            pool.wait_ge(tables_out, 16 * 2 * NT)

        @block.tensor
        def _(pe):
            pe.wait_ge(bq_in, 16)
            for t in range(NT):
                for b in range(5):
                    if t >= 1:
                        if b == 0:
                            pe.wait_ge(q_copied, t)
                        elif b <= 2:
                            pe.wait_ge(kv_copied, 2 * (t - 1) + b)
                        elif b == 3:
                            pe.wait_ge(own_mul, t)
                        else:
                            pe.wait_ge(v2_copied, t)
                    for c in range(C):
                        rhs = WqT[:, c, :] if b == 0 else Mn[:, (b - 1) // 2, c, ((b - 1) % 2) * D:((b - 1) % 2 + 1) * D]
                        last = pe.matmul(banks[b][:, :], xnT[:, c, t * P:(t + 1) * P], rhs,
                                         start=c == 0, stop=c == C - 1 and b in (1, 2))
                    if b == 0:
                        last = pe.matmul(banks[b][:, :], ones[:, :], bq_row[:, :], start=False, stop=True)
                    elif b >= 3:
                        last = pe.matmul(banks[b][:, :], ones[:, :], kv_bias[:, (b - 3) * D:(b - 2) * D],
                                         start=False, stop=True)
                    last.then_inc(done, 1)

        @block.scalar
        def _(act):
            for t in range(NT):
                act.wait_ge(done, 5 * t + 1)
                if t >= 2:
                    act.wait_ge(q_stored[t % 2], 16 * (t // 2))
                act.activation(q_out[:, t % 2, 0:D], banks[0][:, :], ACT.Copy).then_inc(q_copied, 1)
                if t >= 2:
                    act.wait_ge(kv_stored[t % 2], 16 * (t // 2))
                for half in range(2):
                    act.wait_ge(done, 5 * t + 2 + half)
                    act.activation(kv_out[:, t % 2, half * D:(half + 1) * D], banks[1 + half][:, :],
                                   ACT.Copy).then_inc(kv_copied, 1)
                act.wait_ge(done, 5 * t + 5)
                act.activation(v2[:, t, :], banks[4][:, :], ACT.Copy).then_inc(v2_copied, 1)

        @block.vector
        def _(dve):
            for t in range(NT):
                dve.wait_ge(done, 5 * t + 4)
                dve.wait_ge(q_copied, t + 1)
                if t >= 1:
                    dve.wait_ge(own_sum, t)
                dve.tensor_tensor(own[:, :], banks[3][:, :], q_out[:, t % 2, 0:D], ALU.mult).then_inc(own_mul, 1)
                dve.wait_ge(own_mul, t + 1)
                dve.tensor_reduce(q_out[:, t % 2, D:QROW], own[:, :].rearrange("p (h d) -> p h d", h=H),
                                  AX.X, ALU.add).then_inc(own_sum, 1)


def mix_branch(nc, w_qkv, w_proj, b_proj, xnT, ident, ones, res):
    with ExitStack() as ctx:
        def sb(name, shape, dt=F32):
            return ctx.enter_context(nc.sbuf_tensor(name, shape, dt))

        def sem(name):
            return ctx.enter_context(nc.semaphore(name))

        PAIR = 2 * HW
        w = sb("w_mix", [P, C, 3 * D])
        wp = sb("wp", [P, C, D])
        bp = sb("bp", [1, D])
        qfT = sb("qfT", [P, C, NP])
        small = sb("small", [P, 2, D])
        big = sb("big", [P, 2, D])
        kf = sb("kf", [P, 2, D])
        v1 = sb("v1", [P, 2, H, HW])
        kvd = sb("kvd", [P, C, PAIR])
        z = sb("z", [P, 2, H])
        y = sb("y", [P, 2, D])
        yT = sb("yT", [P, 2, D])
        kb = [ctx.enter_context(nc.psum_tensor(f"kb{i}", [P, D], F32)) for i in range(2)]
        vb = [ctx.enter_context(nc.psum_tensor(f"vb{i}", [P, D], F32)) for i in range(2)]
        kvb = [ctx.enter_context(nc.psum_tensor(f"kvb{i}", [P, D], F32)) for i in range(4)]
        w_in, wp_in = sem("w_in"), sem("wp_in")
        k_done, v_done, q_done = sem("k_done"), sem("v_done"), sem("q_done")
        low, exped, high = sem("low"), sem("exped"), sem("high")
        v_copied, v_ones, kv_added, kvd_zero, kvd_done = (
            sem("v_copied"), sem("v_ones"), sem("kv_added"), sem("kvd_zero"), sem("kvd_done"))
        y_done, z_eps, z_inv, y_scaled, y_turned, yT_copied, p_done, res_done = (
            sem("y_done"), sem("z_eps"), sem("z_inv"), sem("y_scaled"), sem("y_turned"), sem("yT_copied"),
            sem("p_done"), sem("res_done"))
        block = ctx.enter_context(nc.Block())
        QJ = [(c, n0, nn) for c in range(C) for n0, nn in NCH]

        @block.sync
        def _(sp):
            sp.dma_start(w[:, :, :], w_qkv.rearrange("(c p) o -> p c o", p=P)).then_inc(w_in, 16)
            sp.dma_start(wp[:, :, :], w_proj.rearrange("(c p) o -> p c o", p=P)).then_inc(wp_in, 16)
            sp.dma_start(bp[:, :], b_proj.unsqueeze(0)).then_inc(wp_in, 16)

        @block.gpsimd
        def _(pool):
            pool.memset(v1[:, :, :, DH:HW], 1.0).then_inc(v_ones, 1)
            pool.memset(kvd[:, :, :], 0.0).then_inc(kvd_zero, 1)

        @block.vector
        def _(dve):
            for t in range(NT):
                dve.wait_ge(k_done, t + 1)
                if t >= 2:
                    dve.wait_ge(high, t - 1)
                dve.tensor_scalar(small[:, t % 2, :], kb[t % 2][:, :], 0.0, None, ALU.min).then_inc(low, 1)
                dve.wait_ge(exped, t + 1)
                if t >= 2:
                    dve.wait_ge(kv_added, t - 1)
                dve.scalar_tensor_tensor(kf[:, t % 2, :], kb[t % 2][:, :], 0.0, big[:, t % 2, :],
                                         ALU.max, ALU.add).then_inc(high, 1)
            for j, (c, n0, nn) in enumerate(QJ):
                t = NT + j
                dve.wait_ge(q_done, j + 1)
                dve.wait_ge(high, t - 1)
                dve.tensor_scalar(small[:, t % 2, 0:nn], kb[t % 2][:, 0:nn], 0.0, None, ALU.min).then_inc(low, 1)
                dve.wait_ge(exped, t + 1)
                dve.scalar_tensor_tensor(qfT[:, c, n0:n0 + nn], kb[t % 2][:, 0:nn], 0.0, big[:, t % 2, 0:nn],
                                         ALU.max, ALU.add).then_inc(high, 1)
            dve.wait_ge(kv_added, NT)
            dve.wait_ge(kvd_zero, 1)
            for c in range(C):
                dve.tensor_copy(kvd[0:DH, c, 0:HW], kvb[c][0:DH, 0:HW]).then_inc(kvd_done, 1)
                dve.tensor_copy(kvd[DH:P, c, HW:PAIR], kvb[c][DH:P, HW:PAIR]).then_inc(kvd_done, 1)
            for t in range(NT):
                dve.wait_ge(y_done, t + 1)
                if t >= 1:
                    dve.wait_ge(y_scaled, 2 * t)
                for b in range(2):
                    heads = kb[b][:, 0:2 * PAIR].rearrange("p (h e) -> p h e", e=HW)
                    dve.tensor_scalar(z[:, 0, 4 * b:4 * b + 4], heads[:, :, DH], MIX_EPS, None,
                                      ALU.add).then_inc(z_eps, 1)
                dve.wait_ge(z_eps, 2 * (t + 1))
                dve.reciprocal(z[:, 1, :], z[:, 0, :]).then_inc(z_inv, 1)
                dve.wait_ge(z_inv, t + 1)
                if t >= 2:
                    dve.wait_ge(y_turned, t - 1)
                for b in range(2):
                    heads = kb[b][:, 0:2 * PAIR].rearrange("p (h e) -> p h e", e=HW)
                    dve.tensor_tensor(y[:, t % 2, b * 256:(b + 1) * 256].rearrange("p (h d) -> p h d", d=DH),
                                      heads[:, :, 0:DH], bc(z[:, 1, 4 * b:4 * b + 4], DH), ALU.mult).then_inc(y_scaled, 1)
                dve.wait_ge(p_done, t + 1)
                dve.tensor_tensor(res[:, t, :], vb[1][:, :], res[:, t, :], ALU.add).then_inc(res_done, 1)

        @block.scalar
        def _(act):
            for t in range(NT):
                act.wait_ge(low, t + 1)
                if t >= 2:
                    act.wait_ge(high, t - 1)
                act.activation(big[:, t % 2, :], small[:, t % 2, :], ACT.Exp).then_inc(exped, 1)
                act.wait_ge(v_done, t + 1)
                act.wait_ge(v_ones, 1)
                if t >= 2:
                    act.wait_ge(kv_added, t - 1)
                act.activation(v1[:, t % 2, :, 0:DH], vb[t % 2][:, :].rearrange("p (h d) -> p h d", h=H),
                               ACT.Copy).then_inc(v_copied, 1)
            for j, (c, n0, nn) in enumerate(QJ):
                t = NT + j
                act.wait_ge(low, t + 1)
                act.wait_ge(high, t - 1)
                act.activation(big[:, t % 2, 0:nn], small[:, t % 2, 0:nn], ACT.Exp).then_inc(exped, 1)
            for t in range(NT):
                act.wait_ge(y_turned, t + 1)
                if t >= 2:
                    act.wait_ge(p_done, t - 1)
                act.activation(yT[:, t % 2, :], vb[0][:, :], ACT.Copy).then_inc(yT_copied, 1)

        @block.tensor
        def _(pe):
            pe.wait_ge(w_in, 16)

            def add_kv(t):
                pe.wait_ge(high, t + 1)
                pe.wait_ge(v_copied, t + 1)
                r = node_rows(t)
                for c in range(C):
                    last = pe.matmul(kvb[c][:, 0:PAIR], kf[0:r, t % 2, c * P:(c + 1) * P],
                                     v1[0:r, t % 2, 2 * c:2 * c + 2, :], start=t == 0, stop=t == NT - 1)
                last.then_inc(kv_added, 1)

            for t in range(NT):
                if t >= 2:
                    pe.wait_ge(high, t - 1)
                for c in range(C):
                    last = pe.matmul(kb[t % 2][:, :], xnT[:, c, t * P:(t + 1) * P], w[:, c, D:2 * D],
                                     start=c == 0, stop=c == C - 1)
                last.then_inc(k_done, 1)
                if t >= 2:
                    pe.wait_ge(v_copied, t - 1)
                for c in range(C):
                    last = pe.matmul(vb[t % 2][:, :], xnT[:, c, t * P:(t + 1) * P], w[:, c, 2 * D:3 * D],
                                     start=c == 0, stop=c == C - 1)
                last.then_inc(v_done, 1)
                if t >= 1:
                    add_kv(t - 1)
            add_kv(NT - 1)
            for j, (c, n0, nn) in enumerate(QJ):
                pe.wait_ge(high, NT + j - 1)
                for k in range(C):
                    last = pe.matmul(kb[(NT + j) % 2][:, 0:nn], w[:, k, c * P:(c + 1) * P], xnT[:, k, n0:n0 + nn],
                                     start=k == 0, stop=k == C - 1)
                last.then_inc(q_done, 1)
            pe.wait_ge(kvd_done, 2 * C)
            pe.wait_ge(high, NT + len(QJ))
            pe.wait_ge(v_copied, NT)
            pe.wait_ge(wp_in, 32)
            for t in range(NT):
                if t >= 1:
                    pe.wait_ge(y_scaled, 2 * t)
                for c in range(C):
                    last = pe.matmul(kb[c // 2][:, (c % 2) * PAIR:(c % 2 + 1) * PAIR], qfT[:, c, t * P:(t + 1) * P],
                                     kvd[:, c, :], start=True, stop=True)
                last.then_inc(y_done, 1)
                pe.wait_ge(y_scaled, 2 * (t + 1))
                if t >= 1:
                    pe.wait_ge(yT_copied, t)
                for c in range(C):
                    last = pe.transpose(vb[0][:, c * P:(c + 1) * P], y[:, t % 2, c * P:(c + 1) * P], ident[:, :])
                last.then_inc(y_turned, 1)
                pe.wait_ge(yT_copied, t + 1)
                if t >= 1:
                    pe.wait_ge(res_done, t)
                for c in range(C):
                    pe.matmul(vb[1][:, :], yT[:, t % 2, c * P:(c + 1) * P], wp[:, c, :], start=c == 0, stop=False)
                pe.matmul(vb[1][:, :], ones[:, :], bp[:, :], start=False, stop=True).then_inc(p_done, 1)


def edges(nc, src, dst, ef, q_table, kv_table, merge, ident, Me_hi, Me_lo):
    with ExitStack() as ctx:
        def sb(name, shape, dt=F32):
            return ctx.enter_context(nc.sbuf_tensor(name, shape, dt))

        def two(name, shape, dt=F32):
            return [sb(f"{name}{u}", shape, dt) for u in range(2)]

        def sem(name):
            return ctx.enter_context(nc.semaphore(name))

        ident16 = sb("ident16", [P, 4, P], BF16)
        pick = sb("pick", [3 * H, H, P], BF16)
        before = sb("before", [P, P])
        efs = two("efs", [P, D])
        efT = two("efT", [P, C, P])
        efT_hi = two("efT_hi", [P, C, P], F32R)
        efT_lo = two("efT_lo", [P, C, P], F32R)
        src_id = two("src_id", [P, 1], I32)
        dst_id = two("dst_id", [P, 1], I32)
        dst_row = two("dst_row", [P, P], I32)
        dst_col = two("dst_col", [P, 1], I32)
        same = two("same", [P, P])
        apart = two("apart", [P, P], BF16)
        junk = sb("junk", [P, P])
        count = two("count", [P, 1])
        put_id = two("put_id", [P, 1], I32)
        kv = two("kv", [P, 2 * D])
        qc = two("qc", [P, QROW])
        old = two("old", [P, TROW])
        new = two("new", [P, TROW])
        score0 = sb("score_sum", [P, H])
        score = two("score", [P, H])
        rest = sb("rest", [P, 2, H])
        parts = sb("parts", [P, 3 * H], BF16)
        partsT = sb("partsT", [3 * H, P], BF16)
        top = two("top", [P, H])
        diff = two("diff", [P, 2 * H])
        expd = two("expd", [P, 2 * H])
        wv = two("wv", [P, H, HW])
        psT = ctx.enter_context(nc.psum_tensor("psT", [P, D], F32))
        psK = ctx.enter_context(nc.psum_tensor("psK", [P, D], F32))
        psV = [ctx.enter_context(nc.psum_tensor(f"psV{u}", [P, D], F32)) for u in range(2)]
        psB = ctx.enter_context(nc.psum_tensor("psB", [P, 2, D], F32))
        psS = ctx.enter_context(nc.psum_tensor("psS", [P, 2, D], F32))
        psA = psB[:, 0, :].bitcast(BF16)

        consts = sem("consts")
        ids_in, pair_in, ef_in, kv_in, q_in, old_in, put = ([sem(f"{n}{u}") for u in range(2)] for n in
                                                   ("ids_in", "pair_in", "ef_in", "kv_in", "q_in", "old_in", "put"))
        turned, efT_ready, k_done, v_done = sem("ef_turned"), sem("efT_ready"), sem("k_edges"), sem("v_edges")
        same_ready, apart_ready, counted, putid_ready = (
            sem("same_ready"), sem("apart_ready"), sem("counted"), sem("putid_ready"))
        k_added, k_times_q, k_summed, score_ready = (
            sem("k_added"), sem("k_times_q"), sem("k_summed"), sem("score_ready"))
        part_step, parts_ready, parts_turned, partsT_ready, spread = (
            sem("part_step"), sem("parts_ready"), sem("parts_turned"), sem("partsT_ready"), sem("spread"))
        v_added, top_ready, newmax_ready, diff_ready, exp_ready = (
            sem("v_added"), sem("top_ready"), sem("newmax_ready"), sem("diff_ready"), sem("exp_ready"))
        efT_hi_ready, efT_lo_ready, wv_ready = (
            sem("efT_hi_ready"), sem("efT_lo_ready"), sem("wv_ready"))
        summed, old_scaled, new_ready = sem("summed"), sem("old_scaled"), sem("new_ready")
        block = ctx.enter_context(nc.Block())
        J = ET // 2
        assert ET % 2 == 1 and ELAST == 32

        def over_tiles(eng, engine, body):
            body(0, 0, P)
            body(0, 1, P)
            with nc.Fori(1, J, engines=[engine]) as i:
                j = eng.snap(i)
                body(j, 0, P)
                body(j, 1, P)
            body(J, 0, ELAST)

        def later(j):
            return not (isinstance(j, int) and j == 0)

        def fixed(eng):
            eng.wait_ge(consts, 8)

        def value(eng, v):
            if not isinstance(v, int):
                v = eng.snap(v)
                eng.compute_val(v)
            return v

        @block.sync
        def _(sp):
            def load(j, u, r):
                t = 2 * j + u
                row, before_last, dmas = value(sp, t * P), value(sp, t - 1), value(sp, 16 * j)
                if later(j):
                    fixed(sp)
                    sp.wait_ge(turned, before_last)
                sp.dma_start(efs[u][0:r, :], ef[bass.ds(row, r), :]).then_inc(ef_in[u], 16)
                if later(j):
                    fixed(sp)
                    sp.wait_ge(same_ready, before_last)
                sp.dma_start(dst_row[u][0:r, 0:r],
                             dst[bass.ds(row, r)].unsqueeze(0).to_broadcast([r, r])).then_inc(pair_in[u], 16)
                sp.dma_start(dst_col[u][0:r, :], dst[bass.ds(row, r)].unsqueeze(1)).then_inc(pair_in[u], 16)
                if later(j):
                    fixed(sp)
                    sp.wait_ge(putid_ready, before_last)
                    sp.wait_ge(kv_in[u], dmas)
                    sp.wait_ge(q_in[u], dmas)
                    sp.wait_ge(old_in[u], dmas)
                sp.dma_start(src_id[u][0:r, :], src[bass.ds(row, r)].unsqueeze(1)).then_inc(ids_in[u], 16)
                sp.dma_start(dst_id[u][0:r, :], dst[bass.ds(row, r)].unsqueeze(1)).then_inc(ids_in[u], 16)
            over_tiles(sp, mybir.EngineType.SP, load)

        @block.gpsimd
        def _(pool):
            pool.memset(ident16[:, :, :], 0.0).then_inc(consts, 1)
            pool.memset(pick[:, :, :], 0.0).then_inc(consts, 1)
            pool.memset(before[:, :], 1.0).then_inc(consts, 1)
            pool.wait_ge(consts, 3)
            pool.affine_select(out=ident16[:, :, :], in_=ident16[:, :, :], compare_op=ALU.not_equal, fill=1.0, base=0,
                               pattern=[[0, 4], [-1, P]], channel_multiplier=1).then_inc(consts, 1)
            pool.affine_select(out=before[:, :], in_=before[:, :], compare_op=ALU.is_gt, fill=0.0, base=0,
                               pattern=[[-1, P]], channel_multiplier=1).then_inc(consts, 1)
            for part in range(3):
                pool.wait_ge(consts, 5 + part)
                pool.affine_select(out=pick[:, :, :], in_=pick[:, :, :], compare_op=ALU.not_equal, fill=1.0,
                                   base=-H * part, pattern=[[-1, H], [0, P]], channel_multiplier=1).then_inc(consts, 1)

            def fetch(out, table, ids, r, done):
                pool.indirect_dma_start(out=out[0:r, :], out_offset=None, in_=table[:, :],
                                        in_offset=bass.IndirectOffsetOnAxis(ap=ids[0:r, 0:1], axis=0)).then_inc(done, 16)

            def low_part(t, j, u, r):
                pool.wait_ge(efT_ready, value(pool, t + 1))
                pool.wait_ge(efT_hi_ready, value(pool, t + 1))
                if later(j):
                    pool.wait_ge(v_done, value(pool, t - 1))
                pool.tensor_tensor(efT_lo[u][:, :, 0:r], efT[u][:, :, 0:r], efT_hi[u][:, :, 0:r].bitcast(F32),
                                   ALU.subtract).then_inc(efT_lo_ready, 1)

            def fetch_edges(t, j, u, r):
                ids = value(pool, 32 * (j + 1))
                before_last = value(pool, t - 1)
                fixed(pool)
                pool.wait_ge(ids_in[u], ids)
                if later(j):
                    pool.wait_ge(v_added, before_last)
                    pool.wait_ge(score_ready, before_last)
                fetch(kv[u], kv_table, src_id[u], r, kv_in[u])
                fetch(qc[u], q_table, dst_id[u], r, q_in[u])

            def fetch_old(j, u, r):
                if later(j):
                    dmas = value(pool, 16 * j)
                    fixed(pool)
                    pool.wait_ge(put[u], dmas)
                fetch(old[u], merge[u], dst_id[u], r, old_in[u])

            def store(t, u, r):
                done = value(pool, t + 1)
                fixed(pool)
                pool.wait_ge(new_ready, done)
                pool.wait_ge(putid_ready, done)
                pool.indirect_dma_start(out=merge[u][:, :], out_offset=bass.IndirectOffsetOnAxis(ap=put_id[u][0:r, 0:1], axis=0),
                                        in_=new[u][0:r, :], in_offset=None, bounds_check=N - 1,
                                        oob_is_err=False).then_inc(put[u], 16)

            def scale_old(t, u, r):
                pool.wait_ge(exp_ready, value(pool, t + 1))
                pool.tensor_tensor(old[u][0:r, 0:ROW].rearrange("p (h e) -> p h e", e=HW),
                                   old[u][0:r, 0:ROW].rearrange("p (h e) -> p h e", e=HW),
                                   bc(expd[u][0:r, H:2 * H], HW), ALU.mult).then_inc(old_scaled, 1)

            def move(j, u, r, ahead, ahead2):
                t = 2 * j + u
                if ahead is not None:
                    ja, ua, ra = ahead
                    fetch_edges(t + 1, ja, ua, ra)
                if not (isinstance(t, int) and t == 0):
                    store(t - 1, 1 - u, P)
                if ahead2 is not None:
                    low_part(t + 2, j + 1, u, ahead2)
                scale_old(t, u, r)
                if ahead is not None:
                    fetch_old(ja, ua, ra)

            fetch_edges(0, 0, 0, P)
            fetch_old(0, 0, P)
            low_part(0, 0, 0, P)
            low_part(1, 0, 1, P)
            move(0, 0, P, (0, 1, P), P)
            move(0, 1, P, (1, 0, P), P)
            with nc.Fori(1, J - 1, engines=[mybir.EngineType.Pool]) as i:
                j = pool.snap(i)
                move(j, 0, P, (j, 1, P), P)
                move(j, 1, P, (j + 1, 0, P), P)
            move(J - 1, 0, P, (J - 1, 1, P), ELAST)
            move(J - 1, 1, P, (J, 0, ELAST), None)
            move(J, 0, ELAST, None, None)
            store(2 * J, 0, ELAST)
            pool.wait_ge(put[0], 16 * (J + 1))
            pool.wait_ge(put[1], 16 * J)

        @block.scalar
        def _(act):
            def turn(j, u, r):
                t = 2 * j + u
                act.wait_ge(turned, t + 1)
                if later(j):
                    act.wait_ge(v_done, t - 1)
                turned_ef = psT[:, :].rearrange("p (c e) -> p c e", c=C)[:, :, 0:r]
                act.activation(efT_hi[u][:, :, 0:r], turned_ef, ACT.Copy).then_inc(efT_hi_ready, 1)
                if later(j):
                    act.wait_ge(efT_lo_ready, t - 1)
                act.activation(efT[u][:, :, 0:r], turned_ef, ACT.Copy).then_inc(efT_ready, 1)

            def spread_parts(j, u, r):
                t = 2 * j + u
                act.wait_ge(parts_turned, t + 1)
                if not (isinstance(t, int) and t == 0):
                    act.wait_ge(spread, t)
                act.activation(partsT[:, 0:r], psA[0:3 * H, 0:r], ACT.Copy).then_inc(partsT_ready, 1)

            def weights(j, u, r):
                t = 2 * j + u
                act.wait_ge(diff_ready, 2 * (t + 1))
                if later(j):
                    act.wait_ge(old_scaled, t - 1)
                act.activation(expd[u][0:r, :], diff[u][0:r, :], ACT.Exp, scale=SCALE).then_inc(exp_ready, 1)
                act.wait_ge(exp_ready, t + 1)
                act.wait_ge(v_added, t + 1)
                if later(j):
                    act.wait_ge(summed, t - 1)
                act.activation(wv[u][0:r, :, DH:HW], expd[u][0:r, 0:H].unsqueeze(2), ACT.Copy).then_inc(wv_ready, 1)
                for h in range(H):
                    act.activation(wv[u][0:r, h, 0:DH], psV[u][0:r, h * DH:(h + 1) * DH], ACT.Copy,
                                   scale=expd[u][0:r, h:h + 1]).then_inc(wv_ready, 1)

            def tile(j, u, r, ahead2):
                spread_parts(j, u, r)
                if ahead2 is not None:
                    turn(j + 1, u, ahead2)
                weights(j, u, r)

            turn(0, 0, P)
            turn(0, 1, P)
            tile(0, 0, P, P)
            tile(0, 1, P, P)
            with nc.Fori(1, J - 1, engines=[mybir.EngineType.Activation]) as i:
                j = act.snap(i)
                tile(j, 0, P, P)
                tile(j, 1, P, P)
            tile(J - 1, 0, P, ELAST)
            tile(J - 1, 1, P, None)
            tile(J, 0, ELAST, None)

        @block.vector
        def _(dve):
            def merge_step(j, u, r):
                t = 2 * j + u
                dve.wait_ge(summed, t + 1)
                dve.wait_ge(old_scaled, t + 1)
                dve.tensor_tensor(new[u][0:r, 0:ROW].rearrange("p (b e) -> p b e", b=2), psS[0:r, :, 0:4 * HW],
                                  old[u][0:r, 0:ROW].rearrange("p (b e) -> p b e", b=2), ALU.add).then_inc(new_ready, 1)

            def find_same(t, j, u, r):
                dve.wait_ge(pair_in[u], 32 * (j + 1))
                if later(j):
                    dve.wait_ge(summed, t - 1)
                dve.tensor_scalar(same[u][0:r, 0:r], dst_row[u][0:r, 0:r], dst_col[u][0:r, 0:1], None,
                                  ALU.is_equal).then_inc(same_ready, 1)

            def find_apart(t, j, u, r):
                dve.wait_ge(same_ready, t + 1)
                dve.tensor_scalar(apart[u][0:r, 0:r], same[u][0:r, 0:r], -1.0, -NEG, ALU.add,
                                  ALU.mult).then_inc(apart_ready, 1)

            def count_before(t, j, u, r):
                if later(j):
                    dve.wait_ge(putid_ready, t - 1)
                dve.tensor_tensor_reduce(out=junk[0:r, 0:r], in0=same[u][0:r, 0:r], in1=before[0:r, 0:r], scale=OOB,
                                         scalar=0.0, op0=ALU.mult, op1=ALU.add,
                                         accum_out=count[u][0:r, 0:1]).then_inc(counted, 1)

            def tile(j, u, r, ahead):
                t = 2 * j + u
                first = isinstance(t, int) and t == 0
                dve.wait_ge(k_done, t + 1)
                dve.wait_ge(kv_in[u], 16 * (j + 1))
                dve.tensor_tensor(psK[0:r, :], psK[0:r, :], kv[u][0:r, 0:D], ALU.add).then_inc(k_added, 1)
                dve.wait_ge(k_added, t + 1)
                dve.wait_ge(q_in[u], 16 * (j + 1))
                dve.tensor_tensor(psK[0:r, :], psK[0:r, :], qc[u][0:r, 0:D], ALU.mult).then_inc(k_times_q, 1)
                dve.wait_ge(k_times_q, t + 1)
                dve.tensor_reduce(score0[0:r, :], psK[0:r, :].rearrange("p (h d) -> p h d", h=H), AX.X,
                                  ALU.add).then_inc(k_summed, 1)
                dve.wait_ge(k_summed, t + 1)
                if later(j):
                    dve.wait_ge(diff_ready, 2 * (t - 1))
                dve.tensor_tensor(score[u][0:r, :], score0[0:r, :], qc[u][0:r, D:QROW], ALU.add).then_inc(score_ready, 1)
                dve.wait_ge(score_ready, t + 1)
                if not first:
                    dve.wait_ge(parts_turned, t)
                dve.tensor_copy(parts[0:r, 0:H], score[u][0:r, :]).then_inc(part_step, 1)
                dve.wait_ge(part_step, 4 * t + 1)
                dve.tensor_tensor(rest[0:r, 0, :], score[u][0:r, :], parts[0:r, 0:H], ALU.subtract).then_inc(part_step, 1)
                dve.wait_ge(part_step, 4 * t + 2)
                dve.tensor_copy(parts[0:r, H:2 * H], rest[0:r, 0, :]).then_inc(part_step, 1)
                dve.wait_ge(part_step, 4 * t + 3)
                dve.tensor_tensor(rest[0:r, 1, :], rest[0:r, 0, :], parts[0:r, H:2 * H], ALU.subtract).then_inc(part_step, 1)
                dve.wait_ge(part_step, 4 * t + 4)
                dve.tensor_copy(parts[0:r, 2 * H:3 * H], rest[0:r, 1, :]).then_inc(parts_ready, 1)
                dve.wait_ge(v_done, t + 1)
                dve.tensor_tensor(psV[u][0:r, :], psV[u][0:r, :], kv[u][0:r, D:2 * D], ALU.add).then_inc(v_added, 1)
                if ahead is not None:
                    find_same(t + 1, *ahead)
                if not first:
                    merge_step(j if u == 1 else j - 1, 1 - u, P)
                if ahead is not None:
                    find_apart(t + 1, *ahead)
                    count_before(t + 1, *ahead)
                dve.wait_ge(counted, t + 1)
                dve.wait_ge(ids_in[u], 32 * (j + 1))
                if later(j):
                    dve.wait_ge(put[u], 16 * j)
                dve.tensor_tensor(put_id[u][0:r, :], count[u][0:r, :], dst_id[u][0:r, :], ALU.add).then_inc(putid_ready, 1)
                dve.wait_ge(spread, t + 1)
                dve.tensor_reduce(top[u][0:r, :], psB[0:r, :, 0:4 * r].rearrange("p b (h e) -> p b h e", h=4), AX.X,
                                  ALU.max).then_inc(top_ready, 1)
                dve.wait_ge(top_ready, t + 1)
                dve.wait_ge(old_in[u], 16 * (j + 1))
                dve.tensor_tensor(new[u][0:r, ROW:TROW], old[u][0:r, ROW:TROW], top[u][0:r, :], ALU.max).then_inc(newmax_ready, 1)
                dve.wait_ge(newmax_ready, t + 1)
                dve.tensor_tensor(diff[u][0:r, 0:H], score[u][0:r, :], new[u][0:r, ROW:TROW], ALU.subtract).then_inc(diff_ready, 1)
                dve.tensor_tensor(diff[u][0:r, H:2 * H], old[u][0:r, ROW:TROW], new[u][0:r, ROW:TROW],
                                  ALU.subtract).then_inc(diff_ready, 1)

            dve.wait_ge(consts, 5)
            find_same(0, 0, 0, P)
            find_apart(0, 0, 0, P)
            count_before(0, 0, 0, P)
            tile(0, 0, P, (0, 1, P))
            tile(0, 1, P, (1, 0, P))
            with nc.Fori(1, J - 1, engines=[mybir.EngineType.DVE]) as i:
                j = dve.snap(i)
                tile(j, 0, P, (j, 1, P))
                tile(j, 1, P, (j + 1, 0, P))
            tile(J - 1, 0, P, (J - 1, 1, P))
            tile(J - 1, 1, P, (J, 0, ELAST))
            tile(J, 0, ELAST, None)
            merge_step(J, 0, ELAST)

        @block.tensor
        def _(pe):
            def turn(j, u, r):
                t = 2 * j + u
                pe.wait_ge(ef_in[u], 16 * (j + 1))
                if not (isinstance(t, int) and t == 0):
                    pe.wait_ge(efT_ready, t)
                for c in range(C):
                    last = pe.transpose(psT[:, c * P:c * P + r], efs[u][0:r, c * P:(c + 1) * P], ident[0:r, 0:r])
                last.then_inc(turned, 1)

            def sum_step(j, u, r):
                t = 2 * j + u
                pe.wait_ge(wv_ready, 9 * (t + 1))
                pe.wait_ge(same_ready, t + 1)
                if not (isinstance(t, int) and t == 0):
                    pe.wait_ge(new_ready, t)
                for b in range(2):
                    last = pe.matmul(psS[0:r, b, 0:4 * HW], same[u][0:r, 0:r], wv[u][0:r, 4 * b:4 * b + 4, :],
                                     start=True, stop=True)
                last.then_inc(summed, 1)

            def product(out, u, col):
                for c in range(C):
                    pe.matmul(out[:, :], efT_hi[u][:, c, :], Me_hi[:, c, col:col + D], start=c == 0, stop=False)
                    pe.matmul(out[:, :], efT_hi[u][:, c, :], Me_lo[:, c, col:col + D], start=False, stop=False)
                    last = pe.matmul(out[:, :], efT_lo[u][:, c, :], Me_hi[:, c, col:col + D],
                                     start=False, stop=c == C - 1)
                return last

            def tile(j, u, r, ahead2):
                t = 2 * j + u
                first = isinstance(t, int) and t == 0
                pe.wait_ge(efT_hi_ready, t + 1)
                pe.wait_ge(efT_lo_ready, t + 1)
                if not first:
                    pe.wait_ge(k_summed, t)
                product(psK, u, 0).then_inc(k_done, 1)
                if later(j):
                    pe.wait_ge(wv_ready, 9 * (t - 1))
                product(psV[u], u, D).then_inc(v_done, 1)
                if not first:
                    sum_step(j if u == 1 else j - 1, 1 - u, P)
                pe.wait_ge(parts_ready, t + 1)
                if not first:
                    pe.wait_ge(top_ready, t)
                pe.transpose(psA[0:3 * H, 0:r], parts[0:r, :], ident16[0:r, 0, 0:r]).then_inc(parts_turned, 1)
                if ahead2 is not None:
                    turn(j + 1, u, ahead2)
                pe.wait_ge(partsT_ready, t + 1)
                pe.wait_ge(apart_ready, t + 1)
                for b in range(2):
                    pe.matmul(psB[0:r, b, 0:4 * r].rearrange("p (h e) -> p h e", h=4), apart[u][0:r, 0:r],
                              ident16[0:r, :, 0:r], start=True, stop=True)
                    for h in range(4):
                        last = pe.matmul(psB[0:r, b, h * r:(h + 1) * r], pick[:, 4 * b + h, 0:r], partsT[:, 0:r],
                                         start=False, stop=True, skip_group_check=True)
                last.then_inc(spread, 1)

            pe.wait_ge(consts, 8)
            turn(0, 0, P)
            turn(0, 1, P)
            tile(0, 0, P, P)
            tile(0, 1, P, P)
            with nc.Fori(1, J - 1, engines=[mybir.EngineType.PE]) as i:
                j = pe.snap(i)
                tile(j, 0, P, P)
                tile(j, 1, P, P)
            tile(J - 1, 0, P, ELAST)
            tile(J - 1, 1, P, None)
            tile(J, 0, ELAST, None)
            sum_step(J, 0, ELAST)


def gnn_end(nc, merge, bo, gamma, beta, ident, xnT, v2, WoT, res):
    with ExitStack() as ctx:
        def sb(name, shape, dt=F32):
            return ctx.enter_context(nc.sbuf_tensor(name, shape, dt))

        def sem(name):
            return ctx.enter_context(nc.semaphore(name))

        rows = sb("rows", [P, 2, 2, TROW])
        nmax = sb("nmax", [P, H])
        dif = sb("dif", [P, 2, H])
        scl = sb("scl", [P, 2, H])
        part = sb("part", [P, 2, ROW])
        tot = sb("tot", [P, ROW])
        safe = sb("safe", [P, 3, H])
        own = sb("own2", [P, D])
        g = sb("g", [P, 2, D])
        gT = sb("gT", [P, C, NP])
        oT = sb("oT", [P, C, NP])
        col = sb("col", [P, 3, C])
        stats = sb("bstats", [P, C, 3, 6])
        mv = sb("bmv", [P, C, 2])
        sd = sb("sd", [P, 4, C])
        banks = [ctx.enter_context(nc.psum_tensor(f"gbank{i}", [P, D], F32)) for i in range(4)]
        rows_in = [sem(f"rows_in{i}") for i in range(2)]
        col_in, step, dif_done, scl_done, g_done, g_turned, gT_done, o_done, oT_done, bn, sd_in, sd_out, norm, back, added = (
            sem(n) for n in ("col_in", "merge_link", "dif_done", "scl_done", "g_done", "g_turned", "gT_done", "o_done",
                             "oT_done", "bn_link", "sd_in", "sd_out", "norm", "back", "added"))
        block = ctx.enter_context(nc.Block())
        OJ = [(c, n0, nn) for c in range(C) for n0, nn in NCH]
        REAL = [(0, 512), (512, 512), (1024, N - 1024)]

        @block.sync
        def _(sp):
            for i, v in enumerate((bo, gamma, beta)):
                sp.dma_start(col[:, i, :], v.rearrange("(c p) -> p c", p=P),
                              allow_slow_non_contiguous=True).then_inc(col_in, 16)
            for t in range(NT):
                if t >= 2:
                    sp.wait_ge(g_done, t - 1)
                for i in range(2):
                    sp.dma_start(rows[:, t % 2, i, :], merge[i][t * P:(t + 1) * P, :]).then_inc(rows_in[t % 2], 16)

        @block.vector
        def _(dve):
            links = [0]

            def link(ins):
                links[0] += 1
                ins.then_inc(step, 1)
                dve.wait_ge(step, links[0])

            for t in range(NT):
                a = rows[:, t % 2, :, :]
                dve.wait_ge(rows_in[t % 2], 32 * (t // 2 + 1))
                link(dve.tensor_tensor(nmax[:, :], a[:, 0, ROW:TROW], a[:, 1, ROW:TROW], ALU.max))
                for i in range(2):
                    last = dve.tensor_tensor(dif[:, i, :], a[:, i, ROW:TROW], nmax[:, :], ALU.subtract)
                    last.then_inc(dif_done, 1)
                dve.wait_ge(scl_done, t + 1)
                for i in range(2):
                    link(dve.tensor_tensor(part[:, i, :].rearrange("p (h e) -> p h e", e=HW),
                                           a[:, i, 0:ROW].rearrange("p (h e) -> p h e", e=HW),
                                           bc(scl[:, i, :], HW), ALU.mult))
                link(dve.tensor_tensor(tot[:, :], part[:, 0, :], part[:, 1, :], ALU.add))
                th = tot[:, :].rearrange("p (h e) -> p h e", e=HW)
                link(dve.tensor_scalar(safe[:, 0, :], th[:, :, DH], 0.0, None, ALU.is_equal))
                link(dve.tensor_tensor(safe[:, 1, :], safe[:, 0, :], th[:, :, DH], ALU.add))
                link(dve.reciprocal(safe[:, 2, :], safe[:, 1, :]))
                link(dve.tensor_scalar(safe[:, 1, :], th[:, :, DH], 0.0, None, ALU.is_gt))
                link(dve.tensor_tensor(own[:, :].rearrange("p (h d) -> p h d", h=H),
                                       v2[:, t, :].rearrange("p (h d) -> p h d", h=H), bc(safe[:, 1, :], DH), ALU.mult))
                if t >= 2:
                    dve.wait_ge(g_turned, t - 1)
                link(dve.tensor_tensor(g[:, t % 2, :].rearrange("p (h d) -> p h d", h=H), th[:, :, 0:DH],
                                       bc(safe[:, 2, :], DH), ALU.mult))
                dve.tensor_tensor(g[:, t % 2, :], g[:, t % 2, :], own[:, :], ALU.add).then_inc(g_done, 1)
                dve.wait_ge(g_done, t + 1)
            dve.wait_ge(col_in, 48)
            for j, (c, n0, nn) in enumerate(OJ):
                dve.wait_ge(o_done, j + 1)
                dve.scalar_tensor_tensor(oT[:, c, n0:n0 + nn], banks[j % 4][:, 0:nn], col[:, 0, c:c + 1],
                                         xnT[:, c, n0:n0 + nn], ALU.add, ALU.add).then_inc(oT_done, 1)
                dve.wait_ge(oT_done, j + 1)
            for c in range(C):
                for k, (n0, nn) in enumerate(REAL):
                    link(dve.bn_stats(stats[:, c, k, :], oT[:, c, n0:n0 + nn]))
                link(dve.bn_aggr(mv[:, c, :], stats[:, c, :, :].rearrange("p k s -> p (k s)")))
            dve.tensor_scalar(sd[:, 0, :], mv[:, :, 1], LN_EPS, None, ALU.add).then_inc(sd_in, 1)
            dve.wait_ge(sd_out, 1)
            link(dve.reciprocal(sd[:, 2, :], sd[:, 1, :]))
            link(dve.tensor_tensor(sd[:, 3, :], sd[:, 2, :], col[:, 1, :], ALU.mult))
            link(dve.tensor_tensor(sd[:, 0, :], mv[:, :, 0], sd[:, 3, :], ALU.mult))
            link(dve.tensor_tensor(sd[:, 2, :], col[:, 2, :], sd[:, 0, :], ALU.subtract))
            for c in range(C):
                dve.tensor_scalar(oT[:, c, :], oT[:, c, :], sd[:, 3, c:c + 1], sd[:, 2, c:c + 1], ALU.mult,
                                  ALU.add).then_inc(norm, 1)
            for t in range(NT):
                dve.wait_ge(back, t + 1)
                dve.tensor_tensor(res[:, t, :], banks[t % 4][:, :], res[:, t, :], ALU.add).then_inc(added, 1)

        @block.scalar
        def _(act):
            for t in range(NT):
                act.wait_ge(dif_done, 2 * (t + 1))
                act.activation(scl[:, :, :], dif[:, :, :], ACT.Exp, scale=SCALE).then_inc(scl_done, 1)
                act.wait_ge(g_turned, t + 1)
                act.activation(gT[:, :, t * P:(t + 1) * P], banks[t % 4][:, :].rearrange("p (c e) -> p c e", c=C),
                               ACT.Copy).then_inc(gT_done, 1)
            act.wait_ge(sd_in, 1)
            act.activation(sd[:, 1, :], sd[:, 0, :], ACT.Sqrt).then_inc(sd_out, 1)

        @block.tensor
        def _(pe):
            for t in range(NT):
                pe.wait_ge(g_done, t + 1)
                if t >= 4:
                    pe.wait_ge(gT_done, t - 3)
                for c in range(C):
                    last = pe.transpose(banks[t % 4][:, c * P:(c + 1) * P], g[:, t % 2, c * P:(c + 1) * P], ident[:, :])
                last.then_inc(g_turned, 1)
            pe.wait_ge(gT_done, NT)
            for j, (c, n0, nn) in enumerate(OJ):
                if j >= 4:
                    pe.wait_ge(oT_done, j - 3)
                for k in range(C):
                    last = pe.matmul(banks[j % 4][:, 0:nn], WoT[:, k, c * P:(c + 1) * P], gT[:, k, n0:n0 + nn],
                                     start=k == 0, stop=k == C - 1)
                last.then_inc(o_done, 1)
            pe.wait_ge(norm, C)
            for t in range(NT):
                if t >= 4:
                    pe.wait_ge(added, t - 3)
                for c in range(C):
                    last = pe.transpose(banks[t % 4][:, c * P:(c + 1) * P], oT[:, c, t * P:(t + 1) * P], ident[:, :])
                last.then_inc(back, 1)


def ffn(nc, w_up, w_down, ident, res, out):
    with ExitStack() as ctx:
        def sb(name, shape, dt=F32):
            return ctx.enter_context(nc.sbuf_tensor(name, shape, dt))

        def sem(name):
            return ctx.enter_context(nc.semaphore(name))

        UC, DC = FF // P, C
        wu = sb("wu", [P, UC, D])
        wd = sb("wd", [P, DC, FF])
        tern = sb("tern", [P, 2, 2 * D])
        tern16 = sb("tern16", [P, 2, 2 * D], BF16)
        wuT = sb("wuT", [P, C, FF], BF16)
        wdT = sb("wdT", [P, UC, D], BF16)
        ident_b = sb("ident_b", [P, P], BF16)
        sums = sb("sums", [P, 2])
        onem = sb("onem", [P, P])
        wsc = sb("wsc", [P, 3, 2])
        stats = sb("fstats", [P, NT, 6])
        mv = sb("fmv", [P, NT, 2])
        sd = sb("fsd", [P, 3, NT])
        xn = sb("fxn", [P, D])
        xs = sb("xs", [P, 2, 4])
        xq = sb("xq", [P, D])
        xq16 = sb("xq16", [P, 2, D], BF16)
        xqT = sb("xqT", [P, 2, D], BF16)
        hid = sb("hid", [P, FF])
        hs = sb("hs", [P, 2, 4])
        hq16 = sb("hq16", [P, 2, FF], BF16)
        hqT = sb("hqT", [P, 2, FF], BF16)
        y = sb("fy", [P, 2, D])
        pw = ctx.enter_context(nc.psum_tensor("pw", [P, D], F32))
        pt = ctx.enter_context(nc.psum_tensor("pt", [P, 2 * D], BF16))
        ph = [ctx.enter_context(nc.psum_tensor(f"ph{i}", [P, D], F32)) for i in range(2)]
        pht = ctx.enter_context(nc.psum_tensor("pht", [P, 2 * D], BF16))
        py = [ctx.enter_context(nc.psum_tensor(f"py{i}", [P, D], F32)) for i in range(2)]
        w_in, cst, idb, step, total, sd_in, sd_out = (sem(n) for n in (
            "fw_in", "fcst", "fidb", "ffn_link", "w_total", "fsd_in", "fsd_out"))
        w_ready, w_turned, w_copied = sem("w_ready"), sem("fw_turned"), sem("fw_copied")
        x_ready, x_turned, xT_ready, h_done, h_ready, h_turned, hT_ready, y_done, y_ready = (sem(n) for n in (
            "fx_ready", "fx_turned", "fxT_ready", "fh_done", "fh_ready", "fh_turned", "fhT_ready", "fy_done", "fy_ready"))
        stored = [sem(f"stored{i}") for i in range(2)]
        block = ctx.enter_context(nc.Block())

        @block.sync
        def _(sp):
            sp.dma_start(wu[:, :, :], w_up.rearrange("(c p) i -> p c i", p=P)).then_inc(w_in, 16)
            sp.dma_start(wd[:, :, :], w_down.rearrange("(c p) i -> p c i", p=P)).then_inc(w_in, 16)
            for t in range(NT):
                sp.wait_ge(y_ready, t + 1)
                r = node_rows(t)
                sp.dma_start(out[t * P:t * P + r, :], y[0:r, t % 2, :]).then_inc(stored[t % 2], 16)
            sp.wait_ge(stored[0], 16 * (NT // 2))
            sp.wait_ge(stored[1], 16 * (NT // 2))

        @block.gpsimd
        def _(pool):
            pool.memset(onem[:, :], 1.0).then_inc(cst, 1)

        @block.vector
        def _(dve):
            links = [0]

            def link(ins):
                links[0] += 1
                ins.then_inc(step, 1)
                dve.wait_ge(step, links[0])

            dve.tensor_copy(ident_b[:, :], ident[:, :]).then_inc(idb, 1)
            dve.wait_ge(w_in, 32)
            flat = [wu[:, :, :].rearrange("p a b -> p (a b)"), wd[:, :, :].rearrange("p a b -> p (a b)")]
            for i in range(2):
                link(dve.tensor_reduce(sums[:, i:i + 1], flat[i], AX.X, ALU.add, apply_absolute_value=True))
            dve.wait_ge(total, 1)
            link(dve.tensor_scalar(wsc[:, 0, :], pw[:, 0:2], 1.0 / (FF * D), LN_EPS, ALU.mult, ALU.max))
            link(dve.reciprocal(wsc[:, 1, :], wsc[:, 0, :]))
            for i in range(2):
                link(dve.tensor_scalar(tern[:, i, :], flat[i], wsc[:, 1, i:i + 1], RINT, ALU.mult, ALU.add))
                link(dve.tensor_scalar(tern[:, i, :], tern[:, i, :], -RINT, -1.0, ALU.add, ALU.max))
                dve.tensor_scalar(tern16[:, i, :], tern[:, i, :], 1.0, None, ALU.min).then_inc(w_ready, 1)
            for t in range(NT):
                link(dve.bn_stats(stats[:, t, :], res[:, t, :]))
                link(dve.bn_aggr(mv[:, t, :], stats[:, t, :]))
            dve.tensor_scalar(sd[:, 0, :], mv[:, :, 1], LN_EPS, None, ALU.add).then_inc(sd_in, 1)
            dve.wait_ge(sd_out, 1)
            link(dve.reciprocal(sd[:, 2, :], sd[:, 1, :]))

            def quantise(t):
                s = xs[:, t % 2, :]
                link(dve.tensor_scalar(xn[:, :], res[:, t, :], mv[:, t, 0:1], sd[:, 2, t:t + 1], ALU.subtract, ALU.mult))
                link(dve.tensor_reduce(s[:, 0:1], xn[:, :], AX.X, ALU.max, apply_absolute_value=True))
                link(dve.tensor_scalar(s[:, 0:1], s[:, 0:1], LN_EPS, None, ALU.max))
                link(dve.reciprocal(s[:, 1:2], s[:, 0:1]))
                link(dve.tensor_scalar(s[:, 2:3], s[:, 1:2], 127.0, None, ALU.mult))
                link(dve.tensor_scalar(s[:, 3:4], s[:, 0:1], 1.0 / 127.0, wsc[:, 0, 0:1], ALU.mult, ALU.mult))
                link(dve.tensor_scalar(xq[:, :], xn[:, :], s[:, 2:3], RINT, ALU.mult, ALU.add))
                link(dve.tensor_scalar(xq[:, :], xq[:, :], -RINT, -128.0, ALU.add, ALU.max))
                if t >= 2:
                    dve.wait_ge(x_turned, t - 1)
                dve.tensor_scalar(xq16[:, t % 2, :], xq[:, :], 127.0, None, ALU.min).then_inc(x_ready, 1)
                dve.wait_ge(x_ready, t + 1)

            def hidden(t):
                s = hs[:, t % 2, :]
                dve.wait_ge(h_done, t + 1)
                link(dve.tensor_scalar(hid[:, :], ph[t % 2][:, 0:FF], xs[:, t % 2, 3:4], 0.0, ALU.mult, ALU.max))
                link(dve.tensor_scalar(hid[:, :], hid[:, :], RINT, -RINT, ALU.add, ALU.add))
                link(dve.tensor_scalar(hid[:, :], hid[:, :], 127.0, None, ALU.min))
                link(dve.tensor_reduce(s[:, 0:1], hid[:, :], AX.X, ALU.max))
                link(dve.tensor_scalar(s[:, 0:1], s[:, 0:1], LN_EPS, None, ALU.max))
                link(dve.reciprocal(s[:, 1:2], s[:, 0:1]))
                link(dve.tensor_scalar(s[:, 2:3], s[:, 1:2], 127.0, None, ALU.mult))
                link(dve.tensor_scalar(s[:, 3:4], s[:, 0:1], 1.0 / 127.0, wsc[:, 0, 1:2], ALU.mult, ALU.mult))
                link(dve.tensor_scalar(hid[:, :], hid[:, :], s[:, 2:3], RINT, ALU.mult, ALU.add))
                link(dve.tensor_scalar(hid[:, :], hid[:, :], -RINT, 127.0, ALU.add, ALU.min))
                if t >= 2:
                    dve.wait_ge(h_turned, t - 1)
                dve.tensor_copy(hq16[:, t % 2, :], hid[:, :]).then_inc(h_ready, 1)
                dve.wait_ge(h_ready, t + 1)

            def finish(t):
                dve.wait_ge(y_done, t + 1)
                if t >= 2:
                    dve.wait_ge(stored[t % 2], 16 * (t // 2))
                dve.scalar_tensor_tensor(y[:, t % 2, :], py[t % 2][:, :], hs[:, t % 2, 3:4], res[:, t, :],
                                         ALU.mult, ALU.add).then_inc(y_ready, 1)
                dve.wait_ge(y_ready, t + 1)

            quantise(0)
            for t in range(NT):
                if t + 1 < NT:
                    quantise(t + 1)
                hidden(t)
                if t >= 1:
                    finish(t - 1)
            finish(NT - 1)

        @block.scalar
        def _(act):
            for k in range(3):
                act.wait_ge(w_turned, k + 1)
                if k < 2:
                    act.activation(wuT[:, :, k * P:(k + 1) * P], pt[:, 0:D].rearrange("p (c f) -> p c f", c=C),
                                   ACT.Copy).then_inc(w_copied, 1)
                else:
                    act.activation(wdT[:, :, :], pt[:, :].rearrange("p (a o) -> p a o", a=UC), ACT.Copy).then_inc(w_copied, 1)
            act.wait_ge(sd_in, 1)
            act.activation(sd[:, 1, :], sd[:, 0, :], ACT.Sqrt).then_inc(sd_out, 1)

            def x_copy(t):
                act.wait_ge(x_turned, t + 1)
                if t >= 2:
                    act.wait_ge(h_done, t - 1)
                act.activation(xqT[:, t % 2, :], pt[:, 0:D], ACT.Copy).then_inc(xT_ready, 1)

            x_copy(0)
            for t in range(NT):
                if t + 1 < NT:
                    x_copy(t + 1)
                act.wait_ge(h_turned, t + 1)
                if t >= 2:
                    act.wait_ge(y_done, t - 1)
                act.activation(hqT[:, t % 2, :], pht[:, 0:FF], ACT.Copy).then_inc(hT_ready, 1)

        @block.tensor
        def _(pe):
            pe.wait_ge(cst, 1)
            pe.wait_ge(step, 2)
            pe.matmul(pw[:, 0:2], onem[:, :], sums[:, :], start=True, stop=True).then_inc(total, 1)
            pe.wait_ge(idb, 1)
            pe.wait_ge(w_ready, 1)
            for k in range(2):
                if k:
                    pe.wait_ge(w_copied, k)
                for c in range(C):
                    last = pe.transpose(pt[:, c * P:(c + 1) * P], tern16[:, 0, k * D + c * P:k * D + (c + 1) * P], ident_b[:, :])
                last.then_inc(w_turned, 1)
            pe.wait_ge(w_ready, 2)
            pe.wait_ge(w_copied, 2)
            for a in range(UC):
                for o in range(DC):
                    last = pe.transpose(pt[:, a * D + o * P:a * D + (o + 1) * P],
                                        tern16[:, 1, o * FF + a * P:o * FF + (a + 1) * P], ident_b[:, :])
            last.then_inc(w_turned, 1)
            pe.wait_ge(w_copied, 3)

            def up(t):
                pe.wait_ge(x_ready, t + 1)
                if t >= 1:
                    pe.wait_ge(xT_ready, t)
                for c in range(C):
                    last = pe.transpose(pt[:, c * P:(c + 1) * P], xq16[:, t % 2, c * P:(c + 1) * P], ident_b[:, :])
                last.then_inc(x_turned, 1)
                pe.wait_ge(xT_ready, t + 1)
                if t >= 2:
                    pe.wait_ge(h_ready, t - 1)
                for c in range(C):
                    last = pe.matmul(ph[t % 2][:, 0:FF], xqT[:, t % 2, c * P:(c + 1) * P], wuT[:, c, :],
                                     start=c == 0, stop=c == C - 1)
                last.then_inc(h_done, 1)

            def down(t):
                pe.wait_ge(h_ready, t + 1)
                if t >= 1:
                    pe.wait_ge(hT_ready, t)
                for a in range(UC):
                    last = pe.transpose(pht[:, a * P:(a + 1) * P], hq16[:, t % 2, a * P:(a + 1) * P], ident_b[:, :])
                last.then_inc(h_turned, 1)
                pe.wait_ge(hT_ready, t + 1)
                if t >= 2:
                    pe.wait_ge(y_ready, t - 1)
                for a in range(UC):
                    last = pe.matmul(py[t % 2][:, :], hqT[:, t % 2, a * P:(a + 1) * P], wdT[:, a, :],
                                     start=a == 0, stop=a == UC - 1)
                last.then_inc(y_done, 1)

            up(0)
            for t in range(NT):
                if t + 1 < NT:
                    up(t + 1)
                down(t)


_INS = ["x", "src", "dst", "edge_attr_512", "L0_gnn_Wq", "L0_gnn_bq", "L0_gnn_Wr", "L0_gnn_br", "L0_gnn_Wk", "L0_gnn_bk",
        "L0_gnn_Wv", "L0_gnn_bv", "L0_gnn_Wo", "L0_gnn_bo", "L0_gnn_gamma", "L0_gnn_beta", "L0_mix_w_qkv",
        "L0_mix_w_proj", "L0_mix_b_proj", "L0_ffn_w_up", "L0_ffn_w_down"]


def kernel(**inputs):
    import numpy as _np
    import concourse.bacc as _bacc
    from concourse import mybir as _mybir
    from concourse.bass_utils import run_bass_kernel_spmd as _run

    nc = _bacc.Bacc("TRN2", target_bir_lowering=False, num_devices=1)
    arrays, args = {}, []
    for name in _INS:
        a = _np.ascontiguousarray(inputs[name])
        arrays[f"in_{name}_dram"] = a
        args.append(nc.dram_tensor(f"in_{name}_dram", a.shape, _mybir.dt.from_np(a.dtype), kind="ExternalInput").ap())
    out = nc.dram_tensor("out_dram", [N, D], _mybir.dt.float32, kind="ExternalOutput").ap()
    layer(nc, *args, out)
    r = _run(nc, [arrays], core_ids=[0])
    return r.results[0]["out_dram"]
```

```python
import numpy as np
import concourse.bass as bass
from concourse import mybir
from contextlib import ExitStack

F32 = mybir.dt.float32
F32R = mybir.dt.float32r
BF16 = mybir.dt.bfloat16
I32 = mybir.dt.int32
ALU = mybir.AluOpType
ACT = mybir.ActivationFunctionType
AX = mybir.AxisListType

P = 128
N, D, E, H = 1250, 512, 20000, 8
DH = D // H
C = D // P
NT = -(-N // P)
NP = NT * P
NLAST = N - (NT - 1) * P
ET = -(-E // P)
ELAST = E - (ET - 1) * P
HW = DH + 1
ROW = H * HW
TROW = ROW + H
QROW = D + H
FF = 256
SCALE = 1.0 / 8.0
NEG = -3.0e38
OOB = 2048.0
LN_EPS = 1e-5
MIX_EPS = 1e-6
RINT = 12582912.0
NCH = [(0, 512), (512, 512), (1024, 256)]


def node_rows(t):
    return P if t < NT - 1 else NLAST


def bc(ap, n):
    return ap.unsqueeze(len(ap.shape)).to_broadcast(list(ap.shape) + [n])


def layer(nc, x, src, dst, ef, Wq, bq, Wr, br, Wk, bk, Wv, bv, Wo, bo, gamma, beta,
          w_qkv, w_proj, b_proj, w_up, w_down, out):
    q_table = nc.dram_tensor("q_table", [NP, QROW], F32, kind="Internal").ap()
    kv_table = nc.dram_tensor("kv_table", [NP, 2 * D], F32, kind="Internal").ap()
    merge = [nc.dram_tensor(f"merge{i}", [NP, TROW], F32, kind="Internal").ap() for i in range(2)]

    top = ExitStack()
    with top:
        def keep(name, shape, dt=F32):
            return top.enter_context(nc.sbuf_tensor(name, shape, dt))

        ident = keep("ident", [P, P])
        xnT = keep("xnT", [P, C, NP])
        res = keep("res", [P, NT, D])
        v2 = keep("v2", [P, NT, D])
        WoT = keep("WoT", [P, C, D])
        ones = keep("ones", [1, P])

        with ExitStack() as early:
            Me_hi = early.enter_context(nc.sbuf_tensor("Me_hi", [P, C, 2 * D], F32R))
            Me_lo = early.enter_context(nc.sbuf_tensor("Me_lo", [P, C, 2 * D], F32R))
            with ExitStack() as mid:
                Mn = mid.enter_context(nc.sbuf_tensor("Mn", [P, 2, C, 2 * D], F32))
                WqT = mid.enter_context(nc.sbuf_tensor("WqT", [P, C, D], F32))
                kv_bias = mid.enter_context(nc.sbuf_tensor("kv_bias", [1, 2 * D], F32))
                prepare(nc, x, Wq, bq, Wr, br, Wk, bk, Wv, bv, Wo, ident, ones, xnT, res, WqT, WoT, Me_hi, Me_lo, Mn, kv_bias, v2)
                node_tables(nc, bq, q_table, kv_table, merge, xnT, ones, WqT, Mn, kv_bias, v2)
            edges(nc, src, dst, ef, q_table, kv_table, merge, ident, Me_hi, Me_lo)
        with ExitStack() as end:
            gT = end.enter_context(nc.sbuf_tensor("gT", [P, C, NP], F32))
            mix_and_sums(nc, w_qkv, w_proj, b_proj, merge, xnT, v2, gT, ident, ones, res)
            gnn_end(nc, bo, gamma, beta, ident, xnT, gT, WoT, res)
        ffn(nc, w_up, w_down, ident, res, out)


def prepare(nc, x, Wq, bq, Wr, br, Wk, bk, Wv, bv, Wo, ident, ones, xnT, res, WqT, WoT, Me_hi, Me_lo, Mn, kv_bias, v2):
    with ExitStack() as ctx:
        def sb(name, shape, dt=F32):
            return ctx.enter_context(nc.sbuf_tensor(name, shape, dt))

        def sem(name):
            return ctx.enter_context(nc.semaphore(name))

        raw = sb("raw", [P, C, D])
        raw2 = sb("raw2", [P, C, D])
        wr = sb("wr", [P, C, 3 * D])
        WkT = sb("WkT", [P, C, D])
        WvT = sb("WvT", [P, C, D])
        br_col = sb("br_col", [P, C])
        bkv = sb("bkv", [1, 2 * D])
        stats = sb("stats", [P, NT, 6])
        mv = sb("mv", [P, NT, 2])
        std = sb("std", [P, NT])
        rstd = sb("rstd", [P, NT])
        xn = v2[:, 0:2, :]
        banks = [ctx.enter_context(nc.psum_tensor(f"bank{i}", [P, D], F32)) for i in range(8)]
        x_clear, x_in, w_in = sem("x_clear"), sem("x_in"), [sem(f"w_in{i}") for i in range(4)]
        wr_in, small_in = sem("wr_in"), sem("small_in")
        ident_step, ones_set = sem("ident_step"), sem("ones_set")
        stats_done, mv_done, var_eps, std_done, rstd_done, xn_done = (
            sem("stats_done"), sem("mv_done"), sem("var_eps"), sem("std_done"), sem("rstd_done"), sem("xn_done"))
        turned, copied = sem("turned"), sem("copied")
        folded, fold_copied, hi_ready = sem("folded"), sem("fold_copied"), sem("hi_ready")
        block = ctx.enter_context(nc.Block())
        raws = [raw, raw2]
        weights = [(Wk, WkT), (Wv, WvT), (Wq, WqT), (Wo, WoT)]

        @block.sync
        def _(sp):
            for i, (w, _) in enumerate(weights):
                if i == 2:
                    sp.wait_ge(x_clear, 1)
                    sp.dma_start(res[:, 0:NT - 1, :], x[0:(NT - 1) * P, :].rearrange("(t p) d -> p t d", p=P)).then_inc(x_in, 16)
                    sp.dma_start(res[0:NLAST, NT - 1, :], x[(NT - 1) * P:N, :]).then_inc(x_in, 16)
                if i >= 2:
                    sp.wait_ge(turned, C * (i - 1))
                sp.dma_start(raws[i % 2][:, :, :], w.rearrange("(c p) i -> p c i", p=P)).then_inc(w_in[i], 16)

        @block.gpsimd
        def _(pool):
            pool.memset(ident[:, :], 0.0).then_inc(ident_step, 1)
            pool.memset(ones[:, :], 1.0).then_inc(ones_set, 1)
            pool.wait_ge(ident_step, 1)
            pool.affine_select(out=ident[:, :], in_=ident[:, :], compare_op=ALU.not_equal, fill=1.0, base=0,
                               pattern=[[-1, P]], channel_multiplier=1).then_inc(ident_step, 1)

        @block.vector
        def _(dve):
            dve.memset(res[:, NT - 1, :], 0.0).then_inc(x_clear, 1)
            dve.wait_ge(x_in, 32)
            for t in range(NT):
                dve.bn_stats(stats[:, t, :], res[:, t, :]).then_inc(stats_done, 1)
            for t in range(NT):
                dve.wait_ge(stats_done, t + 1)
                dve.bn_aggr(mv[:, t, :], stats[:, t, :]).then_inc(mv_done, 1)
            dve.wait_ge(mv_done, NT)
            dve.tensor_scalar(std[:, :], mv[:, :, 1], LN_EPS, None, ALU.add).then_inc(var_eps, 1)
            dve.wait_ge(std_done, 1)
            dve.reciprocal(rstd[:, :], std[:, :]).then_inc(rstd_done, 1)
            dve.wait_ge(rstd_done, 1)
            for t in range(NT):
                if t >= 2:
                    dve.wait_ge(turned, 4 * C + t - 1)
                dve.tensor_scalar(xn[:, t % 2, :], res[:, t, :], mv[:, t, 0:1], rstd[:, t:t + 1],
                                  ALU.subtract, ALU.mult).then_inc(xn_done, 1)
            for k in range(16, 24):
                ic, half = k // 2 % C, k % 2
                dve.wait_ge(hi_ready, k - 15)
                dve.tensor_tensor(Me_lo[:, ic, half * D:(half + 1) * D], banks[k % 8][:, :],
                                  Me_hi[:, ic, half * D:(half + 1) * D].bitcast(F32), ALU.subtract).then_inc(fold_copied, 1)
            dve.wait_ge(small_in, 48)
            for half in range(2):
                dve.wait_ge(folded, 24 + half + 1)
                dve.tensor_tensor(kv_bias[0:1, half * D:(half + 1) * D], banks[half][0:1, :],
                                  bkv[0:1, half * D:(half + 1) * D], ALU.add).then_inc(fold_copied, 1)

        @block.scalar
        def _(act):
            act.dma_start(wr[:, :, :], Wr.rearrange("(c p) i -> p c i", p=P)).then_inc(wr_in, 16)
            act.dma_start(br_col[:, :], br.rearrange("(c p) -> p c", p=P),
                              allow_slow_non_contiguous=True).then_inc(small_in, 16)
            act.dma_start(bkv[:, 0:D], bk.unsqueeze(0)).then_inc(small_in, 16)
            act.dma_start(bkv[:, D:2 * D], bv.unsqueeze(0)).then_inc(small_in, 16)
            act.wait_ge(var_eps, 1)
            act.activation(std[:, :], std[:, :], ACT.Sqrt).then_inc(std_done, 1)
            for k in range(4 * C + NT):
                act.wait_ge(turned, k + 1)
                bank = banks[k % 8][:, :].rearrange("p (c o) -> p c o", c=C)
                if k < 4 * C:
                    to = weights[k // C][1][:, :, (k % C) * P:(k % C + 1) * P]
                else:
                    to = xnT[:, :, (k - 4 * C) * P:(k - 4 * C + 1) * P]
                act.activation(to, bank, ACT.Copy).then_inc(copied, 1)
            for k in range(24):
                act.wait_ge(folded, k + 1)
                part, ic, half = k // 8, k // 2 % C, k % 2
                if part == 2:
                    act.activation(Me_hi[:, ic, half * D:(half + 1) * D], banks[k % 8][:, :], ACT.Copy).then_inc(hi_ready, 1)
                else:
                    act.activation(Mn[:, part, ic, half * D:(half + 1) * D], banks[k % 8][:, :],
                                   ACT.Copy).then_inc(fold_copied, 1)

        @block.tensor
        def _(pe):
            pe.wait_ge(ident_step, 2)
            for k in range(4 * C + NT):
                if k >= 8:
                    pe.wait_ge(copied, k - 7)
                if k < 4 * C:
                    pe.wait_ge(w_in[k // C], 16)
                    source = raws[(k // C) % 2][:, k % C, :]
                else:
                    pe.wait_ge(xn_done, k - 4 * C + 1)
                    source = xn[:, (k - 4 * C) % 2, :]
                for c in range(C):
                    last = pe.transpose(banks[k % 8][:, c * P:(c + 1) * P], source[:, c * P:(c + 1) * P], ident[:, :])
                last.then_inc(turned, 1)
            pe.wait_ge(wr_in, 16)
            pe.wait_ge(copied, 4 * C + NT)
            for k in range(24):
                part, ic, half = k // 8, k // 2 % C, k % 2
                if k >= 8:
                    pe.wait_ge(fold_copied, k - 7)
                for rc in range(C):
                    last = pe.matmul(banks[k % 8][:, :], wr[:, rc, part * D + ic * P:part * D + (ic + 1) * P],
                                     (WkT, WvT)[half][:, rc, :], start=rc == 0, stop=rc == C - 1)
                last.then_inc(folded, 1)
            pe.wait_ge(small_in, 48)
            pe.wait_ge(fold_copied, 24)
            for half in range(2):
                for rc in range(C):
                    last = pe.matmul(banks[half][0:1, :], br_col[:, rc:rc + 1], (WkT, WvT)[half][:, rc, :],
                                     start=rc == 0, stop=rc == C - 1)
                last.then_inc(folded, 1)


def node_tables(nc, bq, q_table, kv_table, merge, xnT, ones, WqT, Mn, kv_bias, v2):
    with ExitStack() as ctx:
        def sb(name, shape, dt=F32):
            return ctx.enter_context(nc.sbuf_tensor(name, shape, dt))

        def sem(name):
            return ctx.enter_context(nc.semaphore(name))

        bq_row = sb("bq_row", [1, D])
        q_out = sb("q_out", [P, 2, QROW])
        kv_out = sb("kv_out", [P, 2, 2 * D])
        own = sb("own", [P, D])
        empty = sb("empty", [P, TROW])
        banks = [ctx.enter_context(nc.psum_tensor(f"nbank{i}", [P, D], F32)) for i in range(5)]
        bq_in, done, empty_set, tables_out = sem("bq_in"), sem("done"), sem("empty_set"), sem("tables_out")
        q_copied, kv_copied, own_mul, own_sum, v2_copied = (
            sem("q_copied"), sem("kv_copied"), sem("own_mul"), sem("own_sum"), sem("v2_copied"))
        q_stored = [sem(f"q_stored{i}") for i in range(2)]
        kv_stored = [sem(f"kv_stored{i}") for i in range(2)]
        block = ctx.enter_context(nc.Block())

        @block.sync
        def _(sp):
            sp.dma_start(bq_row[:, :], bq.unsqueeze(0)).then_inc(bq_in, 16)
            for t in range(NT):
                sp.wait_ge(kv_copied, 2 * (t + 1))
                sp.dma_start(kv_table[t * P:(t + 1) * P, :], kv_out[:, t % 2, :]).then_inc(kv_stored[t % 2], 16)
                sp.wait_ge(own_sum, t + 1)
                sp.dma_start(q_table[t * P:(t + 1) * P, :], q_out[:, t % 2, :]).then_inc(q_stored[t % 2], 16)
            for i in range(2):
                sp.wait_ge(kv_stored[i], 16 * (NT // 2))
                sp.wait_ge(q_stored[i], 16 * (NT // 2))

        @block.gpsimd
        def _(pool):
            pool.memset(empty[:, 0:ROW], 0.0).then_inc(empty_set, 1)
            pool.memset(empty[:, ROW:TROW], NEG).then_inc(empty_set, 1)
            pool.wait_ge(empty_set, 2)
            for i in range(2):
                for t in range(NT):
                    pool.dma_start(merge[i][t * P:(t + 1) * P, :], empty[:, :]).then_inc(tables_out, 16)
            pool.wait_ge(tables_out, 16 * 2 * NT)

        @block.tensor
        def _(pe):
            pe.wait_ge(bq_in, 16)
            for t in range(NT):
                for b in range(5):
                    if t >= 1:
                        if b == 0:
                            pe.wait_ge(q_copied, t)
                        elif b <= 2:
                            pe.wait_ge(kv_copied, 2 * (t - 1) + b)
                        elif b == 3:
                            pe.wait_ge(own_mul, t)
                        else:
                            pe.wait_ge(v2_copied, t)
                    for c in range(C):
                        rhs = WqT[:, c, :] if b == 0 else Mn[:, (b - 1) // 2, c, ((b - 1) % 2) * D:((b - 1) % 2 + 1) * D]
                        last = pe.matmul(banks[b][:, :], xnT[:, c, t * P:(t + 1) * P], rhs,
                                         start=c == 0, stop=c == C - 1 and b in (1, 2))
                    if b == 0:
                        last = pe.matmul(banks[b][:, :], ones[:, :], bq_row[:, :], start=False, stop=True)
                    elif b >= 3:
                        last = pe.matmul(banks[b][:, :], ones[:, :], kv_bias[:, (b - 3) * D:(b - 2) * D],
                                         start=False, stop=True)
                    last.then_inc(done, 1)

        @block.scalar
        def _(act):
            for t in range(NT):
                act.wait_ge(done, 5 * t + 1)
                if t >= 2:
                    act.wait_ge(q_stored[t % 2], 16 * (t // 2))
                act.activation(q_out[:, t % 2, 0:D], banks[0][:, :], ACT.Copy).then_inc(q_copied, 1)
                if t >= 2:
                    act.wait_ge(kv_stored[t % 2], 16 * (t // 2))
                for half in range(2):
                    act.wait_ge(done, 5 * t + 2 + half)
                    act.activation(kv_out[:, t % 2, half * D:(half + 1) * D], banks[1 + half][:, :],
                                   ACT.Copy).then_inc(kv_copied, 1)
                act.wait_ge(done, 5 * t + 5)
                act.activation(v2[:, t, :], banks[4][:, :], ACT.Copy).then_inc(v2_copied, 1)

        @block.vector
        def _(dve):
            for t in range(NT):
                dve.wait_ge(done, 5 * t + 4)
                dve.wait_ge(q_copied, t + 1)
                if t >= 1:
                    dve.wait_ge(own_sum, t)
                dve.tensor_tensor(own[:, :], banks[3][:, :], q_out[:, t % 2, 0:D], ALU.mult).then_inc(own_mul, 1)
                dve.wait_ge(own_mul, t + 1)
                dve.tensor_reduce(q_out[:, t % 2, D:QROW], own[:, :].rearrange("p (h d) -> p h d", h=H),
                                  AX.X, ALU.add).then_inc(own_sum, 1)


def mix_and_sums(nc, w_qkv, w_proj, b_proj, merge, xnT, v2, gT, ident, ones, res):
    with ExitStack() as ctx:
        def sb(name, shape, dt=F32):
            return ctx.enter_context(nc.sbuf_tensor(name, shape, dt))

        def sem(name):
            return ctx.enter_context(nc.semaphore(name))

        PAIR = 2 * HW
        w = sb("w_mix", [P, C, 3 * D])
        wp = sb("wp", [P, C, D])
        bp = sb("bp", [1, D])
        qfT = sb("qfT", [P, C, NP])
        small = sb("small", [P, 2, D])
        big = sb("big", [P, 2, D])
        kf = sb("kf", [P, 2, D])
        v1 = sb("v1", [P, 2, H, HW])
        kvd = sb("kvd", [P, C, PAIR])
        z = sb("z", [P, 2, 2, H])
        y = sb("y", [P, 2, D])
        yT = sb("yT", [P, 2, D])
        rows = sb("rows", [P, 2, 2, TROW])
        nmax = sb("nmax", [P, H])
        dif = sb("dif", [P, 2, H])
        scl = sb("scl", [P, 2, H])
        part = sb("part", [P, 2, ROW])
        tot = sb("tot", [P, ROW])
        safe = sb("safe", [P, 4, H])
        own = sb("own2", [P, D])
        g0 = sb("g0", [P, D])
        g = sb("g", [P, 2, D])

        def bank(name):
            return ctx.enter_context(nc.psum_tensor(name, [P, D], F32))
        kb = [bank(f"kb{i}") for i in range(2)]
        vb, gb = bank("vb"), bank("gb")
        kvb = [bank(f"kvb{i}") for i in range(4)]
        ob, tb, pb = [kb, kvb[0:2]], [vb, kvb[2]], [gb, kvb[3]]

        w_in, wp_in, rows_in = sem("w_in"), sem("wp_in"), [sem(f"rows_in{i}") for i in range(2)]
        k_done, v_done, q_done = sem("k_done"), sem("v_done"), sem("q_done")
        low, exped, high = sem("low"), sem("exped"), sem("high")
        v_copied, v_ones, kv_added, kvd_zero, kvd_done = (
            sem("v_copied"), sem("v_ones"), sem("kv_added"), sem("kvd_zero"), sem("kvd_done"))
        link, dif_done, scl_done, g_done, g_turned, gT_done = (
            sem("sum_link"), sem("dif_done"), sem("scl_done"), sem("g_done"), sem("g_turned"), sem("gT_done"))
        own_done, g0_done = sem("own_done"), sem("g0_done")
        y_done, z_eps, z_inv, y_scaled, y_turned, yT_copied, p_done, res_done = (
            sem("y_done"), sem("z_eps"), sem("z_inv"), sem("y_scaled"), sem("y_turned"), sem("yT_copied"),
            sem("p_done"), sem("res_done"))
        block = ctx.enter_context(nc.Block())
        QJ = [(c, n0, nn) for c in range(C) for n0, nn in NCH]

        @block.sync
        def _(sp):
            for half in (1, 2, 0):
                sp.dma_start(w[:, :, half * D:(half + 1) * D],
                             w_qkv.rearrange("(c p) o -> p c o", p=P)[:, :, half * D:(half + 1) * D]).then_inc(w_in, 16)
            sp.dma_start(wp[:, :, :], w_proj.rearrange("(c p) o -> p c o", p=P)).then_inc(wp_in, 16)
            sp.dma_start(bp[:, :], b_proj.unsqueeze(0)).then_inc(wp_in, 16)
            for t in range(NT):
                if t >= 2:
                    sp.wait_ge(g_done, t - 1)
                for i in range(2):
                    sp.dma_start(rows[:, t % 2, i, :], merge[i][t * P:(t + 1) * P, :]).then_inc(rows_in[t % 2], 16)

        @block.gpsimd
        def _(pool):
            pool.memset(v1[:, :, :, DH:HW], 1.0).then_inc(v_ones, 1)
            pool.memset(kvd[:, :, :], 0.0).then_inc(kvd_zero, 1)

        @block.vector
        def _(dve):
            def before_exp(t, nn):
                if t >= 2:
                    dve.wait_ge(high, t - 1)
                dve.tensor_scalar(small[:, t % 2, 0:nn], kb[t % 2][:, 0:nn], 0.0, None, ALU.min).then_inc(low, 1)

            def after_exp(t, out, nn):
                dve.wait_ge(exped, t + 1)
                dve.scalar_tensor_tensor(out, kb[t % 2][:, 0:nn], 0.0, big[:, t % 2, 0:nn],
                                         ALU.max, ALU.add).then_inc(high, 1)

            def sums(t):
                a = rows[:, t % 2, :, :]
                before = 8 * t
                dve.wait_ge(rows_in[t % 2], 32 * (t // 2 + 1))
                dve.tensor_tensor(nmax[:, :], a[:, 0, ROW:TROW], a[:, 1, ROW:TROW], ALU.max).then_inc(link, 1)
                dve.wait_ge(link, before + 1)
                for i in range(2):
                    dve.tensor_tensor(dif[:, i, :], a[:, i, ROW:TROW], nmax[:, :], ALU.subtract).then_inc(dif_done, 1)
                dve.wait_ge(scl_done, t + 1)
                for i in range(2):
                    dve.tensor_tensor(part[:, i, :].rearrange("p (h e) -> p h e", e=HW),
                                      a[:, i, 0:ROW].rearrange("p (h e) -> p h e", e=HW),
                                      bc(scl[:, i, :], HW), ALU.mult).then_inc(link, 1)
                dve.wait_ge(link, before + 3)
                dve.tensor_tensor(tot[:, :], part[:, 0, :], part[:, 1, :], ALU.add).then_inc(link, 1)
                th = tot[:, :].rearrange("p (h e) -> p h e", e=HW)
                dve.wait_ge(link, before + 4)
                dve.tensor_scalar(safe[:, 0, :], th[:, :, DH], 0.0, None, ALU.is_equal).then_inc(link, 1)
                dve.tensor_scalar(safe[:, 3, :], th[:, :, DH], 0.0, None, ALU.is_gt).then_inc(link, 1)
                dve.wait_ge(link, before + 5)
                dve.tensor_tensor(safe[:, 1, :], safe[:, 0, :], th[:, :, DH], ALU.add).then_inc(link, 1)
                dve.wait_ge(link, before + 6)
                dve.tensor_tensor(own[:, :].rearrange("p (h d) -> p h d", h=H),
                                  v2[:, t, :].rearrange("p (h d) -> p h d", h=H), bc(safe[:, 3, :], DH),
                                  ALU.mult).then_inc(own_done, 1)
                dve.wait_ge(link, before + 7)
                dve.reciprocal(safe[:, 2, :], safe[:, 1, :]).then_inc(link, 1)
                dve.wait_ge(link, before + 8)
                dve.tensor_tensor(g0[:, :].rearrange("p (h d) -> p h d", h=H), th[:, :, 0:DH],
                                  bc(safe[:, 2, :], DH), ALU.mult).then_inc(g0_done, 1)
                if t >= 2:
                    dve.wait_ge(g_turned, t - 1)
                dve.wait_ge(g0_done, t + 1)
                dve.wait_ge(own_done, t + 1)
                dve.tensor_tensor(g[:, t % 2, :], g0[:, :], own[:, :], ALU.add).then_inc(g_done, 1)

            for t in range(NT):
                dve.wait_ge(k_done, t + 1)
                before_exp(t, D)
                if t >= 1:
                    dve.wait_ge(g_done, t)
                sums(t)
                if t >= 2:
                    dve.wait_ge(kv_added, t - 1)
                after_exp(t, kf[:, t % 2, :], D)
            for j, (c, n0, nn) in enumerate(QJ):
                dve.wait_ge(q_done, j + 1)
                before_exp(NT + j, nn)
                after_exp(NT + j, qfT[:, c, n0:n0 + nn], nn)
            dve.wait_ge(kv_added, NT)
            dve.wait_ge(kvd_zero, 1)
            for c in range(C):
                dve.tensor_copy(kvd[0:DH, c, 0:HW], kvb[c][0:DH, 0:HW]).then_inc(kvd_done, 1)
                dve.tensor_copy(kvd[DH:P, c, HW:PAIR], kvb[c][DH:P, HW:PAIR]).then_inc(kvd_done, 1)

            def add_projection(t):
                dve.wait_ge(p_done, t + 1)
                dve.tensor_tensor(res[:, t, :], pb[t % 2][:, :], res[:, t, :], ALU.add).then_inc(res_done, 1)

            for t in range(NT):
                u = t % 2
                dve.wait_ge(y_done, t + 1)
                if t >= 2:
                    dve.wait_ge(y_scaled, 2 * (t - 1))
                heads = [ob[u][b][:, 0:2 * PAIR].rearrange("p (h e) -> p h e", e=HW) for b in range(2)]
                for b in range(2):
                    dve.tensor_scalar(z[:, u, 0, 4 * b:4 * b + 4], heads[b][:, :, DH], MIX_EPS, None,
                                      ALU.add).then_inc(z_eps, 1)
                dve.wait_ge(z_eps, 2 * (t + 1))
                dve.reciprocal(z[:, u, 1, :], z[:, u, 0, :]).then_inc(z_inv, 1)
                dve.wait_ge(z_inv, t + 1)
                if t >= 2:
                    dve.wait_ge(y_turned, t - 1)
                for b in range(2):
                    dve.tensor_tensor(y[:, u, b * 256:(b + 1) * 256].rearrange("p (h d) -> p h d", d=DH),
                                      heads[b][:, :, 0:DH], bc(z[:, u, 1, 4 * b:4 * b + 4], DH),
                                      ALU.mult).then_inc(y_scaled, 1)
                if t >= 1:
                    add_projection(t - 1)
            add_projection(NT - 1)

        @block.scalar
        def _(act):
            for t in range(NT):
                act.wait_ge(low, t + 1)
                if t >= 2:
                    act.wait_ge(high, t - 1)
                act.activation(big[:, t % 2, :], small[:, t % 2, :], ACT.Exp).then_inc(exped, 1)
                act.wait_ge(dif_done, 2 * (t + 1))
                act.activation(scl[:, :, :], dif[:, :, :], ACT.Exp, scale=SCALE).then_inc(scl_done, 1)
                act.wait_ge(v_done, t + 1)
                act.wait_ge(v_ones, 1)
                if t >= 2:
                    act.wait_ge(kv_added, t - 1)
                act.activation(v1[:, t % 2, :, 0:DH], vb[:, :].rearrange("p (h d) -> p h d", h=H),
                               ACT.Copy).then_inc(v_copied, 1)
                act.wait_ge(g_turned, t + 1)
                act.activation(gT[:, :, t * P:(t + 1) * P], gb[:, :].rearrange("p (c e) -> p c e", c=C),
                               ACT.Copy).then_inc(gT_done, 1)
            for j, (c, n0, nn) in enumerate(QJ):
                t = NT + j
                act.wait_ge(low, t + 1)
                act.wait_ge(high, t - 1)
                act.activation(big[:, t % 2, 0:nn], small[:, t % 2, 0:nn], ACT.Exp).then_inc(exped, 1)
            for t in range(NT):
                act.wait_ge(y_turned, t + 1)
                if t >= 2:
                    act.wait_ge(p_done, t - 1)
                act.activation(yT[:, t % 2, :], tb[t % 2][:, :], ACT.Copy).then_inc(yT_copied, 1)

        @block.tensor
        def _(pe):
            pe.wait_ge(w_in, 48)

            def add_kv(t):
                pe.wait_ge(high, t + 1)
                pe.wait_ge(v_copied, t + 1)
                r = node_rows(t)
                for c in range(C):
                    last = pe.matmul(kvb[c][:, 0:PAIR], kf[0:r, t % 2, c * P:(c + 1) * P],
                                     v1[0:r, t % 2, 2 * c:2 * c + 2, :], start=t == 0, stop=t == NT - 1)
                last.then_inc(kv_added, 1)

            for t in range(NT):
                if t >= 2:
                    pe.wait_ge(high, t - 1)
                for c in range(C):
                    last = pe.matmul(kb[t % 2][:, :], xnT[:, c, t * P:(t + 1) * P], w[:, c, D:2 * D],
                                     start=c == 0, stop=c == C - 1)
                last.then_inc(k_done, 1)
                if t >= 1:
                    pe.wait_ge(v_copied, t)
                for c in range(C):
                    last = pe.matmul(vb[:, :], xnT[:, c, t * P:(t + 1) * P], w[:, c, 2 * D:3 * D],
                                     start=c == 0, stop=c == C - 1)
                last.then_inc(v_done, 1)
                if t >= 1:
                    add_kv(t - 1)
                pe.wait_ge(g_done, t + 1)
                if t >= 1:
                    pe.wait_ge(gT_done, t)
                for c in range(C):
                    last = pe.transpose(gb[:, c * P:(c + 1) * P], g[:, t % 2, c * P:(c + 1) * P], ident[:, :])
                last.then_inc(g_turned, 1)
            add_kv(NT - 1)
            for j, (c, n0, nn) in enumerate(QJ):
                pe.wait_ge(high, NT + j - 1)
                for k in range(C):
                    last = pe.matmul(kb[(NT + j) % 2][:, 0:nn], w[:, k, c * P:(c + 1) * P], xnT[:, k, n0:n0 + nn],
                                     start=k == 0, stop=k == C - 1)
                last.then_inc(q_done, 1)
            pe.wait_ge(kvd_done, 2 * C)
            pe.wait_ge(high, NT + len(QJ))
            pe.wait_ge(v_copied, NT)
            pe.wait_ge(gT_done, NT)
            pe.wait_ge(wp_in, 32)

            def attend(t):
                if t >= 2:
                    pe.wait_ge(y_scaled, 2 * (t - 1))
                for c in range(C):
                    last = pe.matmul(ob[t % 2][c // 2][:, (c % 2) * PAIR:(c % 2 + 1) * PAIR],
                                     qfT[:, c, t * P:(t + 1) * P], kvd[:, c, :], start=True, stop=True)
                last.then_inc(y_done, 1)

            def turn(t):
                pe.wait_ge(y_scaled, 2 * (t + 1))
                if t >= 2:
                    pe.wait_ge(yT_copied, t - 1)
                for c in range(C):
                    last = pe.transpose(tb[t % 2][:, c * P:(c + 1) * P], y[:, t % 2, c * P:(c + 1) * P], ident[:, :])
                last.then_inc(y_turned, 1)

            def project(t):
                pe.wait_ge(yT_copied, t + 1)
                if t >= 2:
                    pe.wait_ge(res_done, t - 1)
                for c in range(C):
                    pe.matmul(pb[t % 2][:, :], yT[:, t % 2, c * P:(c + 1) * P], wp[:, c, :], start=c == 0, stop=False)
                pe.matmul(pb[t % 2][:, :], ones[:, :], bp[:, :], start=False, stop=True).then_inc(p_done, 1)

            attend(0)
            for t in range(NT):
                if t + 1 < NT:
                    attend(t + 1)
                turn(t)
                if t >= 1:
                    project(t - 1)
            project(NT - 1)


def edges(nc, src, dst, ef, q_table, kv_table, merge, ident, Me_hi, Me_lo):
    with ExitStack() as ctx:
        def sb(name, shape, dt=F32):
            return ctx.enter_context(nc.sbuf_tensor(name, shape, dt))

        def two(name, shape, dt=F32):
            return [sb(f"{name}{u}", shape, dt) for u in range(2)]

        def sem(name):
            return ctx.enter_context(nc.semaphore(name))

        ident16 = sb("ident16", [P, 4, P], BF16)
        pick = sb("pick", [3 * H, H, P], BF16)
        before = sb("before", [P, P])
        efs = two("efs", [P, D])
        efT = two("efT", [P, C, P])
        efT_hi = two("efT_hi", [P, C, P], F32R)
        efT_lo = two("efT_lo", [P, C, P], F32R)
        src_id = two("src_id", [P, 1], I32)
        dst_id = two("dst_id", [P, 1], I32)
        dst_row = two("dst_row", [P, P], I32)
        dst_col = two("dst_col", [P, 1], I32)
        equal = two("equal", [P, P])
        same = two("same", [P, P], F32R)
        apart = two("apart", [P, P], BF16)
        junk = sb("junk", [P, P])
        count = two("count", [P, 1])
        put_id = two("put_id", [P, 1], I32)
        kv = two("kv", [P, 2 * D])
        qc = two("qc", [P, QROW])
        old = two("old", [P, TROW])
        new = two("new", [P, TROW])
        kq = two("kq", [P, H, HW])
        score = two("score", [P, H])
        rest = sb("rest", [P, 2, H])
        parts = sb("parts", [P, 3 * H], BF16)
        partsT = sb("partsT", [3 * H, P], BF16)
        top = two("top", [P, H])
        diff = two("diff", [P, 2 * H])
        expd = two("expd", [P, 2 * H])
        wv = sb("wv", [P, H, HW])
        wv_hi = sb("wv_hi", [P, H, HW], F32R)
        wv_lo = sb("wv_lo", [P, H, HW], F32R)
        psT = ctx.enter_context(nc.psum_tensor("psT", [P, D], F32))
        psK = ctx.enter_context(nc.psum_tensor("psK", [P, D], F32))
        psV = [ctx.enter_context(nc.psum_tensor(f"psV{u}", [P, D], F32)) for u in range(2)]
        psB = ctx.enter_context(nc.psum_tensor("psB", [P, 2, D], F32))
        psS = ctx.enter_context(nc.psum_tensor("psS", [P, 2, D], F32))
        psA = psT[:, :].bitcast(BF16)

        consts = sem("consts")
        ids_in, pair_in, ef_in, kv_in, q_in, old_in, put = ([sem(f"{n}{u}") for u in range(2)] for n in
                                                   ("ids_in", "pair_in", "ef_in", "kv_in", "q_in", "old_in", "put"))
        turned, efT_ready, k_done, v_done = sem("ef_turned"), sem("efT_ready"), sem("k_edges"), sem("v_edges")
        equal_ready, same_ready, apart_ready, counted, putid_ready = (
            sem("equal_ready"), sem("same_ready"), sem("apart_ready"), sem("counted"), sem("putid_ready"))
        k_added, own_placed, k_times_q, score_ready = (
            sem("k_added"), sem("own_placed"), sem("k_times_q"), sem("score_ready"))
        part_step, parts_ready, parts_turned, partsT_ready, spread = (
            sem("part_step"), sem("parts_ready"), sem("parts_turned"), sem("partsT_ready"), sem("spread"))
        v_added, top_ready, newmax_ready, diff_ready, exp_ready = (
            sem("v_added"), sem("top_ready"), sem("newmax_ready"), sem("diff_ready"), sem("exp_ready"))
        efT_hi_ready, efT_lo_ready, wv_ready, wv_hi_ready, wv_lo_ready = (
            sem("efT_hi_ready"), sem("efT_lo_ready"), sem("wv_ready"), sem("wv_hi_ready"), sem("wv_lo_ready"))
        summed, old_scaled, new_ready = sem("summed"), sem("old_scaled"), sem("new_ready")
        block = ctx.enter_context(nc.Block())
        J = ET // 2
        assert ET % 2 == 1 and ELAST == 32

        def over_tiles(eng, engine, step):
            for j in range(2):
                step(j, 0)
                step(j, 1)
            with nc.Fori(2, J - 1, engines=[engine]) as i:
                j = eng.snap(i)
                step(j, 0)
                step(j, 1)
            for j in range(J - 1, J + 1):
                step(j, 0)
                step(j, 1)
            step(J + 1, 0)

        def tile_at(j, u, d):
            ud = (u + d) % 2
            jd = j + (u + d) // 2
            t = 2 * jd + ud
            if isinstance(t, int) and not 0 <= t < ET:
                return None
            return t, jd, ud, ELAST if isinstance(t, int) and t == ET - 1 else P

        def run(stage, j, u, d):
            tile = tile_at(j, u, d)
            if tile is not None:
                stage(*tile)

        def zero(t):
            return isinstance(t, int) and t == 0

        def later(j):
            return not (isinstance(j, int) and j == 0)

        def fixed(eng):
            eng.wait_ge(consts, 8)

        def value(eng, v):
            if not isinstance(v, int):
                v = eng.snap(v)
                eng.compute_val(v)
            return v

        @block.sync
        def _(sp):
            def load_features(t, j, u, r):
                row, before_last = value(sp, t * P), value(sp, t - 1)
                if later(j):
                    fixed(sp)
                    sp.wait_ge(turned, before_last)
                sp.dma_start(efs[u][0:r, :], ef[bass.ds(row, r), :]).then_inc(ef_in[u], 16)

            def load_ids(t, j, u, r):
                row, dmas = value(sp, t * P), value(sp, 16 * j)
                if later(j):
                    fixed(sp)
                    sp.wait_ge(kv_in[u], dmas)
                    sp.wait_ge(q_in[u], dmas)
                sp.dma_start(src_id[u][0:r, :], src[bass.ds(row, r)].unsqueeze(1)).then_inc(ids_in[u], 16)
                sp.dma_start(dst_id[u][0:r, :], dst[bass.ds(row, r)].unsqueeze(1)).then_inc(ids_in[u], 16)

            def load_pairs(t, j, u, r):
                row, before_last, dmas = value(sp, t * P), value(sp, t - 1), value(sp, 16 * j)
                if later(j):
                    fixed(sp)
                    sp.wait_ge(putid_ready, before_last)
                    sp.wait_ge(equal_ready, before_last)
                    sp.wait_ge(old_in[u], dmas)
                sp.dma_start(dst_row[u][0:r, 0:r],
                             dst[bass.ds(row, r)].unsqueeze(0).to_broadcast([r, r])).then_inc(pair_in[u], 16)
                sp.dma_start(dst_col[u][0:r, :], dst[bass.ds(row, r)].unsqueeze(1)).then_inc(pair_in[u], 16)

            def step(j, u):
                if isinstance(j, int) and 2 * j + u == 0:
                    load_features(0, 0, 0, P)
                    load_ids(0, 0, 0, P)
                    load_ids(1, 0, 1, P)
                run(load_features, j, u, 1)
                run(load_ids, j, u, 2)
                run(load_pairs, j, u, 0)
            over_tiles(sp, mybir.EngineType.SP, step)

        @block.gpsimd
        def _(pool):
            pool.memset(ident16[:, :, :], 0.0).then_inc(consts, 1)
            pool.memset(pick[:, :, :], 0.0).then_inc(consts, 1)
            pool.memset(before[:, :], 1.0).then_inc(consts, 1)
            pool.wait_ge(consts, 3)
            pool.affine_select(out=ident16[:, :, :], in_=ident16[:, :, :], compare_op=ALU.not_equal, fill=1.0, base=0,
                               pattern=[[0, 4], [-1, P]], channel_multiplier=1).then_inc(consts, 1)
            pool.affine_select(out=before[:, :], in_=before[:, :], compare_op=ALU.is_gt, fill=0.0, base=0,
                               pattern=[[-1, P]], channel_multiplier=1).then_inc(consts, 1)
            for part in range(3):
                pool.wait_ge(consts, 5 + part)
                pool.affine_select(out=pick[:, :, :], in_=pick[:, :, :], compare_op=ALU.not_equal, fill=1.0,
                                   base=-H * part, pattern=[[-1, H], [0, P]], channel_multiplier=1).then_inc(consts, 1)

            def fetch(out, table, ids, r, done):
                pool.indirect_dma_start(out=out[0:r, :], out_offset=None, in_=table[:, :],
                                        in_offset=bass.IndirectOffsetOnAxis(ap=ids[0:r, 0:1], axis=0)).then_inc(done, 16)

            def low_part(t, j, u, r):
                pool.wait_ge(efT_ready, value(pool, t + 1))
                pool.wait_ge(efT_hi_ready, value(pool, t + 1))
                if later(j):
                    pool.wait_ge(v_done, value(pool, t - 1))
                pool.tensor_tensor(efT_lo[u][:, :, 0:r], efT[u][:, :, 0:r], efT_hi[u][:, :, 0:r].bitcast(F32),
                                   ALU.subtract).then_inc(efT_lo_ready, 1)

            def fetch_kv(t, j, u, r):
                ids, before_last = value(pool, 32 * (j + 1)), value(pool, t - 1)
                fixed(pool)
                pool.wait_ge(ids_in[u], ids)
                if later(j):
                    pool.wait_ge(v_added, before_last)
                fetch(kv[u], kv_table, src_id[u], r, kv_in[u])

            def fetch_q(t, j, u, r):
                ids, before_last = value(pool, 32 * (j + 1)), value(pool, t - 1)
                fixed(pool)
                pool.wait_ge(ids_in[u], ids)
                if later(j):
                    pool.wait_ge(score_ready, before_last)
                fetch(qc[u], q_table, dst_id[u], r, q_in[u])

            def fetch_old(t, j, u, r):
                dmas, ids = value(pool, 16 * j), value(pool, 32 * (j + 1))
                fixed(pool)
                if later(j):
                    pool.wait_ge(put[u], dmas)
                pool.wait_ge(pair_in[u], ids)
                fetch(old[u], merge[u], dst_col[u], r, old_in[u])

            def store(t, j, u, r):
                done = value(pool, t + 1)
                fixed(pool)
                pool.wait_ge(new_ready, done)
                pool.wait_ge(putid_ready, done)
                pool.indirect_dma_start(out=merge[u][:, :], out_offset=bass.IndirectOffsetOnAxis(ap=put_id[u][0:r, 0:1], axis=0),
                                        in_=new[u][0:r, :], in_offset=None, bounds_check=N - 1,
                                        oob_is_err=False).then_inc(put[u], 16)

            def scale_old(t, j, u, r):
                pool.wait_ge(exp_ready, value(pool, t + 1))
                pool.tensor_tensor(old[u][0:r, 0:ROW].rearrange("p (h e) -> p h e", e=HW),
                                   old[u][0:r, 0:ROW].rearrange("p (h e) -> p h e", e=HW),
                                   bc(expd[u][0:r, H:2 * H], HW), ALU.mult).then_inc(old_scaled, 1)

            def step(j, u):
                if isinstance(j, int) and 2 * j + u == 0:
                    for v in range(2):
                        fetch_kv(v, 0, v, P)
                        fetch_q(v, 0, v, P)
                    low_part(0, 0, 0, P)
                run(low_part, j, u, 1)
                run(store, j, u, -2)
                run(fetch_q, j, u, 2)
                run(scale_old, j, u, -1)
                run(fetch_old, j, u, 0)
                run(fetch_kv, j, u, 2)
            over_tiles(pool, mybir.EngineType.Pool, step)
            pool.wait_ge(put[0], 16 * (J + 1))
            pool.wait_ge(put[1], 16 * J)

        @block.scalar
        def _(act):
            def turn(t, j, u, r):
                act.wait_ge(turned, t + 1)
                if later(j):
                    act.wait_ge(v_done, t - 1)
                turned_ef = psT[:, :].rearrange("p (c e) -> p c e", c=C)[:, :, 0:r]
                act.activation(efT_hi[u][:, :, 0:r], turned_ef, ACT.Copy).then_inc(efT_hi_ready, 1)
                if later(j):
                    act.wait_ge(efT_lo_ready, t - 1)
                act.activation(efT[u][:, :, 0:r], turned_ef, ACT.Copy).then_inc(efT_ready, 1)

            def place_own(t, j, u, r):
                act.wait_ge(q_in[u], 16 * (j + 1))
                if later(j):
                    act.wait_ge(score_ready, t - 1)
                act.activation(kq[u][0:r, :, DH:HW], qc[u][0:r, D:QROW].unsqueeze(2), ACT.Copy).then_inc(own_placed, 1)

            def copy_same(t, j, u, r):
                act.wait_ge(equal_ready, t + 1)
                if later(j):
                    act.wait_ge(summed, t - 1)
                act.activation(same[u][0:r, 0:r], equal[u][0:r, 0:r], ACT.Copy).then_inc(same_ready, 1)

            def spread_parts(t, j, u, r):
                act.wait_ge(parts_turned, t + 1)
                if not zero(t):
                    act.wait_ge(spread, t)
                act.activation(partsT[:, 0:r], psA[0:3 * H, 0:r], ACT.Copy).then_inc(partsT_ready, 1)

            def weights(t, j, u, r):
                act.wait_ge(diff_ready, 2 * (t + 1))
                if later(j):
                    act.wait_ge(old_scaled, t - 1)
                act.activation(expd[u][0:r, :], diff[u][0:r, :], ACT.Exp, scale=SCALE).then_inc(exp_ready, 1)

            def weigh_v(t, j, u, r):
                act.wait_ge(exp_ready, t + 1)
                act.wait_ge(v_added, t + 1)
                if not zero(t):
                    act.wait_ge(wv_lo_ready, t)
                act.activation(wv[0:r, :, DH:HW], expd[u][0:r, 0:H].unsqueeze(2), ACT.Copy).then_inc(wv_ready, 1)
                for h in range(H):
                    act.activation(wv[0:r, h, 0:DH], psV[u][0:r, h * DH:(h + 1) * DH], ACT.Copy,
                                   scale=expd[u][0:r, h:h + 1]).then_inc(wv_ready, 1)
                act.wait_ge(wv_ready, 9 * (t + 1))
                if not zero(t):
                    act.wait_ge(summed, t)
                act.activation(wv_hi[0:r, :, :], wv[0:r, :, :], ACT.Copy).then_inc(wv_hi_ready, 1)

            def step(j, u):
                if isinstance(j, int) and 2 * j + u == 0:
                    turn(0, 0, 0, P)
                    place_own(0, 0, 0, P)
                run(turn, j, u, 1)
                run(weights, j, u, -1)
                run(weigh_v, j, u, -1)
                run(spread_parts, j, u, 0)
                run(copy_same, j, u, 0)
                run(place_own, j, u, 1)
            over_tiles(act, mybir.EngineType.Activation, step)

        @block.vector
        def _(dve):
            def merge_rows(t, j, u, r):
                dve.wait_ge(summed, t + 1)
                dve.wait_ge(old_scaled, t + 1)
                dve.tensor_tensor(new[u][0:r, 0:ROW].rearrange("p (b e) -> p b e", b=2), psS[0:r, :, 0:4 * HW],
                                  old[u][0:r, 0:ROW].rearrange("p (b e) -> p b e", b=2), ALU.add).then_inc(new_ready, 1)

            def compare(t, j, u, r):
                dve.wait_ge(pair_in[u], 32 * (j + 1))
                if later(j):
                    dve.wait_ge(same_ready, t - 1)
                dve.tensor_scalar(equal[u][0:r, 0:r], dst_row[u][0:r, 0:r], dst_col[u][0:r, 0:1], None,
                                  ALU.is_equal).then_inc(equal_ready, 1)

            def count_before(t, j, u, r):
                dve.wait_ge(equal_ready, t + 1)
                if later(j):
                    dve.wait_ge(putid_ready, t - 1)
                dve.tensor_tensor_reduce(out=junk[0:r, 0:r], in0=equal[u][0:r, 0:r], in1=before[0:r, 0:r], scale=OOB,
                                         scalar=0.0, op0=ALU.mult, op1=ALU.add,
                                         accum_out=count[u][0:r, 0:1]).then_inc(counted, 1)

            def set_apart(t, j, u, r):
                if later(j):
                    dve.wait_ge(spread, t - 1)
                dve.tensor_scalar(apart[u][0:r, 0:r], equal[u][0:r, 0:r], -1.0, -NEG, ALU.add,
                                  ALU.mult).then_inc(apart_ready, 1)

            def find_rows(t, j, u, r):
                dve.wait_ge(counted, t + 1)
                if later(j):
                    dve.wait_ge(put[u], 16 * j)
                dve.tensor_tensor(put_id[u][0:r, :], count[u][0:r, :], dst_col[u][0:r, :], ALU.add).then_inc(putid_ready, 1)

            def wv_low_part(t, j, u, r):
                dve.wait_ge(wv_ready, 9 * (t + 1))
                dve.wait_ge(wv_hi_ready, t + 1)
                if not zero(t):
                    dve.wait_ge(summed, t)
                dve.tensor_tensor(wv_lo[0:r, :, :], wv[0:r, :, :], wv_hi[0:r, :, :].bitcast(F32),
                                  ALU.subtract).then_inc(wv_lo_ready, 1)

            def add_k(t, j, u, r):
                dve.wait_ge(k_done, t + 1)
                dve.wait_ge(kv_in[u], 16 * (j + 1))
                dve.tensor_tensor(psK[0:r, :], psK[0:r, :], kv[u][0:r, 0:D], ALU.add).then_inc(k_added, 1)


            def multiply_q(t, j, u, r):
                dve.wait_ge(k_added, t + 1)
                dve.wait_ge(q_in[u], 16 * (j + 1))
                if later(j):
                    dve.wait_ge(score_ready, t - 1)
                dve.tensor_tensor(kq[u][0:r, :, 0:DH], psK[0:r, :].rearrange("p (h d) -> p h d", h=H),
                                  qc[u][0:r, 0:D].rearrange("p (h d) -> p h d", h=H), ALU.mult).then_inc(k_times_q, 1)

            def sum_scores(t, j, u, r):
                dve.wait_ge(k_times_q, t + 1)
                dve.wait_ge(own_placed, t + 1)
                if later(j):
                    dve.wait_ge(diff_ready, 2 * (t - 1))
                dve.tensor_reduce(score[u][0:r, :], kq[u][0:r, :, :], AX.X, ALU.add).then_inc(score_ready, 1)

            def cut(t, j, u, r):
                dve.wait_ge(score_ready, t + 1)
                if not zero(t):
                    dve.wait_ge(parts_turned, t)
                dve.tensor_copy(parts[0:r, 0:H], score[u][0:r, :]).then_inc(part_step, 1)
                compare(t, j, u, r)
                dve.wait_ge(part_step, 4 * t + 1)
                dve.tensor_tensor(rest[0:r, 0, :], score[u][0:r, :], parts[0:r, 0:H], ALU.subtract).then_inc(part_step, 1)
                count_before(t, j, u, r)
                dve.wait_ge(part_step, 4 * t + 2)
                dve.tensor_copy(parts[0:r, H:2 * H], rest[0:r, 0, :]).then_inc(part_step, 1)
                set_apart(t, j, u, r)
                dve.wait_ge(part_step, 4 * t + 3)
                dve.tensor_tensor(rest[0:r, 1, :], rest[0:r, 0, :], parts[0:r, H:2 * H], ALU.subtract).then_inc(part_step, 1)
                dve.wait_ge(part_step, 4 * t + 4)
                dve.tensor_copy(parts[0:r, 2 * H:3 * H], rest[0:r, 1, :]).then_inc(parts_ready, 1)

            def add_v(t, j, u, r):
                dve.wait_ge(v_done, t + 1)
                dve.tensor_tensor(psV[u][0:r, :], psV[u][0:r, :], kv[u][0:r, D:2 * D], ALU.add).then_inc(v_added, 1)

            def top_scores(t, j, u, r):
                dve.wait_ge(spread, t + 1)
                dve.tensor_reduce(top[u][0:r, :], psB[0:r, :, 0:4 * r].rearrange("p b (h e) -> p b h e", h=4), AX.X,
                                  ALU.max).then_inc(top_ready, 1)

            def maximum(t, j, u, r):
                dve.wait_ge(top_ready, t + 1)
                dve.wait_ge(old_in[u], 16 * (j + 1))
                dve.tensor_tensor(new[u][0:r, ROW:TROW], old[u][0:r, ROW:TROW], top[u][0:r, :], ALU.max).then_inc(newmax_ready, 1)
                dve.wait_ge(newmax_ready, t + 1)
                if later(j):
                    dve.wait_ge(exp_ready, t - 1)
                dve.tensor_tensor(diff[u][0:r, 0:H], score[u][0:r, :], new[u][0:r, ROW:TROW], ALU.subtract).then_inc(diff_ready, 1)
                dve.tensor_tensor(diff[u][0:r, H:2 * H], old[u][0:r, ROW:TROW], new[u][0:r, ROW:TROW],
                                  ALU.subtract).then_inc(diff_ready, 1)

            def step(j, u):
                run(add_k, j, u, 0)
                run(multiply_q, j, u, 0)
                run(find_rows, j, u, -1)
                run(top_scores, j, u, -1)
                run(merge_rows, j, u, -2)
                run(maximum, j, u, -1)
                run(sum_scores, j, u, 0)
                run(cut, j, u, 0)
                run(add_v, j, u, 0)
                run(wv_low_part, j, u, -1)
            dve.wait_ge(consts, 5)
            over_tiles(dve, mybir.EngineType.DVE, step)

        @block.tensor
        def _(pe):
            def turn(t, j, u, r):
                pe.wait_ge(ef_in[u], 16 * (j + 1))
                if not zero(t):
                    pe.wait_ge(efT_ready, t)
                if later(j):
                    pe.wait_ge(partsT_ready, t - 1)
                for c in range(C):
                    last = pe.transpose(psT[:, c * P:c * P + r], efs[u][0:r, c * P:(c + 1) * P], ident[0:r, 0:r])
                last.then_inc(turned, 1)

            def product(out, u, col, t, between):
                for c in range(C):
                    pe.matmul(out[:, :], efT_hi[u][:, c, :], Me_hi[:, c, col:col + D], start=c == 0, stop=False)
                    pe.matmul(out[:, :], efT_hi[u][:, c, :], Me_lo[:, c, col:col + D], start=False, stop=False)
                pe.wait_ge(efT_lo_ready, t + 1)
                for c in range(C):
                    if c == 2:
                        between()
                    last = pe.matmul(out[:, :], efT_lo[u][:, c, :], Me_hi[:, c, col:col + D],
                                     start=False, stop=c == C - 1)
                return last

            def keys(t, j, u, r):
                pe.wait_ge(efT_hi_ready, t + 1)
                if not zero(t):
                    pe.wait_ge(k_times_q, t)
                product(psK, u, 0, t, lambda: run(turn_parts, j, u, -1)).then_inc(k_done, 1)

            def values(t, j, u, r):
                if later(j):
                    pe.wait_ge(wv_ready, 9 * (t - 1))
                product(psV[u], u, D, t, lambda: None).then_inc(v_done, 1)

            def sum_tile(t, j, u, r):
                pe.wait_ge(wv_hi_ready, t + 1)
                pe.wait_ge(wv_lo_ready, t + 1)
                pe.wait_ge(same_ready, t + 1)
                if not zero(t):
                    pe.wait_ge(new_ready, t)
                for b in range(2):
                    pe.matmul(psS[0:r, b, 0:4 * HW], same[u][0:r, 0:r], wv_hi[0:r, 4 * b:4 * b + 4, :],
                              start=True, stop=False)
                    last = pe.matmul(psS[0:r, b, 0:4 * HW], same[u][0:r, 0:r], wv_lo[0:r, 4 * b:4 * b + 4, :],
                                     start=False, stop=True)
                last.then_inc(summed, 1)

            def turn_parts(t, j, u, r):
                pe.wait_ge(parts_ready, t + 1)
                if isinstance(t, int) and t == ET - 1:
                    pe.wait_ge(efT_ready, t + 1)
                else:
                    pe.wait_ge(efT_ready, t + 2)
                pe.transpose(psA[0:3 * H, 0:r], parts[0:r, :], ident16[0:r, 0, 0:r]).then_inc(parts_turned, 1)

            def spread_scores(t, j, u, r):
                pe.wait_ge(partsT_ready, t + 1)
                pe.wait_ge(apart_ready, t + 1)
                if not zero(t):
                    pe.wait_ge(top_ready, t)
                for b in range(2):
                    pe.matmul(psB[0:r, b, 0:4 * r].rearrange("p (h e) -> p h e", h=4), apart[u][0:r, 0:r],
                              ident16[0:r, :, 0:r], start=True, stop=True)
                    for h in range(4):
                        last = pe.matmul(psB[0:r, b, h * r:(h + 1) * r], pick[:, 4 * b + h, 0:r], partsT[:, 0:r],
                                         start=False, stop=True, skip_group_check=True)
                last.then_inc(spread, 1)

            def step(j, u):
                if isinstance(j, int) and 2 * j + u == 0:
                    turn(0, 0, 0, P)
                run(keys, j, u, 0)
                if isinstance(j, int) and 2 * j + u == ET:
                    run(turn_parts, j, u, -1)
                run(turn, j, u, 1)
                run(spread_scores, j, u, -1)
                run(sum_tile, j, u, -2)
                run(values, j, u, 0)
            pe.wait_ge(consts, 8)
            over_tiles(pe, mybir.EngineType.PE, step)


def gnn_end(nc, bo, gamma, beta, ident, xnT, gT, WoT, res):
    with ExitStack() as ctx:
        def sb(name, shape, dt=F32):
            return ctx.enter_context(nc.sbuf_tensor(name, shape, dt))

        def sem(name):
            return ctx.enter_context(nc.semaphore(name))

        REAL = [(0, 512), (512, 512), (1024, N - 1024)]
        oT = sb("oT", [P, C, NP])
        col = sb("col", [P, 3, C])
        stats = sb("bstats", [P, C, 3, 6])
        mv = sb("bmv", [P, C, 2])
        sd = sb("sd", [P, C, 6])
        banks = [ctx.enter_context(nc.psum_tensor(f"gbank{i}", [P, D], F32)) for i in range(8)]
        col_in, o_done, oT_done, counted, averaged, sd_in, sd_out, link, norm, back, added = (
            sem(n) for n in ("col_in", "o_done", "oT_done", "bn_counted", "bn_averaged", "sd_in", "sd_out", "bn_link",
                             "norm", "back", "added"))
        block = ctx.enter_context(nc.Block())
        OJ = [(c, k, n0, nn) for c in range(C) for k, (n0, nn) in enumerate(NCH)]

        @block.sync
        def _(sp):
            for i, v in enumerate((bo, gamma, beta)):
                sp.dma_start(col[:, i, :], v.rearrange("(c p) -> p c", p=P),
                             allow_slow_non_contiguous=True).then_inc(col_in, 16)

        @block.vector
        def _(dve):
            def statistics(c):
                for k, (n0, nn) in enumerate(REAL):
                    dve.wait_ge(oT_done, 3 * c + k + 1)
                    dve.bn_stats(stats[:, c, k, :], oT[:, c, n0:n0 + nn]).then_inc(counted, 1)
                dve.wait_ge(counted, 3 * (c + 1))
                dve.bn_aggr(mv[:, c, :], stats[:, c, :, :].rearrange("p k s -> p (k s)")).then_inc(averaged, 1)
                dve.wait_ge(averaged, c + 1)
                dve.tensor_scalar(sd[:, c, 0:1], mv[:, c, 1:2], LN_EPS, None, ALU.add).then_inc(sd_in, 1)

            def normalise(c):
                s = sd[:, c, :]
                dve.wait_ge(sd_out, c + 1)
                dve.reciprocal(s[:, 2:3], s[:, 1:2]).then_inc(link, 1)
                dve.wait_ge(link, 4 * c + 1)
                dve.tensor_tensor(s[:, 3:4], s[:, 2:3], col[:, 1, c:c + 1], ALU.mult).then_inc(link, 1)
                dve.wait_ge(link, 4 * c + 2)
                dve.tensor_tensor(s[:, 4:5], mv[:, c, 0:1], s[:, 3:4], ALU.mult).then_inc(link, 1)
                dve.wait_ge(link, 4 * c + 3)
                dve.tensor_tensor(s[:, 5:6], col[:, 2, c:c + 1], s[:, 4:5], ALU.subtract).then_inc(link, 1)
                dve.wait_ge(link, 4 * c + 4)
                dve.tensor_scalar(oT[:, c, :], oT[:, c, :], s[:, 3:4], s[:, 5:6], ALU.mult, ALU.add).then_inc(norm, 1)

            dve.wait_ge(col_in, 48)
            for j, (c, k, n0, nn) in enumerate(OJ):
                dve.wait_ge(o_done, j + 1)
                dve.scalar_tensor_tensor(oT[:, c, n0:n0 + nn], banks[j % 8][:, 0:nn], col[:, 0, c:c + 1],
                                         xnT[:, c, n0:n0 + nn], ALU.add, ALU.add).then_inc(oT_done, 1)
                if k == 2:
                    statistics(c)
                    if c >= 1:
                        normalise(c - 1)
            normalise(C - 1)
            for t in range(NT):
                dve.wait_ge(back, t + 1)
                dve.tensor_tensor(res[:, t, :], banks[t % 8][:, :], res[:, t, :], ALU.add).then_inc(added, 1)

        @block.scalar
        def _(act):
            for c in range(C):
                act.wait_ge(sd_in, c + 1)
                act.activation(sd[:, c, 1:2], sd[:, c, 0:1], ACT.Sqrt).then_inc(sd_out, 1)

        @block.tensor
        def _(pe):
            for j, (c, _, n0, nn) in enumerate(OJ):
                if j >= 8:
                    pe.wait_ge(oT_done, j - 7)
                for k in range(C):
                    last = pe.matmul(banks[j % 8][:, 0:nn], WoT[:, k, c * P:(c + 1) * P], gT[:, k, n0:n0 + nn],
                                     start=k == 0, stop=k == C - 1)
                last.then_inc(o_done, 1)
            pe.wait_ge(oT_done, len(OJ))
            pe.wait_ge(norm, C)
            for t in range(NT):
                if t >= 8:
                    pe.wait_ge(added, t - 7)
                for c in range(C):
                    last = pe.transpose(banks[t % 8][:, c * P:(c + 1) * P], oT[:, c, t * P:(t + 1) * P], ident[:, :])
                last.then_inc(back, 1)


def ffn(nc, w_up, w_down, ident, res, out):
    with ExitStack() as ctx:
        def sb(name, shape, dt=F32):
            return ctx.enter_context(nc.sbuf_tensor(name, shape, dt))

        def sem(name):
            return ctx.enter_context(nc.semaphore(name))

        UC, DC = FF // P, C
        wu = sb("wu", [P, UC, D])
        wd = sb("wd", [P, DC, FF])
        tern = sb("tern", [P, 2, 2 * D])
        tern16 = sb("tern16", [P, 2, 2 * D], BF16)
        wuT = sb("wuT", [P, C, FF], BF16)
        wdT = sb("wdT", [P, UC, D], BF16)
        ident_b = sb("ident_b", [P, P], BF16)
        sums = sb("sums", [P, 2])
        onem = sb("onem", [P, P])
        wsc = sb("wsc", [P, 3, 2])
        stats = sb("fstats", [P, NT, 6])
        mv = sb("fmv", [P, NT, 2])
        sd = sb("fsd", [P, 3, NT])
        xn = sb("fxn", [P, D])
        xs = sb("xs", [P, 2, 4])
        xq = sb("xq", [P, 2, D])
        xq16 = sb("xq16", [P, 2, D], BF16)
        xqT = sb("xqT", [P, 2, D], BF16)
        hid = sb("hid", [P, FF])
        hs = sb("hs", [P, 2, 4])
        hq16 = sb("hq16", [P, 2, FF], BF16)
        hqT = sb("hqT", [P, 2, FF], BF16)
        y = sb("fy", [P, 2, D])
        pw = ctx.enter_context(nc.psum_tensor("pw", [P, D], F32))
        pt = ctx.enter_context(nc.psum_tensor("pt", [P, 2 * D], BF16))
        ph = [ctx.enter_context(nc.psum_tensor(f"ph{i}", [P, D], F32)) for i in range(2)]
        pht = ctx.enter_context(nc.psum_tensor("pht", [P, 2 * D], BF16))
        py = [ctx.enter_context(nc.psum_tensor(f"py{i}", [P, D], F32)) for i in range(2)]
        w_in, cst, idb, step, total, sd_in, sd_out = (sem(n) for n in (
            "fw_in", "fcst", "fidb", "ffn_link", "w_total", "fsd_in", "fsd_out"))
        xq_ready, x_rounded = sem("xq_ready"), sem("x_rounded")
        w_ready, w_turned, w_copied = sem("w_ready"), sem("fw_turned"), sem("fw_copied")
        x_ready, x_turned, xT_ready, h_done, h_ready, h_turned, hT_ready, y_done, y_ready = (sem(n) for n in (
            "fx_ready", "fx_turned", "fxT_ready", "fh_done", "fh_ready", "fh_turned", "fhT_ready", "fy_done", "fy_ready"))
        stored = [sem(f"stored{i}") for i in range(2)]
        block = ctx.enter_context(nc.Block())

        @block.sync
        def _(sp):
            sp.dma_start(wu[:, :, :], w_up.rearrange("(c p) i -> p c i", p=P)).then_inc(w_in, 16)
            sp.dma_start(wd[:, :, :], w_down.rearrange("(c p) i -> p c i", p=P)).then_inc(w_in, 16)
            for t in range(NT):
                sp.wait_ge(y_ready, t + 1)
                r = node_rows(t)
                sp.dma_start(out[t * P:t * P + r, :], y[0:r, t % 2, :]).then_inc(stored[t % 2], 16)
            sp.wait_ge(stored[0], 16 * (NT // 2))
            sp.wait_ge(stored[1], 16 * (NT // 2))

        @block.gpsimd
        def _(pool):
            pool.memset(onem[:, :], 1.0).then_inc(cst, 1)
            for t in range(NT):
                pool.wait_ge(xq_ready, t + 1)
                pool.tensor_scalar(xq[:, t % 2, :], xq[:, t % 2, :], -RINT, -128.0, ALU.add, ALU.max).then_inc(x_rounded, 1)
                pool.wait_ge(x_rounded, t + 1)
                if t >= 2:
                    pool.wait_ge(x_turned, t - 1)
                pool.tensor_scalar(xq16[:, t % 2, :], xq[:, t % 2, :], 127.0, None, ALU.min).then_inc(x_ready, 1)

        @block.vector
        def _(dve):
            links = [0]

            def link(ins):
                links[0] += 1
                ins.then_inc(step, 1)
                dve.wait_ge(step, links[0])

            dve.tensor_copy(ident_b[:, :], ident[:, :]).then_inc(idb, 1)
            dve.wait_ge(w_in, 32)
            flat = [wu[:, :, :].rearrange("p a b -> p (a b)"), wd[:, :, :].rearrange("p a b -> p (a b)")]
            for i in range(2):
                link(dve.tensor_reduce(sums[:, i:i + 1], flat[i], AX.X, ALU.add, apply_absolute_value=True))
            dve.wait_ge(total, 1)
            link(dve.tensor_scalar(wsc[:, 0, :], pw[:, 0:2], 1.0 / (FF * D), LN_EPS, ALU.mult, ALU.max))
            link(dve.reciprocal(wsc[:, 1, :], wsc[:, 0, :]))
            for i in range(2):
                link(dve.tensor_scalar(tern[:, i, :], flat[i], wsc[:, 1, i:i + 1], RINT, ALU.mult, ALU.add))
                link(dve.tensor_scalar(tern[:, i, :], tern[:, i, :], -RINT, -1.0, ALU.add, ALU.max))
                dve.tensor_scalar(tern16[:, i, :], tern[:, i, :], 1.0, None, ALU.min).then_inc(w_ready, 1)
            for t in range(NT):
                link(dve.bn_stats(stats[:, t, :], res[:, t, :]))
                link(dve.bn_aggr(mv[:, t, :], stats[:, t, :]))
            dve.tensor_scalar(sd[:, 0, :], mv[:, :, 1], LN_EPS, None, ALU.add).then_inc(sd_in, 1)
            dve.wait_ge(sd_out, 1)
            link(dve.reciprocal(sd[:, 2, :], sd[:, 1, :]))

            def quantise(t):
                s = xs[:, t % 2, :]
                link(dve.tensor_scalar(xn[:, :], res[:, t, :], mv[:, t, 0:1], sd[:, 2, t:t + 1], ALU.subtract, ALU.mult))
                link(dve.tensor_reduce(s[:, 0:1], xn[:, :], AX.X, ALU.max, apply_absolute_value=True))
                link(dve.tensor_scalar(s[:, 0:1], s[:, 0:1], LN_EPS, None, ALU.max))
                link(dve.reciprocal(s[:, 1:2], s[:, 0:1]))
                link(dve.tensor_scalar(s[:, 2:3], s[:, 1:2], 127.0, None, ALU.mult))
                link(dve.tensor_scalar(s[:, 3:4], s[:, 0:1], 1.0 / 127.0, wsc[:, 0, 0:1], ALU.mult, ALU.mult))
                if t >= 2:
                    dve.wait_ge(x_ready, t - 1)
                dve.tensor_scalar(xq[:, t % 2, :], xn[:, :], s[:, 2:3], RINT, ALU.mult, ALU.add).then_inc(xq_ready, 1)
                dve.wait_ge(xq_ready, t + 1)

            def hidden(t):
                s = hs[:, t % 2, :]
                dve.wait_ge(h_done, t + 1)
                link(dve.tensor_scalar(hid[:, :], ph[t % 2][:, 0:FF], xs[:, t % 2, 3:4], 0.0, ALU.mult, ALU.max))
                link(dve.tensor_scalar(hid[:, :], hid[:, :], RINT, -RINT, ALU.add, ALU.add))
                link(dve.tensor_scalar(hid[:, :], hid[:, :], 127.0, None, ALU.min))
                link(dve.tensor_reduce(s[:, 0:1], hid[:, :], AX.X, ALU.max))
                link(dve.tensor_scalar(s[:, 0:1], s[:, 0:1], LN_EPS, None, ALU.max))
                link(dve.reciprocal(s[:, 1:2], s[:, 0:1]))
                link(dve.tensor_scalar(s[:, 2:3], s[:, 1:2], 127.0, None, ALU.mult))
                link(dve.tensor_scalar(s[:, 3:4], s[:, 0:1], 1.0 / 127.0, wsc[:, 0, 1:2], ALU.mult, ALU.mult))
                link(dve.tensor_scalar(hid[:, :], hid[:, :], s[:, 2:3], RINT, ALU.mult, ALU.add))
                link(dve.tensor_scalar(hid[:, :], hid[:, :], -RINT, 127.0, ALU.add, ALU.min))
                if t >= 2:
                    dve.wait_ge(h_turned, t - 1)
                dve.tensor_copy(hq16[:, t % 2, :], hid[:, :]).then_inc(h_ready, 1)
                dve.wait_ge(h_ready, t + 1)

            def finish(t):
                dve.wait_ge(y_done, t + 1)
                if t >= 2:
                    dve.wait_ge(stored[t % 2], 16 * (t // 2))
                dve.scalar_tensor_tensor(y[:, t % 2, :], py[t % 2][:, :], hs[:, t % 2, 3:4], res[:, t, :],
                                         ALU.mult, ALU.add).then_inc(y_ready, 1)
                dve.wait_ge(y_ready, t + 1)

            quantise(0)
            for t in range(NT):
                if t + 1 < NT:
                    quantise(t + 1)
                hidden(t)
                if t >= 1:
                    finish(t - 1)
            finish(NT - 1)

        @block.scalar
        def _(act):
            for k in range(3):
                act.wait_ge(w_turned, k + 1)
                if k < 2:
                    act.activation(wuT[:, :, k * P:(k + 1) * P], pt[:, 0:D].rearrange("p (c f) -> p c f", c=C),
                                   ACT.Copy).then_inc(w_copied, 1)
                else:
                    act.activation(wdT[:, :, :], pt[:, :].rearrange("p (a o) -> p a o", a=UC), ACT.Copy).then_inc(w_copied, 1)
            act.wait_ge(sd_in, 1)
            act.activation(sd[:, 1, :], sd[:, 0, :], ACT.Sqrt).then_inc(sd_out, 1)

            def x_copy(t):
                act.wait_ge(x_turned, t + 1)
                if t >= 2:
                    act.wait_ge(h_done, t - 1)
                act.activation(xqT[:, t % 2, :], pt[:, 0:D], ACT.Copy).then_inc(xT_ready, 1)

            x_copy(0)
            for t in range(NT):
                if t + 1 < NT:
                    x_copy(t + 1)
                act.wait_ge(h_turned, t + 1)
                if t >= 2:
                    act.wait_ge(y_done, t - 1)
                act.activation(hqT[:, t % 2, :], pht[:, 0:FF], ACT.Copy).then_inc(hT_ready, 1)

        @block.tensor
        def _(pe):
            pe.wait_ge(cst, 1)
            pe.wait_ge(step, 2)
            pe.matmul(pw[:, 0:2], onem[:, :], sums[:, :], start=True, stop=True).then_inc(total, 1)
            pe.wait_ge(idb, 1)
            pe.wait_ge(w_ready, 1)
            for k in range(2):
                if k:
                    pe.wait_ge(w_copied, k)
                for c in range(C):
                    last = pe.transpose(pt[:, c * P:(c + 1) * P], tern16[:, 0, k * D + c * P:k * D + (c + 1) * P], ident_b[:, :])
                last.then_inc(w_turned, 1)
            pe.wait_ge(w_ready, 2)
            pe.wait_ge(w_copied, 2)
            for a in range(UC):
                for o in range(DC):
                    last = pe.transpose(pt[:, a * D + o * P:a * D + (o + 1) * P],
                                        tern16[:, 1, o * FF + a * P:o * FF + (a + 1) * P], ident_b[:, :])
            last.then_inc(w_turned, 1)
            pe.wait_ge(w_copied, 3)

            def up(t):
                pe.wait_ge(x_ready, t + 1)
                if t >= 1:
                    pe.wait_ge(xT_ready, t)
                for c in range(C):
                    last = pe.transpose(pt[:, c * P:(c + 1) * P], xq16[:, t % 2, c * P:(c + 1) * P], ident_b[:, :])
                last.then_inc(x_turned, 1)
                pe.wait_ge(xT_ready, t + 1)
                if t >= 2:
                    pe.wait_ge(h_ready, t - 1)
                for c in range(C):
                    last = pe.matmul(ph[t % 2][:, 0:FF], xqT[:, t % 2, c * P:(c + 1) * P], wuT[:, c, :],
                                     start=c == 0, stop=c == C - 1)
                last.then_inc(h_done, 1)

            def down(t):
                pe.wait_ge(h_ready, t + 1)
                if t >= 1:
                    pe.wait_ge(hT_ready, t)
                for a in range(UC):
                    last = pe.transpose(pht[:, a * P:(a + 1) * P], hq16[:, t % 2, a * P:(a + 1) * P], ident_b[:, :])
                last.then_inc(h_turned, 1)
                pe.wait_ge(hT_ready, t + 1)
                if t >= 2:
                    pe.wait_ge(y_ready, t - 1)
                for a in range(UC):
                    last = pe.matmul(py[t % 2][:, :], hqT[:, t % 2, a * P:(a + 1) * P], wdT[:, a, :],
                                     start=a == 0, stop=a == UC - 1)
                last.then_inc(y_done, 1)

            up(0)
            for t in range(NT):
                if t + 1 < NT:
                    up(t + 1)
                down(t)


_INS = ["x", "src", "dst", "edge_attr_512", "L0_gnn_Wq", "L0_gnn_bq", "L0_gnn_Wr", "L0_gnn_br", "L0_gnn_Wk", "L0_gnn_bk",
        "L0_gnn_Wv", "L0_gnn_bv", "L0_gnn_Wo", "L0_gnn_bo", "L0_gnn_gamma", "L0_gnn_beta", "L0_mix_w_qkv",
        "L0_mix_w_proj", "L0_mix_b_proj", "L0_ffn_w_up", "L0_ffn_w_down"]


def kernel(**inputs):
    import numpy as _np
    import concourse.bacc as _bacc
    from concourse import mybir as _mybir
    from concourse.bass_utils import run_bass_kernel_spmd as _run

    nc = _bacc.Bacc("TRN2", target_bir_lowering=False, num_devices=1)
    arrays, args = {}, []
    for name in _INS:
        a = _np.ascontiguousarray(inputs[name])
        arrays[f"in_{name}_dram"] = a
        args.append(nc.dram_tensor(f"in_{name}_dram", a.shape, _mybir.dt.from_np(a.dtype), kind="ExternalInput").ap())
    out = nc.dram_tensor("out_dram", [N, D], _mybir.dt.float32, kind="ExternalOutput").ap()
    layer(nc, *args, out)
    r = _run(nc, [arrays], core_ids=[0])
    return r.results[0]["out_dram"]
```
